# Optimizing a Trainium2 kernel written in Bass

```python
import numpy as np
import jax
import jax.numpy as jnp

def _softmax(x, axis=-1):
    return jax.nn.softmax(x, axis=axis)

def _gelu(x):
    return jax.nn.gelu(x, approximate=True)

def _silu(x):
    return jax.nn.silu(x)

def _sigmoid(x):
    return jax.nn.sigmoid(x)

def _layernorm(x, axis=-1, eps=1e-05):
    m = jnp.mean(x, axis=axis, keepdims=True)
    v = jnp.var(x, axis=axis, keepdims=True)
    return (x - m) / jnp.sqrt(v + eps)

def _scatter_add(tgt, idx, src, axis=0):
    return tgt.at[idx].add(src)

def _segment_sum(src, seg, n):
    return jax.ops.segment_sum(src, seg, n)
kernel_name = 'mk_perceiver_d2_seqx_r8_f1fff7'

def setup_inputs(seed: int=0):
    np.random.seed(seed)
    _w = jnp.asarray

    def _rec_inputs():
        import jax
        import jax.numpy as jnp
        _rk = jax.random.key(seed)
        x = 7.22e-05 + 1 * jax.random.normal(jax.random.fold_in(_rk, 1), (2, 128, 256), jnp.float32)
        _lenS = 128 - jax.random.randint(jax.random.fold_in(_rk, 7), (2,), 0, max(1, 128 // 4) + 1, jnp.int32)
        _lenS2 = 2048 - jax.random.randint(jax.random.fold_in(_rk, 8), (2,), 0, max(1, 2048 // 4) + 1, jnp.int32)
        _ctx_2048P = jax.random.normal(jax.random.fold_in(_rk, 11), (2, 16, 256), jnp.float32)
        _ctx_2048c = jax.random.dirichlet(jax.random.fold_in(_rk, 511), 0.3 * jnp.ones((16,), jnp.float32), (2, 2048))
        _ctx_2048t = jnp.einsum('bsk,bkd->bsd', _ctx_2048c, _ctx_2048P)
        _ctx_2048t = _ctx_2048t * jax.lax.rsqrt(jnp.mean(jnp.square(_ctx_2048t)) + 1e-12) * 0.953939
        ctx_2048 = 4.13588e-05 + 0.999923 * (_ctx_2048t + 0.3 * jax.random.normal(jax.random.fold_in(_rk, 611), (2, 2048, 256), jnp.float32))
        _validS = jnp.arange(128)[None, :] < _lenS[:, None]
        _validS2 = jnp.arange(2048)[None, :] < _lenS2[:, None]
        _causal = jnp.tril(jnp.ones((128, 128), dtype=bool))
        mask_BxS2_bk0 = jnp.logical_not(jnp.broadcast_to(_validS2[:, :], (2, 2048)))
        return (x, ctx_2048, mask_BxS2_bk0)
    x, ctx_2048, mask_BxS2_bk0 = _rec_inputs()

    def _L0_xattn_setup():
        import math
        import jax, jax.numpy as jnp
        import numpy as np
        HEADS = 16
        MASKED_BIAS = -10000.0

        def _mha(q, k, v):
            B, Sq, D = q.shape
            Sk = k.shape[-2]
            hd = D // HEADS
            qh = q.reshape(B, Sq, HEADS, hd).transpose(0, 2, 1, 3)
            kh = k.reshape(B, Sk, HEADS, hd).transpose(0, 2, 1, 3)
            vh = v.reshape(B, Sk, HEADS, hd).transpose(0, 2, 1, 3)
            scores = jnp.einsum('bhqd,bhkd->bhqk', qh, kh) / math.sqrt(hd)
            qi = jnp.arange(Sq)[:, None] + (Sk - Sq)
            ki = jnp.arange(Sk)[None, :]
            causal = ki <= qi
            scores = jnp.where(causal[None, None], scores, jnp.asarray(MASKED_BIAS, scores.dtype))
            attn = jax.nn.softmax(scores, axis=-1)
            out = jnp.einsum('bhqk,bhkd->bhqd', attn, vh)
            return out.transpose(0, 2, 1, 3).reshape(B, Sq, D)
        key = jax.random.key(seed)
        kq, kk, kv = jax.random.split(key, 3)
        B, S, D = (4, 128, 256)
        q = jax.random.normal(kq, (B, S, D), dtype=jnp.float32)
        k = jax.random.normal(kk, (B, S, D), dtype=jnp.float32)
        v = jax.random.normal(kv, (B, S, D), dtype=jnp.float32)
        return {'q': q, 'k': k, 'v': v}
    _L0_xattn_all = _L0_xattn_setup()
    _L0_xattn_in = {k: v for k, v in _L0_xattn_all.items() if k in ()}
    del _L0_xattn_all

    def _L0_attn_setup():
        import jax, jax.numpy as jnp
        import numpy as np
        D_INNER = 256
        D_STATE = 16
        key = jax.random.key(seed)
        k1, k2 = jax.random.split(key)
        B, L = (4, 256)
        x = jax.random.normal(k1, (B, L, D_INNER), dtype=jnp.float32)
        A_init = jnp.arange(1, D_STATE + 1, dtype=jnp.float32)
        A_log = jnp.log(jnp.broadcast_to(A_init[None, :], (D_INNER, D_STATE)))
        D = jnp.ones((D_INNER,), dtype=jnp.float32)
        fan_in = D_INNER
        bound = 1.0 / np.sqrt(fan_in)
        W_xproj = jax.random.uniform(k2, (D_INNER + 2 * D_STATE, D_INNER), minval=-bound, maxval=bound, dtype=jnp.float32)
        return {'x': x, 'A_log': A_log, 'D': D, 'W_xproj': W_xproj}
    _L0_attn_all = _L0_attn_setup()
    _L0_attn_in = {k: v for k, v in _L0_attn_all.items() if k in ('A_log', 'D', 'W_xproj')}
    del _L0_attn_all

    def _L0_ffn_setup():
        import jax, jax.numpy as jnp
        import numpy as np
        D_IN = 256
        D_OUT = 256
        RANK = 16
        N_EXPERTS = 16
        MAX_EXPERTS = 32
        ROUTER_HID = 64
        TOPK = 2
        ALPHA = 1.0

        def _forward(x, W, bias, rw1, rb1, rw2, rb2, A, B, gates):
            lead = x.shape[:-1]
            x_flat = x.reshape(-1, D_IN)
            n = x_flat.shape[0]
            feat = jax.lax.stop_gradient(x_flat)
            h = jax.nn.silu(feat @ rw1.T + rb1)
            logits = (h @ rw2.T + rb2)[:, :N_EXPERTS] + gates[None, :]
            topv, topi = jax.lax.top_k(logits, TOPK)
            sm = jax.nn.softmax(topv, axis=-1)
            rows = jnp.arange(n)[:, None]
            coeff = jnp.zeros_like(logits).at[rows, topi].set(sm)
            base = x_flat @ W.T + bias
            xa = jnp.einsum('ni,eri->ner', x_flat, A)
            wxa = xa * coeff[:, :, None]
            delta = jnp.einsum('ner,eor->no', wxa, B)
            out = base + ALPHA * delta
            return out.reshape(*lead, D_OUT)
        key = jax.random.key(seed)
        ks = jax.random.split(key, 10)
        s = 0.02
        x = jax.random.normal(ks[0], (4, 512, D_IN), dtype=jnp.float32)
        W = jax.random.normal(ks[1], (D_OUT, D_IN), dtype=jnp.float32) * s
        bias = jax.random.normal(ks[2], (D_OUT,), dtype=jnp.float32) * s
        rw1 = jax.random.normal(ks[3], (ROUTER_HID, D_IN), dtype=jnp.float32) * s
        rb1 = jnp.zeros((ROUTER_HID,), dtype=jnp.float32)
        rw2 = jax.random.normal(ks[4], (MAX_EXPERTS, ROUTER_HID), dtype=jnp.float32) * s
        rb2 = jnp.zeros((MAX_EXPERTS,), dtype=jnp.float32)
        A = jax.random.normal(ks[5], (N_EXPERTS, RANK, D_IN), dtype=jnp.float32) * s
        B = jax.random.normal(ks[6], (N_EXPERTS, D_OUT, RANK), dtype=jnp.float32) * s
        gates = jnp.ones((N_EXPERTS,), dtype=jnp.float32)
        return {'x': x, 'W': W, 'bias': bias, 'rw1': rw1, 'rb1': rb1, 'rw2': rw2, 'rb2': rb2, 'A': A, 'B': B, 'gates': gates}
    _L0_ffn_all = _L0_ffn_setup()
    _L0_ffn_in = {k: v for k, v in _L0_ffn_all.items() if k in ('W', 'bias', 'rw1', 'rb1', 'rw2', 'rb2', 'A', 'B', 'gates')}
    del _L0_ffn_all

    def _L1_xattn_setup():
        import jax, jax.numpy as jnp
        import numpy as np
        key = jax.random.key(seed)
        k1, k2, k3 = jax.random.split(key, 3)
        B, S, D, M = (8, 256, 256, 128)
        hidden_states = jax.random.normal(k1, (B, S, D), dtype=jnp.float32)
        memory_tokens = jax.random.normal(k2, (B, M, D), dtype=jnp.float32)
        memory_mask = jax.random.randint(k3, (B, M), 0, 2).astype(jnp.bool_)
        return {'hidden_states': hidden_states, 'memory_tokens': memory_tokens, 'memory_mask': memory_mask}
    _L1_xattn_all = _L1_xattn_setup()
    _L1_xattn_in = {k: v for k, v in _L1_xattn_all.items() if k in ()}
    del _L1_xattn_all

    def _L1_attn_setup():
        import jax, jax.numpy as jnp
        import numpy as np
        HID = 256
        NH = 16
        HD = 128
        R = 16
        WIN = 128
        ROPE = HD // 2
        EPS = 1e-06

        def rmsnorm(x, w):
            return x * jax.lax.rsqrt(jnp.mean(x * x, axis=-1, keepdims=True) + EPS) * w

        def apply_rope(x, pos):
            half = ROPE // 2
            inv_freq = 1.0 / 10000.0 ** (jnp.arange(half, dtype=jnp.float32) * 2.0 / ROPE)
            ang = pos.astype(jnp.float32)[:, None] * inv_freq[None, :]
            cos, sin = (jnp.cos(ang), jnp.sin(ang))
            x1, x2, rest = (x[..., :half], x[..., half:ROPE], x[..., ROPE:])
            return jnp.concatenate([x1 * cos - x2 * sin, x1 * sin + x2 * cos, rest], axis=-1)
        key = jax.random.key(seed)
        ks = jax.random.split(key, 16)
        s = 0.02
        return {'hidden_states': jax.random.normal(ks[0], (1, 256, HID), jnp.float32), 'Wq': jax.random.normal(ks[1], (HID, NH * HD), jnp.float32) * s, 'bq': jnp.zeros((NH * HD,), jnp.float32), 'Wc': jax.random.normal(ks[2], (HID, 1), jnp.float32) * s, 'bc': jnp.zeros((1,), jnp.float32), 'Wk': jax.random.normal(ks[3], (HID, HD), jnp.float32) * s, 'bk': jnp.zeros((HD,), jnp.float32), 'Wv': jax.random.normal(ks[4], (HID, HD), jnp.float32) * s, 'bv': jnp.zeros((HD,), jnp.float32), 'Wlk': jax.random.normal(ks[5], (HID, NH * HD), jnp.float32) * s, 'blk': jnp.zeros((NH * HD,), jnp.float32), 'Wlv': jax.random.normal(ks[6], (HID, NH * HD), jnp.float32) * s, 'blv': jnp.zeros((NH * HD,), jnp.float32), 'qn_w': jnp.ones((HD,), jnp.float32), 'kn_w': jnp.ones((HD,), jnp.float32), 'sink_k': jax.random.normal(ks[7], (NH, HD), jnp.float32) * s, 'sink_v': jax.random.normal(ks[8], (NH, HD), jnp.float32) * s, 'Wo': jax.random.normal(ks[9], (NH * HD, HID), jnp.float32) * s, 'bo': jnp.zeros((HID,), jnp.float32)}
    _L1_attn_all = _L1_attn_setup()
    _L1_attn_in = {k: v for k, v in _L1_attn_all.items() if k in ('Wq', 'bq', 'Wc', 'bc', 'Wk', 'bk', 'Wv', 'bv', 'Wlk', 'blk', 'Wlv', 'blv', 'qn_w', 'kn_w', 'sink_k', 'sink_v', 'Wo', 'bo')}
    del _L1_attn_all

    def _L1_ffn_setup():
        import jax, jax.numpy as jnp
        import numpy as np
        B, S, D = (4, 128, 256)
        H = 512
        NE = 8
        TOPK = 2
        key = jax.random.key(seed)
        ks = jax.random.split(key, 9)
        s = lambda fan_in: 1.0 / np.sqrt(fan_in)
        return {'x': jax.random.normal(ks[0], (B, S, D), dtype=jnp.float32), 'W1': jax.random.normal(ks[1], (NE, D, H), dtype=jnp.float32) * s(D), 'b1': jnp.zeros((NE, H), dtype=jnp.float32), 'W2': jax.random.normal(ks[2], (NE, H, H), dtype=jnp.float32) * s(H), 'b2': jnp.zeros((NE, H), dtype=jnp.float32), 'W3': jax.random.normal(ks[3], (NE, H, D), dtype=jnp.float32) * s(H), 'b3': jnp.zeros((NE, D), dtype=jnp.float32), 'Wg': jax.random.normal(ks[4], (D, NE), dtype=jnp.float32) * s(D), 'bg': jnp.zeros((NE,), dtype=jnp.float32)}
    _L1_ffn_all = _L1_ffn_setup()
    _L1_ffn_in = {k: v for k, v in _L1_ffn_all.items() if k in ('W1', 'b1', 'W2', 'b2', 'W3', 'b3', 'Wg', 'bg')}
    del _L1_ffn_all
    return {'x': x, 'ctx_2048': ctx_2048, 'mask_BxS2_bk0': mask_BxS2_bk0, 'L0_attn_A_log': _L0_attn_in['A_log'], 'L0_attn_D': _L0_attn_in['D'], 'L0_attn_W_xproj': _L0_attn_in['W_xproj'], 'L0_ffn_W': _L0_ffn_in['W'], 'L0_ffn_bias': _L0_ffn_in['bias'], 'L0_ffn_rw1': _L0_ffn_in['rw1'], 'L0_ffn_rb1': _L0_ffn_in['rb1'], 'L0_ffn_rw2': _L0_ffn_in['rw2'], 'L0_ffn_rb2': _L0_ffn_in['rb2'], 'L0_ffn_A': _L0_ffn_in['A'], 'L0_ffn_B': _L0_ffn_in['B'], 'L0_ffn_gates': _L0_ffn_in['gates'], 'L1_attn_Wq': _L1_attn_in['Wq'], 'L1_attn_bq': _L1_attn_in['bq'], 'L1_attn_Wc': _L1_attn_in['Wc'], 'L1_attn_bc': _L1_attn_in['bc'], 'L1_attn_Wk': _L1_attn_in['Wk'], 'L1_attn_bk': _L1_attn_in['bk'], 'L1_attn_Wv': _L1_attn_in['Wv'], 'L1_attn_bv': _L1_attn_in['bv'], 'L1_attn_Wlk': _L1_attn_in['Wlk'], 'L1_attn_blk': _L1_attn_in['blk'], 'L1_attn_Wlv': _L1_attn_in['Wlv'], 'L1_attn_blv': _L1_attn_in['blv'], 'L1_attn_qn_w': _L1_attn_in['qn_w'], 'L1_attn_kn_w': _L1_attn_in['kn_w'], 'L1_attn_sink_k': _L1_attn_in['sink_k'], 'L1_attn_sink_v': _L1_attn_in['sink_v'], 'L1_attn_Wo': _L1_attn_in['Wo'], 'L1_attn_bo': _L1_attn_in['bo'], 'L1_ffn_W1': _L1_ffn_in['W1'], 'L1_ffn_b1': _L1_ffn_in['b1'], 'L1_ffn_W2': _L1_ffn_in['W2'], 'L1_ffn_b2': _L1_ffn_in['b2'], 'L1_ffn_W3': _L1_ffn_in['W3'], 'L1_ffn_b3': _L1_ffn_in['b3'], 'L1_ffn_Wg': _L1_ffn_in['Wg'], 'L1_ffn_bg': _L1_ffn_in['bg']}

def reference(x, ctx_2048, mask_BxS2_bk0, L0_attn_A_log, L0_attn_D, L0_attn_W_xproj, L0_ffn_W, L0_ffn_bias, L0_ffn_rw1, L0_ffn_rb1, L0_ffn_rw2, L0_ffn_rb2, L0_ffn_A, L0_ffn_B, L0_ffn_gates, L1_attn_Wq, L1_attn_bq, L1_attn_Wc, L1_attn_bc, L1_attn_Wk, L1_attn_bk, L1_attn_Wv, L1_attn_bv, L1_attn_Wlk, L1_attn_blk, L1_attn_Wlv, L1_attn_blv, L1_attn_qn_w, L1_attn_kn_w, L1_attn_sink_k, L1_attn_sink_v, L1_attn_Wo, L1_attn_bo, L1_ffn_W1, L1_ffn_b1, L1_ffn_W2, L1_ffn_b2, L1_ffn_W3, L1_ffn_b3, L1_ffn_Wg, L1_ffn_bg):
    import jax
    import jax.numpy as jnp

    def _L0_xattn_ref(q, k, v):
        import math
        import jax, jax.numpy as jnp
        import numpy as np
        HEADS = 16
        MASKED_BIAS = -10000.0

        def _mha(q, k, v):
            B, Sq, D = q.shape
            Sk = k.shape[-2]
            hd = D // HEADS
            qh = q.reshape(B, Sq, HEADS, hd).transpose(0, 2, 1, 3)
            kh = k.reshape(B, Sk, HEADS, hd).transpose(0, 2, 1, 3)
            vh = v.reshape(B, Sk, HEADS, hd).transpose(0, 2, 1, 3)
            scores = jnp.einsum('bhqd,bhkd->bhqk', qh, kh) / math.sqrt(hd)
            qi = jnp.arange(Sq)[:, None] + (Sk - Sq)
            ki = jnp.arange(Sk)[None, :]
            causal = ki <= qi
            scores = jnp.where(causal[None, None], scores, jnp.asarray(MASKED_BIAS, scores.dtype))
            attn = jax.nn.softmax(scores, axis=-1)
            out = jnp.einsum('bhqk,bhkd->bhqd', attn, vh)
            return out.transpose(0, 2, 1, 3).reshape(B, Sq, D)
        return _mha(q, k, v)

    def _L0_attn_ref(x, A_log, D, W_xproj):
        import jax, jax.numpy as jnp
        import numpy as np
        D_INNER = 256
        D_STATE = 16
        Bsz, L, Dm = x.shape
        N = A_log.shape[1]
        x_proj = jnp.einsum('bld,ed->ble', x, W_xproj)
        dt = jax.nn.softplus(x_proj[..., :Dm])
        B_ssm = x_proj[..., Dm:Dm + N]
        C_ssm = x_proj[..., Dm + N:]
        A = -jnp.exp(A_log)

        def step(h, inp):
            x_t, dt_t, B_t, C_t = inp
            A_bar = jnp.exp(dt_t[..., None] * A)
            B_bar = dt_t[..., None] * B_t[:, None, :]
            h = A_bar * h + B_bar * x_t[..., None]
            y_t = jnp.einsum('bdn,bn->bd', h, C_t) + D * x_t
            return (h, y_t)
        xs = (jnp.swapaxes(x, 0, 1), jnp.swapaxes(dt, 0, 1), jnp.swapaxes(B_ssm, 0, 1), jnp.swapaxes(C_ssm, 0, 1))
        h0 = jnp.zeros((Bsz, Dm, N), dtype=x.dtype)
        _, ys = jax.lax.scan(step, h0, xs)
        return jnp.swapaxes(ys, 0, 1)

    def _L0_ffn_ref(x, W, bias, rw1, rb1, rw2, rb2, A, B, gates):
        import jax, jax.numpy as jnp
        import numpy as np
        D_IN = 256
        D_OUT = 256
        RANK = 16
        N_EXPERTS = 16
        MAX_EXPERTS = 32
        ROUTER_HID = 64
        TOPK = 2
        ALPHA = 1.0

        def _forward(x, W, bias, rw1, rb1, rw2, rb2, A, B, gates):
            lead = x.shape[:-1]
            x_flat = x.reshape(-1, D_IN)
            n = x_flat.shape[0]
            feat = jax.lax.stop_gradient(x_flat)
            h = jax.nn.silu(feat @ rw1.T + rb1)
            logits = (h @ rw2.T + rb2)[:, :N_EXPERTS] + gates[None, :]
            topv, topi = jax.lax.top_k(logits, TOPK)
            sm = jax.nn.softmax(topv, axis=-1)
            rows = jnp.arange(n)[:, None]
            coeff = jnp.zeros_like(logits).at[rows, topi].set(sm)
            base = x_flat @ W.T + bias
            xa = jnp.einsum('ni,eri->ner', x_flat, A)
            wxa = xa * coeff[:, :, None]
            delta = jnp.einsum('ner,eor->no', wxa, B)
            out = base + ALPHA * delta
            return out.reshape(*lead, D_OUT)
        return _forward(x, W, bias, rw1, rb1, rw2, rb2, A, B, gates)

    def _L1_xattn_ref(hidden_states, memory_tokens, memory_mask):
        import jax, jax.numpy as jnp
        import numpy as np
        B, S, D = hidden_states.shape
        scale = 1.0 / jnp.sqrt(jnp.asarray(D, hidden_states.dtype))
        scores = jnp.einsum('bsd,bmd->bsm', hidden_states, memory_tokens) * scale
        neg_inf = jnp.asarray(-1e+30, scores.dtype)
        scores = jnp.where(memory_mask[:, None, :], scores, neg_inf)
        attn = jax.nn.softmax(scores, axis=-1)
        readout = jnp.einsum('bsm,bmd->bsd', attn, memory_tokens)
        valid_b = jnp.any(memory_mask, axis=-1)
        out = jnp.where(valid_b[:, None, None], readout, jnp.zeros_like(readout))
        return out

    def _L1_attn_ref(hidden_states, Wq, bq, Wc, bc, Wk, bk, Wv, bv, Wlk, blk, Wlv, blv, qn_w, kn_w, sink_k, sink_v, Wo, bo):
        import jax, jax.numpy as jnp
        import numpy as np
        HID = 256
        NH = 16
        HD = 128
        R = 16
        WIN = 128
        ROPE = HD // 2
        EPS = 1e-06

        def rmsnorm(x, w):
            return x * jax.lax.rsqrt(jnp.mean(x * x, axis=-1, keepdims=True) + EPS) * w

        def apply_rope(x, pos):
            half = ROPE // 2
            inv_freq = 1.0 / 10000.0 ** (jnp.arange(half, dtype=jnp.float32) * 2.0 / ROPE)
            ang = pos.astype(jnp.float32)[:, None] * inv_freq[None, :]
            cos, sin = (jnp.cos(ang), jnp.sin(ang))
            x1, x2, rest = (x[..., :half], x[..., half:ROPE], x[..., ROPE:])
            return jnp.concatenate([x1 * cos - x2 * sin, x1 * sin + x2 * cos, rest], axis=-1)
        B, S, _ = hidden_states.shape
        pos = jnp.arange(S)
        scale = 1.0 / jnp.sqrt(jnp.float32(HD))
        q = (hidden_states @ Wq + bq).reshape(B, S, NH, HD).transpose(0, 2, 1, 3)
        q = apply_rope(rmsnorm(q, qn_w), pos)
        C = S // R
        w = jax.nn.softmax((hidden_states @ Wc + bc).reshape(B, C, R), axis=-1)
        entries = jnp.einsum('bcr,bcrh->bch', w, hidden_states.reshape(B, C, R, HID))
        block_ends = jnp.arange(C) * R + (R - 1)
        ck = apply_rope(rmsnorm(entries @ Wk + bk, kn_w), block_ends)
        cv = entries @ Wv + bv
        cs = jnp.einsum('bhsd,bcd->bhsc', q, ck) * scale
        cmask = block_ends[None, :] <= pos[:, None]
        cs = jnp.where(cmask, cs, -1000000000.0)
        sink_s = jnp.einsum('bhsd,hd->bhs', q, sink_k) * scale
        attn = jax.nn.softmax(jnp.concatenate([cs, sink_s[..., None]], axis=-1), axis=-1)
        ctx_c = jnp.einsum('bhsc,bcd->bhsd', attn[..., :C], cv) + attn[..., C:] * sink_v[None, :, None, :]
        lk = (hidden_states @ Wlk + blk).reshape(B, S, NH, HD).transpose(0, 2, 1, 3)
        lk = apply_rope(rmsnorm(lk, kn_w), pos)
        lv = (hidden_states @ Wlv + blv).reshape(B, S, NH, HD).transpose(0, 2, 1, 3)
        ls = jnp.einsum('bhsd,bhtd->bhst', q, lk) * scale
        d = pos[:, None] - pos[None, :]
        lmask = (d >= 0) & (d <= WIN)
        lattn = jax.nn.softmax(jnp.where(lmask, ls, -1000000000.0), axis=-1)
        ctx_l = jnp.einsum('bhst,bhtd->bhsd', lattn, lv)
        merged = 0.5 * (ctx_c + ctx_l)
        out = merged.transpose(0, 2, 1, 3).reshape(B, S, NH * HD) @ Wo + bo
        return out

    def _L1_ffn_ref(x, W1, b1, W2, b2, W3, b3, Wg, bg):
        import jax, jax.numpy as jnp
        import numpy as np
        B, S, D = (4, 128, 256)
        H = 512
        NE = 8
        TOPK = 2
        gate_logits = jnp.einsum('bsd,dn->bsn', x, Wg) + bg
        gate_weights = jax.nn.softmax(gate_logits, axis=-1)
        topv, topi = jax.lax.top_k(gate_weights, TOPK)
        h = jax.nn.gelu(jnp.einsum('bsd,ndh->nbsh', x, W1) + b1[:, None, None, :], approximate=False)
        h = jax.nn.gelu(jnp.einsum('nbsh,nhf->nbsf', h, W2) + b2[:, None, None, :], approximate=False)
        eo = jnp.einsum('nbsf,nfd->nbsd', h, W3) + b3[:, None, None, :]
        comb = jnp.sum(jax.nn.one_hot(topi, NE, dtype=x.dtype) * topv[..., None], axis=-2)
        out = jnp.einsum('nbsd,bsn->bsd', eo, comb)
        return out
    x = x + _L0_xattn_ref(_layernorm(x, axis=-1), ctx_2048, ctx_2048)
    x = x + _L0_attn_ref(_layernorm(x, axis=-1), L0_attn_A_log, L0_attn_D, L0_attn_W_xproj)
    x = x + _L0_ffn_ref(_layernorm(x, axis=-1), L0_ffn_W, L0_ffn_bias, L0_ffn_rw1, L0_ffn_rb1, L0_ffn_rw2, L0_ffn_rb2, L0_ffn_A, L0_ffn_B, L0_ffn_gates)
    x = x + _L1_xattn_ref(_layernorm(x, axis=-1), ctx_2048, mask_BxS2_bk0)
    x = x + _L1_attn_ref(_layernorm(x, axis=-1), L1_attn_Wq, L1_attn_bq, L1_attn_Wc, L1_attn_bc, L1_attn_Wk, L1_attn_bk, L1_attn_Wv, L1_attn_bv, L1_attn_Wlk, L1_attn_blk, L1_attn_Wlv, L1_attn_blv, L1_attn_qn_w, L1_attn_kn_w, L1_attn_sink_k, L1_attn_sink_v, L1_attn_Wo, L1_attn_bo)
    x = x + _L1_ffn_ref(_layernorm(x, axis=-1), L1_ffn_W1, L1_ffn_b1, L1_ffn_W2, L1_ffn_b2, L1_ffn_W3, L1_ffn_b3, L1_ffn_Wg, L1_ffn_bg)
    return x

_drawn_inputs = setup_inputs


def setup_inputs(seed=0):
    import zlib

    import numpy as np

    out = dict(_drawn_inputs(seed))
    spreads = {'L0_attn_D': (1.0, 0.2),
     'L0_ffn_rb1': (0.0, 0.8),
     'L0_ffn_rb2': (0.0, 0.8),
     'L0_ffn_gates': (1.0, 0.6),
     'L1_attn_bq': (0.0, 2.0),
     'L1_attn_bk': (0.0, 2.0),
     'L1_attn_bv': (0.0, 0.729),
     'L1_attn_blk': (0.0, 2.0),
     'L1_attn_blv': (0.0, 0.51),
     'L1_attn_qn_w': (1.0, 0.6),
     'L1_attn_kn_w': (1.0, 0.6),
     'L1_attn_bo': (0.0, 0.1),
     'L1_ffn_b1': (0.0, 0.8),
     'L1_ffn_b2': (0.0, 0.8),
     'L1_ffn_b3': (0.0, 0.557),
     'L1_ffn_bg': (0.0, 0.511)}
    factors = {'L0_ffn_bias': 7.944,
     'L0_ffn_rw1': 8.0,
     'L0_ffn_rw2': 8.0,
     'L0_ffn_A': 8.0,
     'L0_ffn_B': 8.0,
     'L1_attn_Wq': 5.883,
     'L1_attn_Wc': 8.0,
     'L1_attn_Wk': 8.0,
     'L1_attn_Wv': 2.89,
     'L1_attn_Wlk': 21.696,
     'L1_attn_sink_k': 64.0,
     'L1_attn_sink_v': 42.963}
    for name, (base, spread) in spreads.items():
        noise = np.random.default_rng([zlib.crc32(name.encode()), seed]).standard_normal(out[name].shape)
        drawn = base * np.exp(spread * noise) if base else spread * noise
        out[name] = jnp.asarray(drawn.astype(out[name].dtype))
    for name, factor in factors.items():
        out[name] = (out[name] * factor).astype(out[name].dtype)
    return out
```

```python
import math
from contextlib import ExitStack

import numpy as np

import concourse.bass as bass
from concourse import mybir

F32 = mybir.dt.float32
BF16 = mybir.dt.bfloat16
U32 = mybir.dt.uint32
U8 = mybir.dt.uint8
ALU = mybir.AluOpType
ACT = mybir.ActivationFunctionType
X_AXIS = mybir.AxisListType.X

P = 128
NB = 2
D = 256
KD = D // P
KEYS = 2048
NCH = KEYS // P

H0, HD0 = 16, 16
HPG = 4
NHG = H0 // HPG
NG = NB * NHG
HALF_K = KEYS // 2
REP = 12
PARTS = 6
QROWS = PARTS * HD0
SROWS = QROWS + 2
VW = 32
MASKED0 = -10000.0
HIDE = -1.0e30

NS = 16
NE0, RANK, HID0 = 16, 16, 64
NH, HD, BLK, NC = 16, 128, 16, 8
SW = P + NC + 1
ROPE = 64
HALF = ROPE // 2
NE, FF = 8, 512
MF = FF // P

EXP_WORDS = KD * FF + MF * FF + MF * D


def view(region, start, words, dtype=F32):
    part = region[:, start:start + words]
    return part if dtype == F32 else part.bitcast(dtype)


def perceiver_program(nc, io, out):
    ctx = ExitStack()
    sems = {}
    with ctx:
        def sb(name, shape, dt=F32):
            return ctx.enter_context(nc.sbuf_tensor(name, shape, dt))

        def S(name):
            if name not in sems:
                sems[name] = ctx.enter_context(nc.semaphore(name))
            return sems[name]

        reg_a = sb("reg_a", [P, 16384])
        reg_b = sb("reg_b", [P, 26112])
        ctxT = reg_a[:, 0:8192].rearrange("p (b h k) -> p b h k", b=NB, h=KD)
        ctxN = reg_a[:, 8192:16384].rearrange("p (b c d) -> p b c d", b=NB, c=NCH)
        kS = [view(reg_b, 4096 * i, 4096, BF16).rearrange("p (j k) -> p j k", j=HPG) for i in range(3)]
        ctxK = reg_a[:, 0:8192].rearrange("p (b j k) -> p b j k", b=NB, j=HPG)
        ks3 = view(reg_b, 12288, 6144, BF16).rearrange("p (t j k) -> p t j k", t=3, j=HPG)
        kres = reg_b[:, 18432:20480]
        va = [reg_b[:, 20480 + 2048 * i:20480 + 2048 * (i + 1)].rearrange("p (c j w) -> p c j w", c=NCH, j=HPG)
              for i in range(2)]
        pT = [reg_b[:, 24576 + 512 * i:24576 + 512 * (i + 1)] for i in range(3)]
        ssm_at = [12288, 0]
        bc_row = [reg_b[:, a:a + 4096].rearrange("p (n l) -> p n l", n=2 * NS) for a in ssm_at]
        decay = [reg_b[:, a + 4096:a + 8192].rearrange("p (h n l) -> p h n l", h=KD, n=NS) for a in ssm_at]
        state = [reg_b[:, a + 8192:a + 12288].rearrange("p (h n l) -> p h n l", h=KD, n=NS) for a in ssm_at]
        w_qkv = reg_b[:, 0:12288].rearrange("p (j k n) -> p j k n", j=3, k=KD)
        w_o = reg_b[:, 12288:16384].rearrange("p (h n) -> p h n", h=NH)
        p3 = [reg_b[:, 16384 + 2048 * b:16384 + 2048 * (b + 1)] for b in range(NB)]
        p3T = [reg_b[:, 20480 + 2048 * b:20480 + 2048 * (b + 1)].rearrange("p (c q) -> p c q", c=NCH)
               for b in range(NB)]
        roped = reg_b[:, 16384:18432].rearrange("p (h d) -> p h d", h=NH)
        cvs = reg_b[:, 18432:20480].rearrange("p (h d) -> p h d", h=NH)
        bias3 = view(reg_b, 20480, 1024, BF16)
        squares = reg_b[:, 21504:23552].rearrange("p (h d) -> p h d", h=NH)
        act = [reg_a[:, 8192 * b:8192 * (b + 1)] for b in range(NB)]
        qf = [a[:, 0:2048].rearrange("p (h d) -> p h d", h=NH) for a in act]
        kf = [a[:, 2048:2048 + NH * SW].rearrange("p (h d) -> p h d", h=NH) for a in act]
        lv = [a[:, 4240:6288].rearrange("p (h d) -> p h d", h=NH) for a in act]
        pr = [a[:, 6288:6288 + HPG * SW].rearrange("p (j d) -> p j d", j=HPG) for a in act]
        prT = [a[:, 6836:7348].rearrange("p (j d) -> p j d", j=HPG) for a in act]
        pcT = [a[:, 7348:7860].rearrange("p (j d) -> p j d", j=HPG) for a in act]
        expert_at = [(reg_b, 0), (reg_b, 4096), (reg_b, 8192), (reg_b, 12288), (reg_b, 16384), (reg_b, 20480),
                     (reg_a, 0), (reg_a, 4096)]
        w1 = [r[:, a:a + KD * FF].rearrange("p (k n) -> p k n", k=KD) for r, a in expert_at]
        w2 = [r[:, a + 1024:a + 3072].rearrange("p (k n) -> p k n", k=MF) for r, a in expert_at]
        w3 = [r[:, a + 3072:a + 4096].rearrange("p (k n) -> p k n", k=MF) for r, a in expert_at]
        h1 = reg_a[:, 8192:9216].rearrange("p (m t) -> p m t", m=MF)
        h2 = reg_a[:, 9216:10240].rearrange("p (m t) -> p m t", m=MF)
        h1b = reg_a[:, 10240:11264].rearrange("p (m t) -> p m t", m=MF)
        h2b = reg_a[:, 11264:12288].rearrange("p (m t) -> p m t", m=MF)

        cf = sb("cf", [P, 2 * P + 1 + NC + NC * 0 + 16 + 1])
        ident = cf[:, 0:P]
        later = cf[:, P:2 * P]
        floor0 = cf[:, 2 * P:2 * P + 1]
        in_block = cf[:, 2 * P + 1:2 * P + 9]
        iota = cf[:, 2 * P + 9:2 * P + 25]
        neg_half = cf[:, 2 * P + 25:2 * P + 26]
        cb = sb("cb", [P, 5 * P], BF16)
        identb = cb[:, 0:P]
        hide_q = cb[:, P:2 * P]
        hide_k = cb[:, 2 * P:3 * P]
        hide_s = cb[:, 3 * P:3 * P + SW]
        onesb = sb("onesb", [P, P], BF16)

        x = [sb(f"x{b}", [P, D]) for b in range(NB)]
        xn = [sb(f"xn{b}", [P, D]) for b in range(NB)]
        xT2 = sb("xT", [P, KD, NB * P])
        xT = [xT2[:, :, b * P:(b + 1) * P] for b in range(NB)]
        stats = [sb(f"stats{b}", [P, 6]) for b in range(NB)]
        mean_var = [sb(f"mv{b}", [P, 2]) for b in range(NB)]
        var_eps = [sb(f"ve{b}", [P, 1]) for b in range(NB)]
        rstd = [sb(f"rstd{b}", [P, 1]) for b in range(NB)]
        tmp = [sb(f"tmp{b}", [P, D]) for b in range(NB)]
        tmp2 = [sb(f"tmpb{b}", [P, D]) for b in range(NB)]
        oreg = sb("oreg", [P, 2048])
        q_split = [view(oreg, 1024 * b, 768, BF16).rearrange("p (h t d) -> p h t d", h=H0, t=PARTS)
                   for b in range(NB)]
        o_all = [oreg[:, 1024 * b:1024 * (b + 1)].rearrange("p (g u j w) -> p g u j w", g=NHG, u=2, j=HPG)
                 for b in range(NB)]
        qreg = sb("qreg", [P, 2048])
        qT = [view(qreg, 1024 * b, 1024, BF16).rearrange("p (h q) -> p h q", h=H0) for b in range(NB)]
        mx = sb("mx", [P, HPG, 2])
        m4 = sb("m4", [P, HPG])
        negm = sb("negm", [P, HPG])
        nm = [sb(f"nm{b}", [P, H0, 2], BF16) for b in range(NB)]
        e_arg = [sb(f"e_arg{b}", [P, H0]) for b in range(NB)]
        e_val = [sb(f"e_val{b}", [P, H0]) for b in range(NB)]
        rec = [sb(f"rec{b}", [P, H0]) for b in range(NB)]
        o_sb = sb("o_sb", [P, P])
        wx = sb("wx", [P, KD, D + 2 * NS])
        a_log = sb("a_log", [P, KD, NS])
        ea = sb("ea", [P, KD, NS])
        d_row = oreg[:, 0:256]
        dt = [tmp2[b] for b in range(NB)]
        w_lora = sb("w_lora", [P, KD, 2 * D])
        w_up = oreg[:, 256:768].rearrange("p (k n) -> p k n", k=KD)
        rw1 = oreg[:, 768:896].rearrange("p (k n) -> p k n", k=KD)
        rb1 = sb("rb1", [HID0, 1])
        rw2 = sb("rw2", [HID0, NE0])
        rb2 = sb("rb2", [P, NE0])
        gates = sb("gates", [P, NE0])
        bias0 = oreg[:, 896:1152]
        top8 = [sb(f"top8_{b}", [P, 8]) for b in range(NB)]
        idx8 = [sb(f"idx8_{b}", [P, 8], U32) for b in range(NB)]
        idxf = [sb(f"idxf_{b}", [P, 8]) for b in range(NB)]
        logit = [sb(f"logit{b}", [P, NE0]) for b in range(NB)]
        coef = [sb(f"coef{b}", [P, NE0]) for b in range(NB)]
        coef2 = [sb(f"coefb{b}", [P, NE0]) for b in range(NB)]
        small = [sb(f"small{b}", [P, 8]) for b in range(NB)]
        xmask = view(reg_b, 20480, 2048, BF16)
        mask8 = reg_b[0:1, 16384:16384 + NB * KEYS // 4]
        mask_row = xmask[0:1, :]
        m3 = [sb(f"m3_{b}", [P, 4]) for b in range(NB)]
        tab = qreg
        cos2 = tab[:, 0:64]
        sin2 = tab[:, 64:128]
        wq_n = tab[:, 128:256]
        wk_n = tab[:, 256:384]
        ct = {"q": tab[:, 384:448], "k": tab[:, 448:512], "e": tab[:, 512:576]}
        st = {"q": tab[:, 576:640], "k": tab[:, 640:704], "e": tab[:, 704:768]}
        cose = tab[:, 768:832]
        sine = tab[:, 832:896]
        w_n = {"q": wq_n, "k": wk_n, "e": wk_n}
        bias48 = tab[:, 896:1024]
        split48 = view(tab, 1024, 192, BF16).rearrange("p (t d) -> p t d", t=3)
        res48 = tab[:, 1216:1344]
        b_out = tab[:, 1344:1600]
        sinkT = tab[:, 1600:1616]
        w_c = tab[:, 1616:1618]
        b_c = tab[0:1, 1618:1619]
        rms = [tab[:, 1620 + 64 * b:1684 + 64 * b] for b in range(NB)]
        wkv = reg_b[:, 24576:25088].rearrange("p (k n) -> p k n", k=KD)
        b_kv = reg_b[0:NC, 25088:25344]
        comp = [sb(f"comp{b}", [P, 160]) for b in range(NB)]
        ckv = [reg_b[0:NC, 23552 + 512 * b:23808 + 512 * b] for b in range(NB)]
        ckr = [reg_b[0:NC, 23808 + 512 * b:23936 + 512 * b] for b in range(NB)]
        cks = [reg_b[0:NC, 23936 + 512 * b:24064 + 512 * b] for b in range(NB)]
        att = [sb(f"att{b}", [P, 32]) for b in range(NB)]
        wg = sb("wg", [P, KD, NE])
        bg = sb("bg", [P, NE])
        b1 = sb("b1", [P, NE, MF])
        b2 = sb("b2", [P, NE, MF])
        b3 = reg_b[0:NE, 25344:25600]
        comb = [sb(f"comb{b}", [P, NE]) for b in range(NB)]
        combT = reg_b[0:NE, 25600:25856]

        ps = ctx.enter_context(nc.psum_tensor("ps", [P, 8, 512], F32))
        score_a = [ps[:, 0:2, :], ps[:, 2:4, :]]
        score_b = [ps[:, 4, :], ps[:, 5, :]]

        def bank(b, i, cols=512):
            return ps[:, 4 * b + i, 0:cols]

        def bankb(i):
            return ps[:, i, :].bitcast(BF16)

        block = ctx.enter_context(nc.Block())

        @block.sync
        def _(sp):
            def load(dst, src, name):
                sp.dma_start(dst, src).then_inc(S(name), 16)

            for b in range(NB):
                load(x[b][:, :], io["x"][b], "x_in")
            load(cf[:, :], io["cf"], "const_in")
            load(cb[:, :], io["cb"], "const_in")
            for n in range(2):
                load(ctxK[:, 0, 2 * n:2 * n + 2, :], io["ctxK"][0][:, 2 * n:2 * n + 2, :], f"ctxK_in{n}")
            for i in range(3):
                load(kS[i][QROWS:SROWS, :, :], io["ones"].rearrange("r (j k) -> r j k", j=HPG), "ones_in")
            load(ctxN[:, 0, :, :], io["ctx"][0].rearrange("(c p) d -> p c d", p=P), "ctxN_in0")
            load(ctxN[:, 1, :, :], io["ctx"][1].rearrange("(c p) d -> p c d", p=P), "ctxN_in1")
            for n in range(2):
                load(ctxK[:, 1, 2 * n:2 * n + 2, :], io["ctxK"][1][:, 2 * n:2 * n + 2, :], f"ctxK_in{n + 2}")
            load(wx[:, :, :], io["wx"].rearrange("(k p) n -> p k n", p=P), "ssm_in")
            load(a_log[:, :, :], io["a_log"].rearrange("(k p) n -> p k n", p=P), "ssm_in")
            load(w_lora[:, :, :], io["w_lora"].rearrange("(k p) n -> p k n", p=P), "lora_in")
            load(rb1[:, :], io["rb1"].unsqueeze(1), "lora_in")
            load(rw2[:, :], io["rw2"], "lora_in")
            load(rb2[:, :], io["rb2"].partition_broadcast(P), "lora_in")
            load(gates[:, :], io["gates"].partition_broadcast(P), "lora_in")
            load(wg[:, :, :], io["wg"].rearrange("(k p) n -> p k n", p=P), "ffn_in")
            load(bg[:, :], io["bg"].partition_broadcast(P), "ffn_in")
            load(b1[:, :, :], io["b1"], "ffn_in")
            load(b2[:, :, :], io["b2"], "ffn_in")

            for g in range(NG):
                b, hg = divmod(g, NHG)
                sp.wait_ge(S("k3_done"), 2 * (b + 1))
                if g >= 3:
                    sp.wait_ge(S("pv_done"), NCH * (g - 2))
                for t, part in enumerate((0, 1, 2, 0, 1, 0)):
                    for half in range(2):
                        row = 32 * hg + HD0 * half
                        sp.dma_start(kS[g % 3][HD0 * t:HD0 * (t + 1), :, HALF_K * half:HALF_K * (half + 1)],
                                     ks3[row:row + HD0, part, :, :]).then_inc(S(f"kS_in{g % 3}"), 16)
                if g in (4, 5):
                    load(ctxT[:, g - 4, :, :], io["ctxT"][g - 4].rearrange("(h p) k -> p h k", p=P), f"ctxT_in{g - 4}")

            sp.wait_ge(S("x_done"), 1 * NB)
            load(d_row, io["d"].partition_broadcast(P), "d_in")
            load(w_up, io["w_up"].rearrange("(k p) n -> p k n", p=P), "lora_in")
            load(rw1, io["rw1"].rearrange("(k p) n -> p k n", p=P), "lora_in")
            load(bias0, io["bias0"].partition_broadcast(P), "bias0_in")
            load(wkv, io["wkv"].rearrange("(k p) n -> p k n", p=P), "att_in")
            load(b_kv, io["b_kv"].partition_broadcast(NC), "att_in")
            load(b3, io["b3"], "b3_in")
            load(cos2, io["cos2"], "tab_in")
            load(sin2, io["sin2"], "tab_in")
            load(cose[0:NC, :], io["cose"], "tab_in")
            load(sine[0:NC, :], io["sine"], "tab_in")
            load(wq_n, io["qn_w"].partition_broadcast(P), "tab_in")
            load(wk_n, io["kn_w"].partition_broadcast(P), "tab_in")
            load(bias48[0:48, :], io["b48"], "tab_in")
            load(b_out, io["bo"].partition_broadcast(P), "tab_in")
            load(sinkT, io["sink_kT"], "tab_in")
            load(w_c, io["wc"], "tab_in")
            load(b_c, io["bc"].unsqueeze(0), "tab_in")
            sp.wait_ge(S("x_done"), 2 * NB)
            load(mask8, io["mask"], "mask_in")
            for j in range(3):
                load(w_qkv[:, j, :, :], io["w_qkv"][j].rearrange("(k p) n -> p k n", p=P), f"wqkv_in{j}")
            load(w_o[:, :, :], io["wo"].rearrange("(h p) n -> p h n", p=P), "wo_in")
            sp.wait_ge(S("x_done"), 4 * NB)
            sp.wait_ge(S("b48_split"), 1)
            for j in range(3):
                for t in range(3):
                    sp.dma_start(bias3[32 * j + t:32 * j + t + 1, :].rearrange("o (a d) -> o a d", d=HD),
                                 split48[16 * j:16 * j + 16, t, :]).then_inc(S("bias3_in"), 16)
            for b in range(NB):
                load(cvs[32 * b + NC:32 * b + NC + 1, :, :], io["sink_v"].unsqueeze(0), "sinkv_in")
            for e in range(NE):
                if e == 0:
                    sp.wait_ge(S("proj_ps"), 12 * NB)
                if e == 3:
                    sp.wait_ge(S("x_done"), 5 * NB)
                load(w1[e], io["w1"][e].rearrange("(k p) n -> p k n", p=P), f"expert_in{e}")
                load(w2[e], io["w2"][e].rearrange("(k p) n -> p k n", p=P), f"expert_in{e}")
                load(w3[e], io["w3"][e].rearrange("(k p) n -> p k n", p=P), f"expert_in{e}")
            sp.wait_ge(S("x_done"), 6 * NB)
            for b in range(NB):
                sp.dma_start(out[b], x[b][:, :]).then_inc(S("out_sent"), 16)
            sp.wait_ge(S("out_sent"), 16 * NB)

        @block.gpsimd
        def _(pool):
            def inv_sqrt(t):
                for b in range(NB):
                    pool.wait_ge(S("ln_var"), NB * t + b + 1)
                    pool.tensor_tensor(rstd[b][:, :], var_eps[b][:, :], neg_half, ALU.pow)\
                        .then_inc(S("ln_rstd"), 1)

            pool.memset(onesb[:, :], 1.0).then_inc(S("ones_set"), 1)
            pool.wait_ge(S("const_in"), 32)
            inv_sqrt(0)
            for i in range(2):
                pool.memset(va[i][:, :, :, :], 0.0).then_inc(S("va_zero"), 1)
            for i in range(2):
                pool.wait_ge(S("va_zero"), 2)
                pool.memset(va[i][:, :, :, HD0:HD0 + 1], 1.0).then_inc(S("va_one"), 1)
            for g in range(NG):
                b, hg = divmod(g, NHG)
                if hg == 0:
                    pool.wait_ge(S(f"ctxN_in{b}"), 16)
                if g >= 2:
                    pool.wait_ge(S("oT_ready"), g - 1)
                src = ctxN[:, b, :, hg * HPG * HD0:(hg + 1) * HPG * HD0].rearrange("p c (j d) -> p c j d", j=HPG)
                pool.tensor_copy(va[g % 2][:, :, :, 0:HD0], src).then_inc(S("va_ready"), 1)
            inv_sqrt(1)
            for b in range(NB):
                pool.wait_ge(S("dtx_done"), b + 1)
                pool.wait_ge(S("bc_sb"), 8 * b + 4)
                for h in range(KD):
                    pool.tensor_tensor(state[b][:, h], tmp[b][:, h * P:(h + 1) * P].unsqueeze(1).to_broadcast([P, NS, P]),
                                       bc_row[b][:, 0:NS, :], ALU.mult).then_inc(S("dbx_done"), 1)
            inv_sqrt(2)
            inv_sqrt(3)
            inv_sqrt(4)
            for b in range(NB):
                pool.wait_ge(S("cms_done"), b + 1)
                pool.tensor_tensor(comp[b][0:NC, 40:41], comp[b][0:NC, 39:40], neg_half[0:NC, :], ALU.pow)\
                    .then_inc(S("crstd_done"), 1)
            for b in range(NB):
                for i in range(2):
                    pool.wait_ge(S("ms_done"), 2 * b + i + 1)
                    pool.tensor_tensor(rms[b][:, 16 + 32 * i:32 + 32 * i], rms[b][:, 32 * i:16 + 32 * i],
                                       neg_half.to_broadcast([P, NH]), ALU.pow).then_inc(S("qkrstd_done"), 1)
            inv_sqrt(5)

        @block.scalar
        def _(sc):
            steps = [0]

            def link(ins):
                steps[0] += 1
                ins.then_inc(S("act_step"), 1)
                sc.wait_ge(S("act_step"), steps[0])

            def transposed_x(t, bank_of=None):
                for b in range(NB):
                    sc.wait_ge(S("xT_ps"), NB * (t - 1) + b + 1)
                    sc.copy(xT[b], bank(b, 0, D).rearrange("p (k q) -> p k q", k=KD)).then_inc(S("xT_sb"), 1)

            def key_part1(n):
                b, pair = divmod(n, 2)
                if b == 1:
                    sc.wait_ge(S("kS_in0"), 16 * REP * 2)
                sc.wait_ge(S(f"ctxK_in{n}"), 16)
                sc.copy(ks3[:, 0, 2 * pair:2 * pair + 2, :], ctxK[:, b, 2 * pair:2 * pair + 2, :])\
                    .then_inc(S("k1_done"), 1)

            def key_part2(n):
                pair = n % 2
                sc.wait_ge(S("kres_done"), n + 1)
                sc.copy(ks3[:, 1, 2 * pair:2 * pair + 2, :], kres.rearrange("p (j k) -> p j k", j=2))\
                    .then_inc(S("k2_done"), 1)

            key_part1(0)
            key_part1(1)
            key_part2(0)
            key_part2(1)
            for b in range(NB):
                sc.wait_ge(S("qT_ps"), b + 1)
                for i in range(2):
                    sc.copy(qT[b][0:QROWS, 8 * i:8 * i + 8, :],
                            bankb(2 * b + i)[0:QROWS, :].rearrange("p (h q) -> p h q", h=8))\
                        .then_inc(S("qT_sb"), 1)

            def max_rows(g):
                b, hg = divmod(g, NHG)
                sc.wait_ge(S("nmT_ready"), g + 1)
                sc.copy(qT[b][QROWS:SROWS, HPG * hg:HPG * (hg + 1), :],
                        bankb(6)[0:2, 0:HPG * P].rearrange("p (j q) -> p j q", j=HPG)).then_inc(S("nm_rows"), 1)

            max_rows(0)
            for g in range(NG):
                for c in range(NCH):
                    n = NCH * g + c
                    if (g, c) == (1, 12):
                        key_part1(2)
                    if (g, c) == (2, 2):
                        key_part2(2)
                    if (g, c) == (2, 4):
                        key_part1(3)
                    if (g, c) == (2, 8):
                        key_part2(3)
                    if g >= 1 and c == 3:
                        sc.wait_ge(S("oT_ready"), g)
                        pb, pg = divmod(g - 1, NHG)
                        sc.copy(o_all[pb][:, pg], ps[:, 6, 0:2 * P].rearrange("p (u j w) -> p u j w", u=2, j=HPG))\
                            .then_inc(S("o_all"), 1)
                    sc.wait_ge(S("score_b"), n + 1)
                    if n >= 3:
                        sc.wait_ge(S("pv_done"), n - 2)
                    sc.activation(pT[n % 3], score_b[n % 2], ACT.Exp).then_inc(S("exp_done"), 1)
                if g + 1 < NG:
                    max_rows(g + 1)
                sc.wait_ge(S("pv_done"), NCH * (g + 1))
                sc.copy(o_sb[:, :], ps[:, 7, 0:P]).then_inc(S("o_sb"), 1)
            sc.wait_ge(S("oT_ready"), NG)
            sc.copy(o_all[1][:, NHG - 1], ps[:, 6, 0:2 * P].rearrange("p (u j w) -> p u j w", u=2, j=HPG))\
                .then_inc(S("o_all"), 1)
            for b in range(NB):
                sc.wait_ge(S("e_arg"), b + 1)
                sc.activation(e_val[b][:, :], e_arg[b][:, :], ACT.Exp).then_inc(S("e_val"), 1)

            sc.wait_ge(S("ssm_in"), 32)
            sc.activation(ea[:, :, :], a_log[:, :, :], ACT.Exp).then_inc(S("ea_done"), 1)
            transposed_x(1)
            for b in range(NB):
                sc.wait_ge(S("z_ready"), b + 1)
                link(sc.activation(tmp[b][:, :], bank(b, 1, D), ACT.Abs))
                link(sc.activation(tmp[b][:, :], tmp[b][:, :], ACT.Exp, scale=-1.0))
                sc.activation(tmp[b][:, :], tmp[b][:, :], ACT.Ln, bias=1.0).then_inc(S("log_done"), 1)
            for b in range(NB):
                for i in range(8):
                    sc.wait_ge(S("bc_ps"), 8 * b + i + 1)
                    sc.copy(bc_row[b][:, 4 * i:4 * i + 4, :],
                            bank(b, 2 + i % 2).rearrange("p (n l) -> p n l", n=4)).then_inc(S("bc_sb"), 1)
                for h in range(KD):
                    sc.wait_ge(S("dta_done"), KD * b + h + 1)
                    sc.activation(decay[b][:, h], decay[b][:, h], ACT.Exp, scale=-1.0).then_inc(S("decay_done"), 1)

            transposed_x(2)
            for b in range(NB):
                sc.wait_ge(S("hid_lin"), b + 1)
                sc.activation(tmp2[b][0:HID0, 0:P], tmp[b][0:HID0, 0:P], ACT.Exp, scale=-1.0)\
                    .then_inc(S("hid_exp"), 1)
            for b in range(NB):
                sc.wait_ge(S("gap_done"), b + 1)
                sc.activation(small[b][:, 1:2], small[b][:, 0:1], ACT.Exp).then_inc(S("gap_exp"), 1)
            for b in range(NB):
                sc.wait_ge(S("wxaT_ps"), b + 1)
                sc.copy(tmp2[b][:, :], bank(b, 0, D)).then_inc(S("wxaT_sb"), 1)

            transposed_x(3)
            for b in range(NB):
                sc.wait_ge(S("m3_done"), b + 1)
                sc.activation(p3[b].rearrange("p (i k) -> p i k", i=4), ps[:, 4 * b:4 * b + 4, :], ACT.Exp,
                              bias=m3[b][:, 1:2], scale=1.0 / 16.0, accum_out=m3[b][:, 2:3])\
                    .then_inc(S("p3_done"), 1)
            for i in range(4):
                for b in range(NB):
                    sc.wait_ge(S("p3T_ps"), NB * i + b + 1)
                    sc.copy(p3T[b][:, 4 * i:4 * i + 4, :],
                            bank(b, i).rearrange("p (c q) -> p c q", c=4)).then_inc(S("p3T_sb"), 1)

            transposed_x(4)
            for b in range(NB):
                sc.wait_ge(S("c_shift"), b + 1)
                sc.activation(ckr[b][0:1, :], ckr[b][0:1, :], ACT.Exp).then_inc(S("c_exp"), 1)
            for b in range(NB):
                sc.wait_ge(S("entT_ps"), b + 1)
                sc.copy(comp[b][:, 0:2 * NC], bank(b, 2, 2 * NC)).then_inc(S("entT_sb"), 1)
            for b in range(NB):
                for i in range(12):
                    sc.wait_ge(S("proj_ps"), 12 * b + i + 1)
                    j, n = divmod(i, 4)
                    dst = (qf, kf, lv)[j][b][:, 4 * n:4 * n + 4, 0:HD]
                    sc.copy(dst, bank(b, i % 2).rearrange("p (h d) -> p h d", h=4)).then_inc(S("proj_sb"), 1)
                    if n == 3 and j < 2:
                        sc.wait_ge(S("proj_sb"), 12 * b + i + 1)
                        if j == 1:
                            sc.wait_ge(S("q_roped"), b + 1)
                        elif b > 0:
                            sc.wait_ge(S("k_roped"), b)
                        sc.activation(squares, (qf, kf)[j][b][:, :, 0:HD], ACT.Square).then_inc(S("sq_done"), 1)
                sc.wait_ge(S("ckT_ps"), b + 1)
                sc.copy(comp[b][:, 16:16 + NC], bank(b, 3, NC)).then_inc(S("ckT_sb"), 1)
                for i in range(4):
                    sc.wait_ge(S("qkT_ps"), 8 * b + i + 1)
                    sc.copy(qf[b][:, 4 * i:4 * i + 4, :],
                            bank(b, i % 2).rearrange("p (h d) -> p h d", h=4)).then_inc(S("qkT_sb"), 1)
                sc.wait_ge(S("ckT_sb"), b + 1)
                sc.copy(kf[b][:, :, HD:HD + NC], comp[b][:, 16:16 + NC].unsqueeze(1).to_broadcast([P, NH, NC]))\
                    .then_inc(S("kT_tail"), 1)
                sc.copy(kf[b][:, :, HD + NC:SW], sinkT.unsqueeze(2)).then_inc(S("kT_tail"), 1)
                for i in range(4):
                    sc.wait_ge(S("qkT_ps"), 8 * b + 4 + i + 1)
                    sc.copy(kf[b][:, 4 * i:4 * i + 4, 0:HD],
                            bank(b, i % 2).rearrange("p (h d) -> p h d", h=4)).then_inc(S("qkT_sb"), 1)
            for g in range(NHG):
                for b in range(NB):
                    n = NB * g + b
                    sc.wait_ge(S("nb_done"), n + 1)
                    for j in range(HPG):
                        s = ps[:, 4 * b + j // 2, 256 * (j % 2):256 * (j % 2) + SW]
                        scale = rms[b][:, 16 + HPG * g + j:17 + HPG * g + j]
                        sc.activation(pr[b][:, j, 0:P], s[:, 0:P], ACT.Exp, bias=att[b][:, 8 + j:9 + j],
                                      scale=scale, accum_out=att[b][:, 16 + j:17 + j]).then_inc(S("pr_exp"), 1)
                        sc.activation(pr[b][:, j, P:SW], s[:, P:SW], ACT.Exp, bias=att[b][:, 12 + j:13 + j],
                                      scale=scale, accum_out=att[b][:, 20 + j:21 + j]).then_inc(S("pr_exp"), 1)
                for b in range(NB):
                    n = NB * g + b
                    sc.wait_ge(S("prT_ps"), n + 1)
                    sc.copy(prT[b], bank(b, 2).rearrange("p (j q) -> p j q", j=HPG)).then_inc(S("prT_sb"), 1)
                    sc.copy(pcT[b][32 * b:32 * b + NC + 1, :, :],
                            bank(b, 3)[0:NC + 1, :].rearrange("p (j q) -> p j q", j=HPG)).then_inc(S("prT_sb"), 1)
                for b in range(NB):
                    n = NB * g + b
                    sc.wait_ge(S("mT_ps"), n + 1)
                    sc.copy(qf[b][:, HPG * g:HPG * (g + 1), :],
                            bank(b, 3).rearrange("p (j q) -> p j q", j=HPG)).then_inc(S("mT_sb"), 1)

            transposed_x(5)
            for b in range(NB):
                sc.wait_ge(S("g_shift"), b + 1)
                sc.activation(comb[b][:, :], logit[b][:, 0:NE], ACT.Exp, accum_out=small[b][:, 2:3])\
                    .then_inc(S("g_exp"), 1)
            for e in range(NE):
                for m in range(MF):
                    sc.wait_ge(S("h1_ps"), MF * e + m + 1)
                    sc.activation((h1, h1b)[e % 2][:, m, :], ps[:, 2 + m % 2, 0:NB * P], ACT.Gelu,
                                  bias=b1[:, e, m:m + 1]).then_inc(S("h1_sb"), 1)
                if e == 0:
                    sc.wait_ge(S("combT_ps"), 1)
                    sc.copy(combT, ps[0:NE, 0, 0:NB * P]).then_inc(S("combT_sb"), 1)
                for m in range(MF):
                    sc.wait_ge(S("h2_ps"), MF * e + m + 1)
                    sc.activation((h2, h2b)[e % 2][:, m, :], ps[:, 4 + m % 2, 0:NB * P], ACT.Gelu,
                                  bias=b2[:, e, m:m + 1]).then_inc(S("h2_sb"), 1)

        @block.tensor
        def _(pe):
            def x_to_columns(t):
                for b in range(NB):
                    pe.wait_ge(S("xn_done"), NB * t + b + 1)
                    for k in range(KD):
                        mm = pe.transpose(bank(b, 0)[:, k * P:(k + 1) * P], xn[b][:, k * P:(k + 1) * P], ident)
                    mm.then_inc(S("xT_ps"), 1)

            pe.wait_ge(S("const_in"), 32)
            for b in range(NB):
                pe.wait_ge(S("q_split"), b + 1)
                for h in range(H0):
                    mm = pe.transpose(bankb(2 * b + h // 8)[0:QROWS, P * (h % 8):P * (h % 8 + 1)],
                                      q_split[b][:, h].rearrange("p t d -> p (t d)"), identb)
                mm.then_inc(S("qT_ps"), 1)

            def scores_for_max(g, piece):
                b, hg = divmod(g, NHG)
                j, half = divmod(piece, 2)
                m = 8 * g + piece
                if piece == 0:
                    pe.wait_ge(S(f"kS_in{g % 3}"), 16 * REP * (g // 3 + 1))
                    pe.wait_ge(S("qT_sb"), 4)
                if m >= 2:
                    pe.wait_ge(S("max_done"), m - 1)
                q = qT[b][0:QROWS, HPG * hg + j, :]
                k = kS[g % 3][0:QROWS, j, 1024 * half:1024 * (half + 1)]
                pe.matmul(score_a[m % 2][:, 0, :], q, k[:, 0:512], start=True, stop=True)
                if half == 0:
                    mm = pe.matmul(score_a[m % 2][:, 1, :], q, k[:, 512:1024], start=True, stop=True)
                else:
                    pe.matmul(score_a[m % 2][:, 1, 0:384], q, k[:, 512:896], start=True, stop=True)
                    pe.matmul(score_a[m % 2][:, 1, 384:512], q, k[:, 896:1024], start=True, stop=False)
                    mm = pe.matmul(score_a[m % 2][:, 1, 384:512], identb, hide_q, start=False, stop=True)
                mm.then_inc(S("score_a"), 1)

            def max_to_rows(g):
                b, hg = divmod(g, NHG)
                pe.wait_ge(S("nm_done"), g + 1)
                if g >= 2:
                    pe.wait_ge(S("o_all"), g - 1)
                for j in range(HPG):
                    mm = pe.transpose(bankb(6)[0:2, P * j:P * (j + 1)], nm[b][:, HPG * hg + j, :], identb)
                mm.then_inc(S("nmT_ready"), 1)

            def scores_shifted(g, c):
                b, hg = divmod(g, NHG)
                n = NCH * g + c
                if c == 0:
                    pe.wait_ge(S("nm_rows"), g + 1)
                    pe.wait_ge(S("ones_in"), 48)
                if n >= 2:
                    pe.wait_ge(S("exp_done"), n - 1)
                last = c == NCH - 1
                for j in range(HPG):
                    cols = score_b[n % 2][:, P * j:P * (j + 1)]
                    if last:
                        pe.matmul(cols, identb, hide_k, start=True, stop=False)
                    mm = pe.matmul(cols, kS[g % 3][0:SROWS, j, P * c:P * (c + 1)], qT[b][0:SROWS, HPG * hg + j, :],
                                   start=not last, stop=True)
                mm.then_inc(S("score_b"), 1)

            def values(g, c):
                n = NCH * g + c
                if c == 0:
                    pe.wait_ge(S("va_ready"), g + 1)
                    pe.wait_ge(S("va_one"), 2)
                    if g >= 1:
                        pe.wait_ge(S("o_sb"), g)
                pe.wait_ge(S("exp_done"), n + 1)
                for j in range(HPG):
                    mm = pe.matmul(ps[VW * j:VW * (j + 1), 7, 0:P], va[g % 2][:, c, j, :], pT[n % 3][:, P * j:P * (j + 1)],
                                   start=c == 0, stop=c == NCH - 1)
                mm.then_inc(S("pv_done"), 1)

            def outputs_to_rows(g):
                pe.wait_ge(S("o_sb"), g + 1)
                if g + 1 < NG:
                    pe.wait_ge(S("nm_rows"), g + 2)
                pe.transpose(ps[:, 6, 0:P], o_sb[:, :], ident)
                pe.matmul(ps[:, 6, P:2 * P], later, va[g % 2][:, NCH - 1].rearrange("p j w -> p (j w)"),
                          start=True, stop=True).then_inc(S("oT_ready"), 1)

            for piece in range(8):
                scores_for_max(0, piece)
            max_to_rows(0)
            for g in range(NG):
                for c in range(NCH):
                    scores_shifted(g, c)
                    if c == NCH - 1 and g + 1 < NG:
                        max_to_rows(g + 1)
                    if c > 0:
                        values(g, c - 1)
                    if c == 2 and g >= 1:
                        outputs_to_rows(g - 1)
                    if g + 1 < NG and c in (0, 2, 3, 5, 6, 8, 9, 11):
                        scores_for_max(g + 1, (0, 2, 3, 5, 6, 8, 9, 11).index(c))
                values(g, NCH - 1)
            outputs_to_rows(NG - 1)

            x_to_columns(1)
            pe.wait_ge(S("ssm_in"), 32)
            for b in range(NB):
                pe.wait_ge(S("xT_sb"), b + 1)
                for h in range(KD):
                    for k in range(KD):
                        mm = pe.matmul(bank(b, 1)[:, P * h:P * (h + 1)], wx[:, k, P * h:P * (h + 1)], xT[b][:, k, :],
                                       start=k == 0, stop=k == KD - 1)
                mm.then_inc(S("z_ready"), 1)
            for b in range(NB):
                for i in range(8):
                    if i >= 2:
                        pe.wait_ge(S("bc_sb"), 8 * b + i - 1)
                    for r in range(4):
                        col = D + 4 * i + r
                        for k in range(KD):
                            mm = pe.matmul(bank(b, 2 + i % 2)[:, P * r:P * (r + 1)],
                                           wx[:, k, col:col + 1].to_broadcast([P, P]), xT[b][:, k, :],
                                           start=k == 0, stop=k == KD - 1)
                    mm.then_inc(S("bc_ps"), 1)
            for b in range(NB):
                for h in range(KD):
                    pe.wait_ge(S("hc_done"), KD * b + h + 1)
                    for n in range(NS):
                        mm = pe.matmul(bank(b, 0)[:, P * h:P * (h + 1)], state[b][:, h, n, :], ident,
                                       start=n == 0, stop=n == NS - 1)
                mm.then_inc(S("y_ps"), 1)

            for b in range(NB):
                pe.wait_ge(S("x_done"), 1 * NB + b + 1)
            x_to_columns(2)
            pe.wait_ge(S("lora_in"), 112)
            for b in range(NB):
                pe.wait_ge(S("xT_sb"), 2 + b + 1)
                for k in range(KD):
                    mm = pe.matmul(bank(b, 1)[0:HID0, 0:P], rw1[:, k, :], xT[b][:, k, :], start=k == 0, stop=k == KD - 1)
                mm.then_inc(S("hid_ps"), 1)
                for k in range(KD):
                    mm = pe.matmul(bank(b, 2, D), xT[b][:, k, :], w_lora[:, k, D:2 * D], start=k == 0, stop=k == KD - 1)
                mm.then_inc(S("xa_ps"), 1)
            for b in range(NB):
                pe.wait_ge(S("hid_sb"), b + 1)
                pe.matmul(bank(b, 3)[:, 0:NE0], tmp[b][0:HID0, P:2 * P], rw2[:, :], start=True, stop=True)\
                    .then_inc(S("logit_ps"), 1)
                for k in range(KD):
                    pe.matmul(bank(b, 1, D), xT[b][:, k, :], w_lora[:, k, 0:D], start=k == 0, stop=False)
            for b in range(NB):
                pe.wait_ge(S("wxa_done"), b + 1)
                for k in range(KD):
                    mm = pe.transpose(bank(b, 0)[:, k * P:(k + 1) * P], tmp[b][:, k * P:(k + 1) * P], ident)
                mm.then_inc(S("wxaT_ps"), 1)
            for b in range(NB):
                pe.wait_ge(S("wxaT_sb"), b + 1)
                for k in range(KD):
                    mm = pe.matmul(bank(b, 1, D), tmp2[b][:, k * P:(k + 1) * P], w_up[:, k, :], start=False,
                                   stop=k == KD - 1)
                mm.then_inc(S("lora_ps"), 1)

            x_to_columns(3)
            pe.wait_ge(S("ones_set"), 1)
            pe.wait_ge(S("mask_row"), 2)
            for b in range(NB):
                pe.wait_ge(S("xT_sb"), 4 + b + 1)
                pe.wait_ge(S(f"ctxT_in{b}"), 16)
                for i in range(4):
                    for k in range(KD):
                        pe.matmul(bank(b, i), xT[b][:, k, :], ctxT[:, b, k, 512 * i:512 * (i + 1)],
                                  start=k == 0, stop=False)
                    mm = pe.matmul(bank(b, i), onesb[0:1, :], mask_row[0:1, KEYS * b + 512 * i:KEYS * b + 512 * (i + 1)],
                                   start=False, stop=True)
                mm.then_inc(S("s3_ps"), 1)
            for i in range(4):
                for b in range(NB):
                    if i == 0:
                        pe.wait_ge(S("p3_done"), b + 1)
                    for c in range(4):
                        mm = pe.transpose(bank(b, i)[:, P * c:P * (c + 1)],
                                          p3[b][:, P * (4 * i + c):P * (4 * i + c + 1)], ident)
                    mm.then_inc(S("p3T_ps"), 1)
            for b in range(NB):
                for c in range(NCH):
                    if c % 4 == 0:
                        pe.wait_ge(S("p3T_sb"), NB * (c // 4) + b + 1)
                    mm = pe.matmul(bank(b, 0, D), p3T[b][:, c, :], ctxN[:, b, c, :], start=c == 0, stop=c == NCH - 1)
                mm.then_inc(S("o3_ps"), 1)

            for b in range(NB):
                pe.wait_ge(S("x_done"), 3 * NB + b + 1)
            x_to_columns(4)
            pe.wait_ge(S("tab_in"), 176)
            pe.wait_ge(S("att_in"), 32)
            for b in range(NB):
                pe.wait_ge(S("xT_sb"), 6 + b + 1)
                for k in range(KD):
                    mm = pe.matmul(bank(b, 2)[0:1, 0:P], w_c[:, k:k + 1], xT[b][:, k, :], start=k == 0, stop=k == KD - 1)
                mm.then_inc(S("c_ps"), 1)

            def projections(b):
                for i in range(12):
                    j, n = divmod(i, 4)
                    if n == 0:
                        pe.wait_ge(S(f"wqkv_in{j}"), 16)
                        pe.wait_ge(S("bias3_in"), 144)
                    if i >= 2:
                        pe.wait_ge(S("proj_sb"), 12 * b + i - 1)
                    pe.matmul(bank(b, i % 2), onesb[32 * j:32 * j + 3, :], bias3[32 * j:32 * j + 3, 512 * n:512 * (n + 1)],
                              start=True, stop=False)
                    for k in range(KD):
                        mm = pe.matmul(bank(b, i % 2), xT[b][:, k, :], w_qkv[:, j, k, 512 * n:512 * (n + 1)],
                                       start=False, stop=k == KD - 1)
                    mm.then_inc(S("proj_ps"), 1)

            for b in range(NB):
                pe.wait_ge(S("c_soft"), b + 1)
                pe.matmul(bank(b, 3)[:, 0:1], ckr[b][0:1, :], ident[0:1, 0:1], start=True, stop=True)\
                    .then_inc(S("ccol_ps"), 1)
            for b in range(NB):
                pe.wait_ge(S("in_blk"), b + 1)
                for k in range(KD):
                    mm = pe.matmul(bank(b, 2)[:, NC * k:NC * (k + 1)], xn[b][:, P * k:P * (k + 1)],
                                   comp[b][:, 24:24 + NC], start=True, stop=True)
                mm.then_inc(S("entT_ps"), 1)
            for b in range(NB):
                pe.wait_ge(S("entT_sb"), b + 1)
                for k in range(KD):
                    mm = pe.matmul(bank(b, 3)[0:NC, 0:2 * HD], comp[b][:, NC * k:NC * (k + 1)], wkv[:, k, :],
                                   start=k == 0, stop=k == KD - 1)
                mm.then_inc(S("ckv_ps"), 1)
            for b in range(NB):
                projections(b)
                pe.wait_ge(S("ck_roped"), b + 1)
                pe.transpose(bank(b, 3)[:, 0:NC], ckr[b][:, :], ident[0:NC, 0:NC]).then_inc(S("ckT_ps"), 1)
                for i in range(8):
                    if i == 0:
                        pe.wait_ge(S("q_roped"), b + 1)
                        pe.wait_ge(S("proj_sb"), 12 * (b + 1))
                    if i == 4:
                        pe.wait_ge(S("k_roped"), b + 1)
                    if i >= 2:
                        pe.wait_ge(S("qkT_sb"), 8 * b + i - 1)
                    for c in range(4):
                        mm = pe.transpose(bank(b, i % 2)[:, P * c:P * (c + 1)], roped[:, 4 * (i % 4) + c, :], ident)
                    mm.then_inc(S("qkT_ps"), 1)
            for b in range(NB):
                pe.wait_ge(S("kT_tail"), 2 * (b + 1))
                pe.wait_ge(S("qkT_sb"), 8 * (b + 1))
            pe.wait_ge(S("cvs_done"), 2)
            pe.wait_ge(S("sinkv_in"), 32)
            for g in range(NHG):
                for b in range(NB):
                    n = NB * g + b
                    if g >= 1:
                        pe.wait_ge(S("pr_exp"), 8 * (n - NB + 1))
                    for j in range(HPG):
                        h = HPG * g + j
                        s = ps[:, 4 * b + j // 2, 256 * (j % 2):256 * (j % 2) + SW]
                        pe.matmul(s, qf[b][:, h, :], kf[b][:, h, :], start=True, stop=False)
                        mm = pe.matmul(s, identb, hide_s, start=False, stop=True)
                    mm.then_inc(S("s4_ps"), 1)
                for b in range(NB):
                    n = NB * g + b
                    pe.wait_ge(S("pr_norm"), 2 * (n + 1))
                    if g >= 1:
                        pe.wait_ge(S("prT_sb"), 2 * (n - NB + 1))
                        pe.wait_ge(S("mT_sb"), n - NB + 1)
                    for j in range(HPG):
                        pe.transpose(bank(b, 2)[:, P * j:P * (j + 1)], pr[b][:, j, 0:P], ident)
                    for j in range(HPG):
                        mm = pe.transpose(bank(b, 3)[0:NC + 1, P * j:P * (j + 1)], pr[b][:, j, P:SW], ident)
                    mm.then_inc(S("prT_ps"), 1)
                for b in range(NB):
                    n = NB * g + b
                    pe.wait_ge(S("prT_sb"), 2 * (n + 1))
                    for j in range(HPG):
                        h = HPG * g + j
                        pe.matmul(bank(b, 3)[:, P * j:P * (j + 1)], lv[b][:, h, :], prT[b][:, j, :], start=True,
                                  stop=False)
                        mm = pe.matmul(bank(b, 3)[:, P * j:P * (j + 1)], cvs[32 * b:32 * b + NC + 1, h, :],
                                       pcT[b][32 * b:32 * b + NC + 1, j, :], start=False, stop=True)
                    mm.then_inc(S("mT_ps"), 1)
            pe.wait_ge(S("wo_in"), 16)
            for b in range(NB):
                pe.wait_ge(S("mT_sb"), NB * NHG)
                pe.wait_ge(S("pr_exp"), 8 * NB * NHG)
                for h in range(NH):
                    mm = pe.matmul(bank(b, 0, D), qf[b][:, h, :], w_o[:, h, :], start=h == 0, stop=h == NH - 1)
                mm.then_inc(S("o4_ps"), 1)

            for b in range(NB):
                pe.wait_ge(S("x_done"), 4 * NB + b + 1)
            x_to_columns(5)
            pe.wait_ge(S("ffn_in"), 64)
            for b in range(NB):
                pe.wait_ge(S("xT_sb"), 8 + b + 1)
                for k in range(KD):
                    mm = pe.matmul(bank(b, 1)[:, 0:NE], xT[b][:, k, :], wg[:, k, :], start=k == 0, stop=k == KD - 1)
                mm.then_inc(S("g_ps"), 1)

            def hidden1(e):
                pe.wait_ge(S(f"expert_in{e}"), 48)
                for m in range(MF):
                    n = MF * e + m
                    if n >= 2:
                        pe.wait_ge(S("h1_sb"), n - 1)
                    for k in range(KD):
                        mm = pe.matmul(ps[:, 2 + m % 2, 0:NB * P], w1[e][:, k, P * m:P * (m + 1)], xT2[:, k, :],
                                       start=k == 0, stop=k == KD - 1)
                    mm.then_inc(S("h1_ps"), 1)

            def hidden2(e):
                pe.wait_ge(S("h1_sb"), MF * (e + 1))
                for m in range(MF):
                    n = MF * e + m
                    if n >= 2:
                        pe.wait_ge(S("h2_sb"), n - 1)
                    for k in range(MF):
                        mm = pe.matmul(ps[:, 4 + m % 2, 0:NB * P], w2[e][:, k, P * m:P * (m + 1)],
                                       (h1, h1b)[e % 2][:, k, :], start=k == 0, stop=k == MF - 1)
                    mm.then_inc(S("h2_ps"), 1)

            def expert_out(e):
                pe.wait_ge(S("h2_sb"), MF * (e + 1))
                for b in range(NB):
                    if e >= 1:
                        pe.wait_ge(S("eo_added"), NB * (e - 1) + b + 1)
                    for k in range(MF):
                        mm = pe.matmul(ps[:, 6 + b, 0:D], (h2, h2b)[e % 2][:, k, P * b:P * (b + 1)], w3[e][:, k, :],
                                       start=k == 0, stop=k == MF - 1)
                    mm.then_inc(S("eo_ps"), 1)

            pe.wait_ge(S("g_read"), NB)
            for e in range(NE):
                hidden1(e)
                if e == 0:
                    for b in range(NB):
                        pe.wait_ge(S("comb_done"), b + 1)
                        mm = pe.transpose(ps[0:NE, 0, P * b:P * (b + 1)], comb[b][:, :], ident)
                    mm.then_inc(S("combT_ps"), 1)
                    pe.wait_ge(S("combT_sb"), 1)
                    pe.wait_ge(S("b3_in"), 16)
                    for b in range(NB):
                        mm = pe.matmul(ps[:, b, 0:D], combT[:, P * b:P * (b + 1)], b3, start=True, stop=True)
                        mm.then_inc(S("b3_ps"), 1)
                else:
                    expert_out(e - 1)
                hidden2(e)
            expert_out(NE - 1)

        @block.vector
        def _(ve):
            steps = [0]

            def link(ins):
                steps[0] += 1
                ins.then_inc(S("dve_step"), 1)
                ve.wait_ge(S("dve_step"), steps[0])

            def layer_norm(t):
                for b in range(NB):
                    link(ve.bn_stats(stats[b][:, :], x[b][:, :]))
                    link(ve.bn_aggr(mean_var[b][:, :], stats[b][:, :]))
                    ve.tensor_scalar(var_eps[b][:, :], mean_var[b][:, 1:2], 1e-5, None, ALU.add)\
                        .then_inc(S("ln_var"), 1)
                for b in range(NB):
                    ve.wait_ge(S("ln_rstd"), NB * t + b + 1)
                    ve.tensor_scalar(xn[b][:, :], x[b][:, :], mean_var[b][:, 0:1], rstd[b][:, :],
                                     ALU.subtract, ALU.mult).then_inc(S("xn_done"), 1)

            ve.wait_ge(S("x_in"), 32)
            layer_norm(0)

            def key_residue(n):
                b, pair = divmod(n, 2)
                ve.wait_ge(S("k1_done"), n + 1)
                if n >= 1:
                    ve.wait_ge(S("k3_done"), n)
                ve.tensor_tensor(kres.rearrange("p (j k) -> p j k", j=2), ctxK[:, b, 2 * pair:2 * pair + 2, :],
                                 ks3[:, 0, 2 * pair:2 * pair + 2, :], ALU.subtract).then_inc(S("kres_done"), 1)

            def key_part3(n):
                pair = n % 2
                ve.wait_ge(S("k2_done"), n + 1)
                ve.tensor_tensor(ks3[:, 2, 2 * pair:2 * pair + 2, :], kres.rearrange("p (j k) -> p j k", j=2),
                                 ks3[:, 1, 2 * pair:2 * pair + 2, :], ALU.subtract).then_inc(S("k3_done"), 1)

            for n in range(2):
                key_residue(n)
                key_part3(n)
            ve.wait_ge(S("xn_done"), NB)
            for b in range(NB):
                q = tmp[b][:, :].rearrange("p (h d) -> p h d", h=H0)
                r = tmp2[b][:, :].rearrange("p (h d) -> p h d", h=H0)
                link(ve.tensor_scalar(tmp[b][:, :], xn[b][:, :], 1.0 / math.sqrt(HD0), None, ALU.mult))
                link(ve.tensor_copy(q_split[b][:, :, 0:3, :], q.unsqueeze(2).to_broadcast([P, H0, 3, HD0])))
                link(ve.tensor_tensor(r, q, q_split[b][:, :, 0, :], ALU.subtract))
                link(ve.tensor_copy(q_split[b][:, :, 3:5, :], r.unsqueeze(2).to_broadcast([P, H0, 2, HD0])))
                ve.tensor_tensor(q_split[b][:, :, 5, :], r, q_split[b][:, :, 3, :], ALU.subtract)\
                    .then_inc(S("q_split"), 1)
            for g in range(NG):
                b, hg = divmod(g, NHG)
                for piece in range(8):
                    m = 8 * g + piece
                    ve.wait_ge(S("score_a"), m + 1)
                    ve.reduce_max(mx[:, piece // 2, piece % 2:piece % 2 + 1],
                                  score_a[m % 2].rearrange("p i k -> p (i k)"), X_AXIS).then_inc(S("max_done"), 1)
                    if (g, piece) == (3, 1):
                        key_part3(2)
                    if (g, piece) == (3, 3):
                        key_residue(3)
                    if (g, piece) == (3, 6):
                        key_part3(3)
                ve.wait_ge(S("max_done"), 8 * g + 8)
                link(ve.tensor_tensor(m4[:, :], mx[:, :, 0], mx[:, :, 1], ALU.max))
                link(ve.tensor_scalar(negm[:, :], m4[:, :], floor0, -1.0, ALU.max, ALU.mult))
                heads = slice(HPG * hg, HPG * (hg + 1))
                link(ve.tensor_copy(nm[b][:, heads, 0], negm[:, :]))
                ve.tensor_tensor(nm[b][:, heads, 1], negm[:, :], nm[b][:, heads, 0], ALU.subtract)\
                    .then_inc(S("nm_done"), 1)
                if g == 2:
                    key_residue(2)
            for b in range(NB):
                link(ve.tensor_tensor(e_arg[b][:, :], nm[b][:, :, 0], nm[b][:, :, 1], ALU.add))
                ve.tensor_scalar(e_arg[b][:, :], e_arg[b][:, :], MASKED0, 80.0, ALU.add, ALU.min)\
                    .then_inc(S("e_arg"), 1)
            for b in range(NB):
                ve.wait_ge(S("o_all"), NHG * (b + 1))
                ve.wait_ge(S("e_val"), b + 1)
                o, u = o_all[b][:, :, 0], o_all[b][:, :, 1]
                weight = e_val[b][:, :].rearrange("p (g j) -> p g j", g=NHG).unsqueeze(3).to_broadcast([P, NHG, HPG, VW])
                link(ve.tensor_tensor(u, u, weight, ALU.mult))
                link(ve.tensor_tensor(o, o, u, ALU.add))
                r3 = rec[b][:, :].rearrange("p (g j) -> p g j", g=NHG)
                link(ve.reciprocal(r3, o[:, :, :, HD0]))
                link(ve.tensor_tensor(tmp[b][:, :].rearrange("p (g j d) -> p g j d", g=NHG, j=HPG), o[:, :, :, 0:HD0],
                                      r3.unsqueeze(3).to_broadcast([P, NHG, HPG, HD0]), ALU.mult))
                ve.tensor_tensor(x[b][:, :], x[b][:, :], tmp[b][:, :], ALU.add).then_inc(S("x_done"), 1)

            ve.wait_ge(S("x_done"), 1 * NB)
            layer_norm(1)
            for b in range(NB):
                ve.wait_ge(S("log_done"), b + 1)
                link(ve.scalar_tensor_tensor(dt[b][:, :], bank(b, 1, D), 0.0, tmp[b][:, :], ALU.max, ALU.add))
                ve.wait_ge(S("xT_sb"), b + 1)
                ve.tensor_tensor(tmp[b][:, :].rearrange("p (k l) -> p k l", k=KD),
                                 dt[b][:, :].rearrange("p (k l) -> p k l", k=KD), xT[b], ALU.mult)\
                    .then_inc(S("dtx_done"), 1)
            ve.wait_ge(S("ea_done"), 1)
            for b in range(NB):
                for h in range(KD):
                    ve.tensor_tensor(decay[b][:, h], dt[b][:, P * h:P * (h + 1)].unsqueeze(1).to_broadcast([P, NS, P]),
                                     ea[:, h, :].unsqueeze(2).to_broadcast([P, NS, P]), ALU.mult)\
                        .then_inc(S("dta_done"), 1)
            for b in range(NB):
                for h in range(KD):
                    ve.wait_ge(S("decay_done"), KD * b + h + 1)
                    link(ve.memset(decay[b][:, h, :, 0:1], 0.0))
                    ve.wait_ge(S("dbx_done"), KD * b + h + 1)
                    link(ve.tensor_tensor_scan(state[b][:, h].rearrange("p n l -> p (n l)"),
                                               decay[b][:, h].rearrange("p n l -> p (n l)"),
                                               state[b][:, h].rearrange("p n l -> p (n l)"), 0.0, ALU.mult, ALU.add))
                    ve.wait_ge(S("bc_sb"), 8 * (b + 1))
                    ve.tensor_tensor(state[b][:, h], state[b][:, h], bc_row[b][:, NS:2 * NS, :], ALU.mult)\
                        .then_inc(S("hc_done"), 1)
            ve.wait_ge(S("d_in"), 16)
            for b in range(NB):
                link(ve.tensor_tensor(tmp2[b][:, :], xn[b][:, :], d_row, ALU.mult))
                link(ve.tensor_tensor(x[b][:, :], x[b][:, :], tmp2[b][:, :], ALU.add))
                ve.wait_ge(S("y_ps"), b + 1)
                ve.tensor_tensor(x[b][:, :], bank(b, 0, D), x[b][:, :], ALU.add).then_inc(S("x_done"), 1)

            ve.wait_ge(S("x_done"), 2 * NB)
            layer_norm(2)
            ve.wait_ge(S("lora_in"), 112)
            ve.wait_ge(S("bias0_in"), 16)
            for b in range(NB):
                ve.wait_ge(S("hid_ps"), b + 1)
                ve.tensor_scalar(tmp[b][0:HID0, 0:P], bank(b, 1)[0:HID0, 0:P], rb1[:, :], None, ALU.add)\
                    .then_inc(S("hid_lin"), 1)
            for b in range(NB):
                ve.wait_ge(S("hid_exp"), b + 1)
                link(ve.tensor_scalar(tmp2[b][0:HID0, 0:P], tmp2[b][0:HID0, 0:P], 1.0, None, ALU.add))
                link(ve.reciprocal(tmp2[b][0:HID0, 0:P], tmp2[b][0:HID0, 0:P]))
                ve.wait_ge(S("hid_lin"), b + 1)
                ve.tensor_tensor(tmp[b][0:HID0, P:2 * P], tmp[b][0:HID0, 0:P], tmp2[b][0:HID0, 0:P], ALU.mult)\
                    .then_inc(S("hid_sb"), 1)
            for b in range(NB):
                ve.wait_ge(S("logit_ps"), b + 1)
                link(ve.tensor_tensor(logit[b][:, :], bank(b, 3, NE0), rb2[:, :], ALU.add))
                link(ve.tensor_tensor(logit[b][:, :], logit[b][:, :], gates[:, :], ALU.add))
                link(ve.max(top8[b][:, :], logit[b][:, :]))
                link(ve.max_index(idx8[b][:, :], top8[b][:, :], logit[b][:, :]))
                link(ve.tensor_copy(idxf[b][:, :], idx8[b][:, :]))
                ve.tensor_tensor(small[b][:, 0:1], top8[b][:, 1:2], top8[b][:, 0:1], ALU.subtract)\
                    .then_inc(S("gap_done"), 1)
            for b in range(NB):
                ve.wait_ge(S("gap_exp"), b + 1)
                link(ve.tensor_scalar(small[b][:, 2:3], small[b][:, 1:2], 1.0, None, ALU.add))
                link(ve.reciprocal(small[b][:, 3:4], small[b][:, 2:3]))
                link(ve.tensor_tensor(small[b][:, 4:5], small[b][:, 1:2], small[b][:, 3:4], ALU.mult))
                link(ve.tensor_scalar(coef[b][:, :], iota, idxf[b][:, 0:1], small[b][:, 3:4], ALU.is_equal, ALU.mult))
                link(ve.tensor_scalar(coef2[b][:, :], iota, idxf[b][:, 1:2], small[b][:, 4:5], ALU.is_equal, ALU.mult))
                link(ve.tensor_tensor(coef[b][:, :], coef[b][:, :], coef2[b][:, :], ALU.add))
                ve.wait_ge(S("xa_ps"), b + 1)
                ve.tensor_tensor(tmp[b][:, :].rearrange("p (e r) -> p e r", e=NE0),
                                 bank(b, 2, D).rearrange("p (e r) -> p e r", e=NE0),
                                 coef[b][:, :].unsqueeze(2).to_broadcast([P, NE0, RANK]), ALU.mult)\
                    .then_inc(S("wxa_done"), 1)
            ve.wait_ge(S("mask_in"), 16)
            ve.tensor_scalar(mask_row[0:1, :], mask8.bitcast(U8), 16.0e30, -16.0e30, ALU.mult, ALU.add)\
                .then_inc(S("mask_row"), 2)
            for b in range(NB):
                link(ve.tensor_tensor(x[b][:, :], x[b][:, :], bias0, ALU.add))
                ve.wait_ge(S("lora_ps"), b + 1)
                ve.tensor_tensor(x[b][:, :], bank(b, 1, D), x[b][:, :], ALU.add).then_inc(S("x_done"), 1)

            ve.wait_ge(S("x_done"), 3 * NB)
            layer_norm(3)
            for b in range(NB):
                ve.wait_ge(S("s3_ps"), b + 1)
                link(ve.reduce_max(m3[b][:, 0:1], ps[:, 4 * b:4 * b + 4, :].rearrange("p i k -> p (i k)"), X_AXIS))
                ve.tensor_scalar(m3[b][:, 1:2], m3[b][:, 0:1], -1.0 / 16.0, None, ALU.mult).then_inc(S("m3_done"), 1)
            for b in range(NB):
                ve.wait_ge(S("p3_done"), b + 1)
                link(ve.reciprocal(m3[b][:, 3:4], m3[b][:, 2:3]))
                link(ve.tensor_scalar(m3[b][:, 3:4], m3[b][:, 0:1], -8.0e30, m3[b][:, 3:4], ALU.is_gt, ALU.mult))
                ve.wait_ge(S("o3_ps"), b + 1)
                ve.scalar_tensor_tensor(x[b][:, :], bank(b, 0, D), m3[b][:, 3:4], x[b][:, :], ALU.mult, ALU.add)\
                    .then_inc(S("x_done"), 1)

            ve.wait_ge(S("tab_in"), 176)
            link(ve.tensor_copy(split48[0:48, 0, :], bias48[0:48, :]))
            link(ve.tensor_tensor(res48[0:48, :], bias48[0:48, :], split48[0:48, 0, :], ALU.subtract))
            link(ve.tensor_copy(split48[0:48, 1, :], res48[0:48, :]))
            ve.tensor_tensor(split48[0:48, 2, :], res48[0:48, :], split48[0:48, 1, :], ALU.subtract)\
                .then_inc(S("b48_split"), 1)
            for name, c, s, rows in (("q", cos2, sin2, P), ("k", cos2, sin2, P), ("e", cose, sine, NC)):
                w = w_n[name]
                link(ve.tensor_tensor(ct[name][0:rows, :], c[0:rows, :], w[0:rows, 0:ROPE], ALU.mult))
                link(ve.tensor_tensor(st[name][0:rows, 0:HALF], s[0:rows, 0:HALF], w[0:rows, HALF:ROPE], ALU.mult))
                link(ve.tensor_tensor(st[name][0:rows, HALF:ROPE], s[0:rows, HALF:ROPE], w[0:rows, 0:HALF], ALU.mult))
            ve.wait_ge(S("x_done"), 4 * NB)
            layer_norm(4)
            for b in range(NB):
                ve.wait_ge(S("c_ps"), b + 1)
                row = ckr[b][0:1, :]
                row3 = row.rearrange("p (c r) -> p c r", c=NC)
                mxb = comp[b][0:1, 120:128]
                link(ve.tensor_scalar(row, bank(b, 2)[0:1, 0:P], b_c, None, ALU.add))
                link(ve.reduce_max(mxb, row3, X_AXIS))
                ve.tensor_tensor(row3, row3, mxb.unsqueeze(2).to_broadcast([1, NC, BLK]), ALU.subtract)\
                    .then_inc(S("c_shift"), 1)
            for b in range(NB):
                row3 = ckr[b][0:1, :].rearrange("p (c r) -> p c r", c=NC)
                mxb = comp[b][0:1, 120:128]
                ve.wait_ge(S("c_exp"), b + 1)
                link(ve.reduce_sum(mxb, row3, X_AXIS))
                link(ve.reciprocal(mxb, mxb))
                ve.tensor_tensor(row3, row3, mxb.unsqueeze(2).to_broadcast([1, NC, BLK]), ALU.mult)\
                    .then_inc(S("c_soft"), 1)
            for b in range(NB):
                ve.wait_ge(S("ccol_ps"), b + 1)
                ve.tensor_scalar(comp[b][:, 24:24 + NC], in_block, bank(b, 3)[:, 0:1], None, ALU.mult)\
                    .then_inc(S("in_blk"), 1)
            for b in range(NB):
                ve.wait_ge(S("ckv_ps"), b + 1)
                ck = ckv[b][:, 0:HD]
                link(ve.tensor_tensor(ckv[b][:, :], bank(b, 3)[0:NC, 0:2 * HD], b_kv, ALU.add))
                link(ve.tensor_tensor(cks[b][:, :], ck, ck, ALU.mult))
                link(ve.reduce_sum(comp[b][0:NC, 38:39], cks[b][:, :], X_AXIS))
                ve.tensor_scalar(comp[b][0:NC, 39:40], comp[b][0:NC, 38:39], 1.0 / HD, 1e-6, ALU.mult, ALU.add)\
                    .then_inc(S("cms_done"), 1)
                ve.wait_ge(S("crstd_done"), b + 1)
                link(ve.tensor_scalar(ck, ck, comp[b][0:NC, 40:41], None, ALU.mult))
                link(ve.tensor_tensor(ckr[b][:, 0:ROPE], ck[:, 0:ROPE], ct["e"][0:NC, :], ALU.mult))
                link(ve.tensor_tensor(cks[b][:, 0:HALF], ck[:, HALF:ROPE], st["e"][0:NC, 0:HALF], ALU.mult))
                link(ve.tensor_tensor(cks[b][:, HALF:ROPE], ck[:, 0:HALF], st["e"][0:NC, HALF:ROPE], ALU.mult))
                link(ve.tensor_tensor(ckr[b][:, ROPE:HD], ck[:, ROPE:HD], wk_n[0:NC, ROPE:HD], ALU.mult))
                ve.tensor_tensor(ckr[b][:, 0:ROPE], ckr[b][:, 0:ROPE], cks[b][:, 0:ROPE], ALU.add)\
                    .then_inc(S("ck_roped"), 1)
                ve.tensor_copy(cvs[32 * b:32 * b + NC, :, :],
                               ckv[b][:, HD:2 * HD].unsqueeze(1).to_broadcast([NC, NH, HD])).then_inc(S("cvs_done"), 1)

            def rope(b, j, src, name, done):
                rows = rms[b][:, 32 * j:32 * j + 16]
                ve.wait_ge(S("sq_done"), 2 * b + j + 1)
                link(ve.reduce_sum(rows, squares, X_AXIS))
                ve.tensor_scalar(rows, rows, 1.0 / HD, 1e-6, ALU.mult, ALU.add).then_inc(S("ms_done"), 1)
                if j == 0:
                    if b > 0:
                        ve.wait_ge(S("qkT_ps"), 8 * b)
                else:
                    ve.wait_ge(S("qkT_ps"), 8 * b + 4)
                rot = squares
                both = [P, NH, ROPE]
                half = [P, NH, HALF]
                link(ve.tensor_tensor(roped[:, :, 0:ROPE], src[:, :, 0:ROPE], ct[name].unsqueeze(1).to_broadcast(both),
                                      ALU.mult))
                link(ve.tensor_tensor(rot[:, :, 0:HALF], src[:, :, HALF:ROPE],
                                      st[name][:, 0:HALF].unsqueeze(1).to_broadcast(half), ALU.mult))
                link(ve.tensor_tensor(rot[:, :, HALF:ROPE], src[:, :, 0:HALF],
                                      st[name][:, HALF:ROPE].unsqueeze(1).to_broadcast(half), ALU.mult))
                link(ve.tensor_tensor(roped[:, :, ROPE:HD], src[:, :, ROPE:HD],
                                      w_n[name][:, ROPE:HD].unsqueeze(1).to_broadcast(both), ALU.mult))
                ve.wait_ge(S("qkrstd_done"), 2 * b + j + 1)
                last = ve.tensor_tensor(roped[:, :, 0:ROPE], roped[:, :, 0:ROPE], rot[:, :, 0:ROPE], ALU.add)
                if j == 1:
                    link(last)
                    last = ve.tensor_tensor(roped, roped, rms[b][:, 48:64].unsqueeze(2).to_broadcast([P, NH, HD]),
                                            ALU.mult)
                last.then_inc(S(done), 1)

            for b in range(NB):
                rope(b, 0, qf[b], "q", "q_roped")
                link(ve.tensor_scalar(rms[b][:, 16:32], rms[b][:, 16:32], 1.0 / math.sqrt(HD), None, ALU.mult))
                rope(b, 1, kf[b][:, :, 0:HD], "k", "k_roped")
            for g in range(NHG):
                for b in range(NB):
                    n = NB * g + b
                    scores = ps[:, 4 * b:4 * b + 2, :].rearrange("p i (j s) -> p (i j) s", j=2)
                    ve.wait_ge(S("s4_ps"), n + 1)
                    link(ve.reduce_max(att[b][:, 0:4], scores[:, :, 0:P], X_AXIS))
                    link(ve.reduce_max(att[b][:, 4:8], scores[:, :, P:SW], X_AXIS))
                    factor = rms[b][:, 16 + HPG * g:20 + HPG * g].unsqueeze(1).to_broadcast([P, 2, HPG])
                    ve.scalar_tensor_tensor(att[b][:, 8:16].rearrange("p (u j) -> p u j", u=2),
                                            att[b][:, 0:8].rearrange("p (u j) -> p u j", u=2), -1.0, factor,
                                            ALU.mult, ALU.mult).then_inc(S("nb_done"), 1)
                for b in range(NB):
                    n = NB * g + b
                    ve.wait_ge(S("pr_exp"), 8 * (n + 1))
                    link(ve.reciprocal(att[b][:, 24:32], att[b][:, 16:24]))
                    link(ve.tensor_scalar(att[b][:, 24:32], att[b][:, 24:32], 0.5, None, ALU.mult))
                    ve.tensor_tensor(pr[b][:, :, 0:P], pr[b][:, :, 0:P],
                                     att[b][:, 24:28].unsqueeze(2).to_broadcast([P, HPG, P]), ALU.mult)\
                        .then_inc(S("pr_norm"), 1)
                    ve.tensor_tensor(pr[b][:, :, P:SW], pr[b][:, :, P:SW],
                                     att[b][:, 28:32].unsqueeze(2).to_broadcast([P, HPG, NC + 1]), ALU.mult)\
                        .then_inc(S("pr_norm"), 1)
            for b in range(NB):
                link(ve.tensor_tensor(x[b][:, :], x[b][:, :], b_out, ALU.add))
                ve.wait_ge(S("o4_ps"), b + 1)
                ve.tensor_tensor(x[b][:, :], bank(b, 0, D), x[b][:, :], ALU.add).then_inc(S("x_done"), 1)

            ve.wait_ge(S("x_done"), 5 * NB)
            layer_norm(5)
            for b in range(NB):
                ve.wait_ge(S("g_ps"), b + 1)
                link(ve.tensor_tensor(logit[b][:, 0:NE], bank(b, 1, NE), bg[:, :], ALU.add))
                link(ve.reduce_max(small[b][:, 0:1], logit[b][:, 0:NE], X_AXIS))
                ve.tensor_scalar(logit[b][:, 0:NE], logit[b][:, 0:NE], small[b][:, 0:1], None, ALU.subtract)\
                    .then_inc(S("g_shift"), 1)
            ve.wait_ge(S("g_shift"), NB)
            ve.engine_nop().then_inc(S("g_read"), NB)
            for b in range(NB):
                ve.wait_ge(S("g_exp"), b + 1)
                link(ve.reciprocal(small[b][:, 3:4], small[b][:, 2:3]))
                link(ve.tensor_scalar(coef[b][:, 0:NE], comb[b][:, :], small[b][:, 3:4], None, ALU.mult))
                link(ve.max(top8[b][:, :], coef[b][:, 0:NE]))
                link(ve.max_index(idx8[b][:, :], top8[b][:, :], coef[b][:, 0:NE]))
                link(ve.tensor_copy(idxf[b][:, :], idx8[b][:, :]))
                link(ve.tensor_scalar(coef[b][:, 8:16], iota[:, 0:NE], idxf[b][:, 0:1], top8[b][:, 0:1],
                                      ALU.is_equal, ALU.mult))
                link(ve.tensor_scalar(coef2[b][:, 0:NE], iota[:, 0:NE], idxf[b][:, 1:2], top8[b][:, 1:2],
                                      ALU.is_equal, ALU.mult))
                ve.tensor_tensor(comb[b][:, :], coef[b][:, 8:16], coef2[b][:, 0:NE], ALU.add)\
                    .then_inc(S("comb_done"), 1)
            for b in range(NB):
                ve.wait_ge(S("b3_ps"), b + 1)
                link(ve.tensor_tensor(x[b][:, :], ps[:, b, 0:D], x[b][:, :], ALU.add))
            for e in range(NE):
                for b in range(NB):
                    ve.wait_ge(S("eo_ps"), NB * e + b + 1)
                    if e >= 1:
                        ve.wait_ge(S("eo_added"), NB * (e - 1) + b + 1)
                    ve.scalar_tensor_tensor(x[b][:, :], ps[:, 6 + b, 0:D], comb[b][:, e:e + 1], x[b][:, :],
                                            ALU.mult, ALU.add).then_inc(S("eo_added"), 1)
            ve.wait_ge(S("eo_added"), NB * NE)
            ve.engine_nop().then_inc(S("x_done"), 6 * NB)


def constants():
    bf16 = mybir.dt.np(BF16)
    q, k = np.arange(P)[:, None], np.arange(P)[None, :]
    cf = np.zeros((P, 2 * P + 26), np.float32)
    cf[:, 0:P] = np.eye(P)
    cf[:, P:2 * P] = q > k
    cf[:, 2 * P] = MASKED0
    cf[P - 1, 2 * P] = -3.0e38
    cf[:, 2 * P + 1:2 * P + 9] = np.arange(P)[:, None] // BLK == np.arange(NC)[None, :]
    cf[:, 2 * P + 9:2 * P + 25] = np.arange(16)
    cf[:, 2 * P + 25] = -0.5
    cb = np.zeros((P, 5 * P), np.float32)
    cb[:, 0:P] = np.eye(P)
    cb[:, P:2 * P] = np.where(k > q, HIDE, 0)
    cb[:, 2 * P:3 * P] = np.where(q > k, HIDE, 0)
    cb[:, 3 * P:4 * P] = np.where(k > q, HIDE, 0)
    ends = np.arange(NC) * BLK + BLK - 1
    cb[:, 4 * P:4 * P + NC] = np.where(ends[None, :] > q, HIDE, 0)
    inv = (1.0 / 10000.0 ** (np.arange(HALF, dtype=np.float32) * 2.0 / ROPE)).astype(np.float32)
    ang = np.arange(P, dtype=np.float32)[:, None] * inv[None, :]
    cos, sin = np.cos(ang), np.sin(ang)
    cos2 = np.concatenate([cos, cos], 1).astype(np.float32)
    sin2 = np.concatenate([-sin, sin], 1).astype(np.float32)
    return {"cf": cf, "cb": cb.astype(bf16), "ones": np.ones((2, HPG * KEYS), bf16), "cos2": cos2, "sin2": sin2,
            "cose": cos2[ends], "sine": sin2[ends]}


def kernel(**inputs):
    import concourse.bacc as bacc
    from concourse.bass_utils import run_bass_kernel_spmd as run

    a = {n: np.asarray(v) for n, v in inputs.items()}
    T = np.transpose
    arrays = {
        "x": a["x"], "ctx": a["ctx_2048"], "ctxT": T(a["ctx_2048"], (0, 2, 1)),
        "ctxK": T(a["ctx_2048"].reshape(NB, 2, HALF_K, NHG, HPG, HD0), (0, 3, 1, 5, 4, 2)).reshape(NB, P, HPG, HALF_K),
        "mask": a["mask_BxS2_bk0"].reshape(1, -1).view(np.float32),
        "a_log": a["L0_attn_A_log"], "d": a["L0_attn_D"], "wx": T(a["L0_attn_W_xproj"]),
        "w_lora": np.concatenate([T(a["L0_ffn_W"]), T(a["L0_ffn_A"].reshape(NE0 * RANK, D))], 1),
        "w_up": T(a["L0_ffn_B"], (0, 2, 1)).reshape(NE0 * RANK, D),
        "rw1": T(a["L0_ffn_rw1"]), "rb1": a["L0_ffn_rb1"], "rw2": T(a["L0_ffn_rw2"])[:, 0:NE0],
        "rb2": a["L0_ffn_rb2"][0:NE0], "gates": a["L0_ffn_gates"], "bias0": a["L0_ffn_bias"],
        "w_qkv": np.stack([a["L1_attn_Wq"], a["L1_attn_Wlk"], a["L1_attn_Wlv"]]),
        "b48": np.concatenate([a["L1_attn_bq"], a["L1_attn_blk"], a["L1_attn_blv"]]).reshape(48, HD),
        "wc": T(a["L1_attn_Wc"].reshape(KD, P)), "bc": a["L1_attn_bc"],
        "wkv": np.concatenate([a["L1_attn_Wk"], a["L1_attn_Wv"]], 1),
        "b_kv": np.concatenate([a["L1_attn_bk"], a["L1_attn_bv"]]),
        "qn_w": a["L1_attn_qn_w"], "kn_w": a["L1_attn_kn_w"], "sink_kT": T(a["L1_attn_sink_k"]),
        "sink_v": a["L1_attn_sink_v"], "wo": a["L1_attn_Wo"], "bo": a["L1_attn_bo"],
        "w1": a["L1_ffn_W1"], "w2": a["L1_ffn_W2"], "w3": a["L1_ffn_W3"], "wg": a["L1_ffn_Wg"], "bg": a["L1_ffn_bg"],
        "b1": T(a["L1_ffn_b1"].reshape(NE, MF, P), (2, 0, 1)), "b2": T(a["L1_ffn_b2"].reshape(NE, MF, P), (2, 0, 1)),
        "b3": a["L1_ffn_b3"],
    }
    arrays.update(constants())
    arrays = {f"in_{n}": np.ascontiguousarray(v) for n, v in arrays.items()}
    nc = bacc.Bacc("TRN2", target_bir_lowering=False, num_devices=1)
    io = {n[3:]: nc.dram_tensor(n, v.shape, mybir.dt.from_np(v.dtype), kind="ExternalInput").ap()
          for n, v in arrays.items()}
    out = nc.dram_tensor("out", (NB, P, D), F32, kind="ExternalOutput").ap()
    perceiver_program(nc, io, out)
    return run(nc, [arrays], core_ids=[0]).results[0]["out"]
```

```python
import math
from contextlib import ExitStack

import numpy as np

import concourse.bass as bass
from concourse import mybir

F32 = mybir.dt.float32
BF16 = mybir.dt.bfloat16
U32 = mybir.dt.uint32
U8 = mybir.dt.uint8
ALU = mybir.AluOpType
ACT = mybir.ActivationFunctionType
X_AXIS = mybir.AxisListType.X

P = 128
NB = 2
D = 256
KD = D // P
KEYS = 2048
NCH = KEYS // P

H0, HD0 = 16, 16
HPG = 4
NHG = H0 // HPG
NG = NB * NHG
HALF_K = KEYS // 2
REP = 12
PARTS = 6
QROWS = PARTS * HD0
SROWS = QROWS + 2
VW = 32
MASKED0 = -10000.0
HIDE = -1.0e30

NS = 16
MAX_AT = [0, 0, 1, 2, 3, 4, 4, 5, 6, 7, 8, 8, 9, 10, 11, 12]
SPREAD_AT = [(5, c) for c in range(8, 15)] + [(6, c) for c in (0, 1, *range(4, 11))]
NE0, RANK, HID0 = 16, 16, 64
NH, HD, BLK, NC = 16, 128, 16, 8
SW = P + NC + 1
ROPE = 64
HALF = ROPE // 2
BLOCKS = [(0, 0), (0, 1), (0, 2), (1, 0), (1, 1), (1, 2)]
NE, FF = 8, 512
MF = FF // P

EXP_WORDS = KD * FF + MF * FF + MF * D


def view(region, start, words, dtype=F32):
    part = region[:, start:start + words]
    return part if dtype == F32 else part.bitcast(dtype)


def perceiver_program(nc, io, out):
    ctx = ExitStack()
    sems = {}
    with ctx:
        def sb(name, shape, dt=F32):
            return ctx.enter_context(nc.sbuf_tensor(name, shape, dt))

        def S(name):
            if name not in sems:
                sems[name] = ctx.enter_context(nc.semaphore(name))
            return sems[name]

        reg_a = sb("reg_a", [P, 16384])
        reg_b = sb("reg_b", [P, 26112])
        ctxT = reg_a[:, 0:8192].rearrange("p (b h k) -> p b h k", b=NB, h=KD)
        ctxN = reg_a[:, 8192:16384].rearrange("p (b c d) -> p b c d", b=NB, c=NCH)
        kS = [view(reg_b, 4096 * i, 4096, BF16).rearrange("p (j k) -> p j k", j=HPG) for i in range(3)]
        ctxK = reg_a[:, 0:8192].rearrange("p (b j k) -> p b j k", b=NB, j=HPG)
        part_at = [((reg_b, 12288), (reg_b, 14336), (reg_b, 16384)), ((reg_a, 0), (reg_a, 2048), (reg_b, 18432))]
        ks3 = [[view(r, a, 2048, BF16).rearrange("p (j k) -> p j k", j=HPG) for r, a in ats] for ats in part_at]
        va = [reg_b[:, 20480 + 2048 * i:20480 + 2048 * (i + 1)].rearrange("p (c j w) -> p c j w", c=NCH, j=HPG)
              for i in range(2)]
        pT = [reg_b[:, 24576 + 512 * i:24576 + 512 * (i + 1)] for i in range(3)]
        bc_row = [reg_b[:, a:a + 4096].rearrange("p (n l) -> p n l", n=2 * NS) for a in (12288, 0)]
        decay = [r[:, a:a + 4096].rearrange("p (h n l) -> p h n l", h=KD, n=NS) for r, a in ((reg_a, 0), (reg_b, 4096))]
        state = [reg_a[:, 4096:8192].rearrange("p (h n l) -> p h n l", h=KD, n=NS),
                 reg_b[:, 8192:12288].rearrange("p (h n l) -> p h n l", h=KD, n=NS)]
        w_qkv = reg_b[:, 0:12288].rearrange("p (j k n) -> p j k n", j=3, k=KD)
        w_o = reg_b[:, 12288:16384].rearrange("p (h n) -> p h n", h=NH)
        p3 = [reg_b[:, 16384 + 2048 * b:16384 + 2048 * (b + 1)] for b in range(NB)]
        p3T = [reg_b[:, 20480 + 2048 * b:20480 + 2048 * (b + 1)].rearrange("p (c q) -> p c q", c=NCH)
               for b in range(NB)]
        roped = reg_b[:, 16384:18432].rearrange("p (h d) -> p h d", h=NH)
        cvs = reg_b[:, 18432:20480].rearrange("p (h d) -> p h d", h=NH)
        bias3 = view(reg_b, 20480, 1024, BF16)
        squares = reg_b[:, 14336:16384].rearrange("p (h d) -> p h d", h=NH)
        act = [reg_a[:, 8192 * b:8192 * (b + 1)] for b in range(NB)]
        qf = [a[:, 0:2048].rearrange("p (h d) -> p h d", h=NH) for a in act]
        kf = [a[:, 2048:2048 + NH * SW].rearrange("p (h d) -> p h d", h=NH) for a in act]
        lv = [a[:, 4240:6288].rearrange("p (h d) -> p h d", h=NH) for a in act]
        pr = [a[:, 6288:6288 + HPG * SW].rearrange("p (j d) -> p j d", j=HPG) for a in act]
        prT = [a[:, 6836:7348].rearrange("p (j d) -> p j d", j=HPG) for a in act]
        pcT = [a[:, 7348:7860].rearrange("p (j d) -> p j d", j=HPG) for a in act]
        expert_at = [(reg_b, 0), (reg_b, 4096), (reg_b, 8192), (reg_b, 12288), (reg_b, 16384), (reg_b, 20480),
                     (reg_a, 0), (reg_a, 4096)]
        w1 = [r[:, a:a + KD * FF].rearrange("p (k n) -> p k n", k=KD) for r, a in expert_at]
        w2 = [r[:, a + 1024:a + 3072].rearrange("p (k n) -> p k n", k=MF) for r, a in expert_at]
        w3 = [r[:, a + 3072:a + 4096].rearrange("p (k n) -> p k n", k=MF) for r, a in expert_at]
        h1 = reg_a[:, 8192:9216].rearrange("p (m t) -> p m t", m=MF)
        h2 = reg_a[:, 9216:10240].rearrange("p (m t) -> p m t", m=MF)
        h1b = reg_a[:, 10240:11264].rearrange("p (m t) -> p m t", m=MF)
        h2b = reg_a[:, 11264:12288].rearrange("p (m t) -> p m t", m=MF)

        cf = sb("cf", [P, 2 * P + 1 + NC + NC * 0 + 16 + 1])
        ident = cf[:, 0:P]
        later = cf[:, P:2 * P]
        floor0 = cf[:, 2 * P:2 * P + 1]
        in_block = cf[:, 2 * P + 1:2 * P + 9]
        iota = cf[:, 2 * P + 9:2 * P + 25]
        neg_half = cf[:, 2 * P + 25:2 * P + 26]
        cb = sb("cb", [P, 5 * P + 2 * NS], BF16)
        identb = cb[:, 0:P]
        hide_q = cb[:, P:2 * P]
        hide_k = cb[:, 2 * P:3 * P]
        hide_s = cb[:, 3 * P:3 * P + SW]
        pick = cb[0:3 * 2 * NS, 5 * P:5 * P + 2 * NS]
        onesb = sb("onesb", [P, P], BF16)
        bc_res = sb("bc_res", [3 * 2 * NS, P])
        bc_split = sb("bc_split", [3 * 2 * NS, P], BF16)

        x = [sb(f"x{b}", [P, D]) for b in range(NB)]
        xn = [sb(f"xn{b}", [P, D]) for b in range(NB)]
        xT2 = sb("xT", [P, KD, NB * P])
        xT = [xT2[:, :, b * P:(b + 1) * P] for b in range(NB)]
        stats = [sb(f"stats{b}", [P, 6]) for b in range(NB)]
        mean_var = [sb(f"mv{b}", [P, 2]) for b in range(NB)]
        var_eps = [sb(f"ve{b}", [P, 1]) for b in range(NB)]
        rstd = [sb(f"rstd{b}", [P, 1]) for b in range(NB)]
        tmp = [sb(f"tmp{b}", [P, D]) for b in range(NB)]
        tmp2 = [sb(f"tmpb{b}", [P, D]) for b in range(NB)]
        oreg = sb("oreg", [P, 2048])
        q_split = [view(oreg, 1024 * b, 768, BF16).rearrange("p (h t d) -> p h t d", h=H0, t=PARTS)
                   for b in range(NB)]
        o_all = [oreg[:, 1024 * b:1024 * (b + 1)].rearrange("p (g u j w) -> p g u j w", g=NHG, u=2, j=HPG)
                 for b in range(NB)]
        qreg = sb("qreg", [P, 2048])
        qT = [view(qreg, 1024 * b, 1024, BF16).rearrange("p (h q) -> p h q", h=H0) for b in range(NB)]
        mx = sb("mx", [P, HPG, 2])
        m4 = sb("m4", [P, HPG])
        negm = sb("negm", [P, HPG])
        nm = [sb(f"nm{b}", [P, H0, 2], BF16) for b in range(NB)]
        e_arg = [sb(f"e_arg{b}", [P, H0]) for b in range(NB)]
        e_val = [sb(f"e_val{b}", [P, H0]) for b in range(NB)]
        rec = [sb(f"rec{b}", [P, H0]) for b in range(NB)]
        o_sb = sb("o_sb", [P, P])
        wx = sb("wx", [P, KD, D + 3 * 2 * NS])
        a_log = sb("a_log", [P, KD, NS])
        ea = sb("ea", [P, KD, NS])
        d_row = oreg[:, 0:256]
        dt = [tmp2[b] for b in range(NB)]
        w_lora = sb("w_lora", [P, KD, 2 * D])
        w_up = oreg[:, 256:768].rearrange("p (k n) -> p k n", k=KD)
        rw1 = oreg[:, 768:896].rearrange("p (k n) -> p k n", k=KD)
        rb1 = sb("rb1", [HID0, 1])
        rw2 = sb("rw2", [HID0, NE0])
        rb2 = sb("rb2", [P, NE0])
        gates = sb("gates", [P, NE0])
        bias0 = reg_b[:, 12288:12544]
        top8 = [sb(f"top8_{b}", [P, 8]) for b in range(NB)]
        idx8 = [sb(f"idx8_{b}", [P, 8], U32) for b in range(NB)]
        idxf = [sb(f"idxf_{b}", [P, 8]) for b in range(NB)]
        logit = [sb(f"logit{b}", [P, NE0]) for b in range(NB)]
        coef = [sb(f"coef{b}", [P, NE0]) for b in range(NB)]
        coef2 = [sb(f"coefb{b}", [P, NE0]) for b in range(NB)]
        small = [sb(f"small{b}", [P, 8]) for b in range(NB)]
        xmask = view(reg_b, 18432, 2048, BF16)
        mask8 = reg_b[0:1, 12544:12544 + NB * KEYS // 4]
        mask_row = xmask[0:1, :]
        m3 = [sb(f"m3_{b}", [P, 4]) for b in range(NB)]
        tab = qreg
        cos2 = tab[:, 0:64]
        sin2 = tab[:, 64:128]
        wq_n = tab[:, 128:256]
        wk_n = tab[:, 256:384]
        ct = {"q": tab[:, 384:448], "k": tab[:, 448:512], "e": tab[:, 512:576]}
        st = {"q": tab[:, 576:640], "k": tab[:, 640:704], "e": tab[:, 704:768]}
        cose = tab[:, 768:832]
        sine = tab[:, 832:896]
        w_n = {"q": wq_n, "k": wk_n, "e": wk_n}
        bias48 = tab[:, 896:1024]
        split48 = view(tab, 1024, 192, BF16).rearrange("p (t d) -> p t d", t=3)
        res48 = tab[:, 1216:1344]
        b_out = tab[:, 1344:1600]
        sinkT = tab[:, 1600:1616]
        w_c = tab[:, 1616:1618]
        b_c = tab[0:1, 1618:1619]
        rms = [tab[:, 1620 + 64 * b:1684 + 64 * b] for b in range(NB)]
        wkv = reg_b[:, 24576:25088].rearrange("p (k n) -> p k n", k=KD)
        b_kv = reg_b[0:NC, 25088:25344]
        comp = [sb(f"comp{b}", [P, 160]) for b in range(NB)]
        ckv = [reg_b[0:NC, 23552 + 512 * b:23808 + 512 * b] for b in range(NB)]
        ckr = [reg_b[0:NC, 23808 + 512 * b:23936 + 512 * b] for b in range(NB)]
        cks = [reg_b[0:NC, 23936 + 512 * b:24064 + 512 * b] for b in range(NB)]
        att = [sb(f"att{b}", [P, 32]) for b in range(NB)]
        wg = sb("wg", [P, KD, NE])
        bg = sb("bg", [P, NE])
        b1 = sb("b1", [P, NE, MF])
        b2 = sb("b2", [P, NE, MF])
        b3 = reg_b[0:NE, 25344:25600]
        comb = [sb(f"comb{b}", [P, NE]) for b in range(NB)]
        combT = reg_b[0:NE, 25600:25856]

        ps = ctx.enter_context(nc.psum_tensor("ps", [P, 8, 512], F32))
        score_a = [ps[:, 0:2, :], ps[:, 2:4, :]]
        score_b = [ps[:, 4, :], ps[:, 5, :]]

        def bank(b, i, cols=512):
            return ps[:, 4 * b + i, 0:cols]

        side = ps[:, 6, 256:512]

        def bankb(i):
            return ps[:, i, :].bitcast(BF16)

        block = ctx.enter_context(nc.Block())

        @block.sync
        def _(sp):
            def load(dst, src, name):
                sp.dma_start(dst, src).then_inc(S(name), 16)

            load(x[0][:, :], io["x"][0], "x_in")
            load(ctxK[:, 0, 0:2, :], io["ctxK"][0][:, 0:2, :], "ctxK_in0")
            load(x[1][:, :], io["x"][1], "x_in")
            load(cf[:, :], io["cf"], "const_in")
            load(cb[:, :], io["cb"], "const_in")
            load(ctxK[:, 0, 2:4, :], io["ctxK"][0][:, 2:4, :], "ctxK_in1")
            for i in range(3):
                load(kS[i][QROWS:SROWS, :, :], io["ones"].rearrange("r (j k) -> r j k", j=HPG), "ones_in")
            load(ctxN[:, 0, :, :], io["ctx"][0].rearrange("(c p) d -> p c d", p=P), "ctxN_in0")
            for g in range(NG):
                b, hg = divmod(g, NHG)
                if g >= 3:
                    sp.wait_ge(S("pv_done"), NCH * (g - 2))
                for part, at in enumerate(((0, 3, 5), (1, 4), (2,))):
                    sp.wait_ge(S(f"k{part + 1}_done"), 2 * (b + 1))
                    for t in at:
                        for half in range(2):
                            row = 32 * hg + HD0 * half
                            sp.dma_start(kS[g % 3][HD0 * t:HD0 * (t + 1), :, HALF_K * half:HALF_K * (half + 1)],
                                         ks3[b][part][row:row + HD0, :, :]).then_inc(S(f"kS_in{g % 3}"), 16)
                if g == 0:
                    for n in range(2):
                        load(ctxK[:, 1, 2 * n:2 * n + 2, :], io["ctxK"][1][:, 2 * n:2 * n + 2, :], f"ctxK_in{n + 2}")
                if g == 2:
                    load(ctxN[:, 1, :, :], io["ctx"][1].rearrange("(c p) d -> p c d", p=P), "ctxN_in1")
                    load(wx[:, :, :], io["wx"].rearrange("(k p) n -> p k n", p=P), "ssm_in")
                    load(a_log[:, :, :], io["a_log"].rearrange("(k p) n -> p k n", p=P), "ssm_in")
                if g == 3:
                    load(w_lora[:, :, :], io["w_lora"].rearrange("(k p) n -> p k n", p=P), "lora_in")
                    load(rb1[:, :], io["rb1"].unsqueeze(1), "lora_in")
                    load(rw2[:, :], io["rw2"], "lora_in")
                    load(rb2[:, :], io["rb2"].partition_broadcast(P), "lora_in")
                    load(gates[:, :], io["gates"].partition_broadcast(P), "lora_in")
                    load(wg[:, :, :], io["wg"].rearrange("(k p) n -> p k n", p=P), "ffn_in")
                    load(bg[:, :], io["bg"].partition_broadcast(P), "ffn_in")
                    load(b1[:, :, :], io["b1"], "ffn_in")
                    load(b2[:, :, :], io["b2"], "ffn_in")

            sp.wait_ge(S("x_done0"), 1)
            load(d_row, io["d"].partition_broadcast(P), "lora_in")
            load(w_up, io["w_up"].rearrange("(k p) n -> p k n", p=P), "lora_in")
            load(rw1, io["rw1"].rearrange("(k p) n -> p k n", p=P), "lora_in")
            sp.wait_ge(S("hc_done"), KD)
            load(ctxT[:, 0, :, :], io["ctxT"][0].rearrange("(h p) k -> p h k", p=P), "ctxT_in0")
            load(mask8, io["mask"], "mask_in")
            load(bias0, io["bias0"].partition_broadcast(P), "mask_in")
            sp.wait_ge(S("y_ps"), 1)
            load(ctxT[:, 1, :, :], io["ctxT"][1].rearrange("(h p) k -> p h k", p=P), "ctxT_in1")
            sp.wait_ge(S("x_done1"), 1)
            load(wkv, io["wkv"].rearrange("(k p) n -> p k n", p=P), "tab_in")
            load(b_kv, io["b_kv"].partition_broadcast(NC), "tab_in")
            load(b3, io["b3"], "tab_in")
            load(cos2, io["cos2"], "tab_in")
            load(sin2, io["sin2"], "tab_in")
            load(cose[0:NC, :], io["cose"], "tab_in")
            load(sine[0:NC, :], io["sine"], "tab_in")
            load(wq_n, io["qn_w"].partition_broadcast(P), "tab_in")
            load(wk_n, io["kn_w"].partition_broadcast(P), "tab_in")
            load(bias48[0:48, :], io["b48"], "tab_in")
            load(b_out, io["bo"].partition_broadcast(P), "tab_in")
            load(sinkT, io["sink_kT"], "tab_in")
            load(w_c, io["wc"], "tab_in")
            load(b_c, io["bc"].unsqueeze(0), "tab_in")
            sp.wait_ge(S("hc_done"), KD * NB)
            for j in range(3):
                if j == 2:
                    sp.wait_ge(S("y_ps"), 2)
                load(w_qkv[:, j, :, :], io["w_qkv"][j].rearrange("(k p) n -> p k n", p=P), f"wqkv_in{j}")
            sp.wait_ge(S("x_done0"), 4)
            sp.wait_ge(S("b48_split"), 1)
            for j in range(3):
                for t in range(3):
                    sp.dma_start(bias3[32 * j + t:32 * j + t + 1, :].rearrange("o (a d) -> o a d", d=HD),
                                 split48[16 * j:16 * j + 16, t, :]).then_inc(S("bias3_in"), 16)
            sp.wait_ge(S("x_done1"), 4)
            for b in range(NB):
                load(cvs[32 * b + NC:32 * b + NC + 1, :, :], io["sink_v"].unsqueeze(0), "sinkv_in")
            for e in range(NE):
                if e == 0:
                    sp.wait_ge(S("proj_ps"), 4 * len(BLOCKS))
                if e == 3:
                    sp.wait_ge(S("k_roped"), NB)
                    load(w_o[:, :, :], io["wo"].rearrange("(h p) n -> p h n", p=P), "wo_in")
                    for b in range(NB):
                        sp.wait_ge(S(f"x_done{b}"), 5)
                load(w1[e], io["w1"][e].rearrange("(k p) n -> p k n", p=P), f"expert_in{e}")
                load(w2[e], io["w2"][e].rearrange("(k p) n -> p k n", p=P), f"expert_in{e}")
                load(w3[e], io["w3"][e].rearrange("(k p) n -> p k n", p=P), f"expert_in{e}")
            for b in range(NB):
                sp.wait_ge(S(f"x_done{b}"), 6)
                sp.dma_start(out[b], x[b][:, :]).then_inc(S("out_sent"), 16)
            sp.wait_ge(S("out_sent"), 16 * NB)

        @block.gpsimd
        def _(pool):
            def inv_sqrt(t, b):
                pool.wait_ge(S(f"ln_var{b}"), t + 1)
                pool.tensor_tensor(rstd[b][:, :], var_eps[b][:, :], neg_half, ALU.pow).then_inc(S(f"ln_rstd{b}"), 1)

            pool.memset(onesb[:, :], 1.0).then_inc(S("ones_set"), 1)
            pool.wait_ge(S("const_in"), 32)
            inv_sqrt(0, 0)
            inv_sqrt(0, 1)
            for i in range(2):
                pool.memset(va[i][:, :, :, :], 0.0).then_inc(S("va_zero"), 1)
            for i in range(2):
                pool.wait_ge(S("va_zero"), 2)
                pool.memset(va[i][:, :, :, HD0:HD0 + 1], 1.0).then_inc(S("va_one"), 1)
            def state_input(b, h):
                pool.wait_ge(S("dtx_done"), b + 1)
                pool.wait_ge(S("bc_sb"), (8, 20)[b])
                pool.tensor_tensor(state[b][:, h], tmp[b][:, h * P:(h + 1) * P].unsqueeze(1).to_broadcast([P, NS, P]),
                                   bc_row[b][:, 0:NS, :], ALU.mult).then_inc(S("dbx_done"), 1)

            def decay_exponent(h):
                pool.wait_ge(S("ea_done"), 1)
                pool.wait_ge(S("kS_in1"), 16 * REP * 3)
                pool.wait_ge(S("dtx_done"), 1)
                pool.tensor_tensor(decay[0][:, h], dt[0][:, P * h:P * (h + 1)].unsqueeze(1).to_broadcast([P, NS, P]),
                                   ea[:, h, :].unsqueeze(2).to_broadcast([P, NS, P]), ALU.mult)\
                    .then_inc(S("dta_done"), 1)

            for g in range(NG):
                b, hg = divmod(g, NHG)
                if hg == 0:
                    pool.wait_ge(S(f"ctxN_in{b}"), 16)
                if g >= 2:
                    pool.wait_ge(S("oT_ready"), g - 1)
                src = ctxN[:, b, :, hg * HPG * HD0:(hg + 1) * HPG * HD0].rearrange("p c (j d) -> p c j d", j=HPG)
                pool.tensor_copy(va[g % 2][:, :, :, 0:HD0], src).then_inc(S("va_ready"), 1)
                if g == 5:
                    inv_sqrt(1, 0)
                if g == 6:
                    decay_exponent(0)
                    decay_exponent(1)
                    state_input(0, 0)
            state_input(0, 1)
            inv_sqrt(2, 0)
            inv_sqrt(1, 1)
            state_input(1, 0)
            inv_sqrt(3, 0)
            state_input(1, 1)
            inv_sqrt(2, 1)
            inv_sqrt(4, 0)
            inv_sqrt(3, 1)

            def rotated_inv_rms(b, j):
                pool.wait_ge(S("ms_done"), 2 * b + j + 1)
                pool.tensor_tensor(rms[b][:, 16 + 32 * j:32 + 32 * j], rms[b][:, 32 * j:16 + 32 * j],
                                   neg_half.to_broadcast([P, NH]), ALU.pow).then_inc(S("qkrstd_done"), 1)

            rotated_inv_rms(0, 0)
            rotated_inv_rms(0, 1)
            inv_sqrt(4, 1)
            for b in range(NB):
                pool.wait_ge(S("cms_done"), b + 1)
                pool.tensor_tensor(comp[b][0:NC, 40:41], comp[b][0:NC, 39:40], neg_half[0:NC, :], ALU.pow)\
                    .then_inc(S("crstd_done"), 1)
            rotated_inv_rms(1, 0)
            rotated_inv_rms(1, 1)
            inv_sqrt(5, 0)
            inv_sqrt(5, 1)

        @block.scalar
        def _(sc):
            steps = [0]

            def link(ins):
                steps[0] += 1
                ins.then_inc(S("act_step"), 1)
                sc.wait_ge(S("act_step"), steps[0])

            def transposed_x(t, b):
                sc.wait_ge(S(f"xT_ps{b}"), t)
                src = side if (t, b) == (1, 0) else bank(b, 0, D)
                sc.copy(xT[b], src.rearrange("p (k q) -> p k q", k=KD)).then_inc(S(f"xT_sb{b}"), 1)

            def key_part1(n):
                b, pair = divmod(n, 2)
                if b == 1:
                    sc.wait_ge(S("k3_done"), 2)
                sc.wait_ge(S(f"ctxK_in{n}"), 16)
                sc.copy(ks3[b][0][:, 2 * pair:2 * pair + 2, :], ctxK[:, b, 2 * pair:2 * pair + 2, :])\
                    .then_inc(S("k1_done"), 1)

            def key_part2(n):
                b, pair = divmod(n, 2)
                sc.wait_ge(S("kres_done"), n + 1)
                sc.copy(ks3[b][1][:, 2 * pair:2 * pair + 2, :], ctxK[:, b, 2 * pair:2 * pair + 2, :])\
                    .then_inc(S("k2_done"), 1)

            key_part1(0)
            key_part1(1)
            key_part2(0)
            key_part2(1)
            for b in range(NB):
                sc.wait_ge(S("qT_ps"), b + 1)
                for i in range(2):
                    sc.copy(qT[b][0:QROWS, 8 * i:8 * i + 8, :],
                            bankb(2 * b + i)[0:QROWS, :].rearrange("p (h q) -> p h q", h=8))\
                        .then_inc(S("qT_sb"), 1)

            def max_rows(g):
                b, hg = divmod(g, NHG)
                sc.wait_ge(S("nmT_ready"), g + 1)
                sc.copy(qT[b][QROWS:SROWS, HPG * hg:HPG * (hg + 1), :],
                        bankb(6)[0:2, 0:HPG * P].rearrange("p (j q) -> p j q", j=HPG)).then_inc(S("nm_rows"), 1)

            key_part1(2)
            key_part1(3)
            def weigh_masked(b):
                sc.wait_ge(S("e_arg"), b + 1)
                sc.activation(e_val[b][:, :], e_arg[b][:, :], ACT.Exp).then_inc(S("e_val"), 1)

            def copy_z(b):
                sc.wait_ge(S("z_ready"), b + 1)
                sc.copy(dt[b][:, :], (side, bank(1, 1, D))[b]).then_inc(S("z_sb"), 1)

            def softplus_exp(b):
                sc.wait_ge(S("z_abs"), b + 1)
                sc.activation(tmp[b][:, :], tmp[b][:, :], ACT.Exp, scale=-1.0).then_inc(S("z_exp"), 1)

            def softplus_log(b):
                sc.wait_ge(S("z_exp"), b + 1)
                sc.activation(tmp[b][:, :], tmp[b][:, :], ACT.Ln, bias=1.0).then_inc(S("log_done"), 1)

            def bc_copy(b, i):
                sc.wait_ge(S("bc_ps"), 16 * b + i + 1)
                rows = (2, 4)[b]
                src = side if b == 0 else bank(1, 2 + i % 2)
                sc.copy(bc_row[b][:, rows * i:rows * (i + 1), :], src.rearrange("p (n l) -> p n l", n=rows))\
                    .then_inc(S("bc_sb"), 1)

            def decay_exp(b, h):
                sc.wait_ge(S("dta_done"), KD * b + h + 1)
                sc.activation(decay[b][:, h], decay[b][:, h], ACT.Exp, scale=-1.0).then_inc(S("decay_done"), 1)

            def hidden_exp(b):
                sc.wait_ge(S("hid_lin"), b + 1)
                sc.activation(tmp2[b][0:HID0, 0:P], tmp[b][0:HID0, 0:P], ACT.Exp, scale=-1.0)\
                    .then_inc(S("hid_exp"), 1)

            def gap_exp(b):
                sc.wait_ge(S("gap_done"), b + 1)
                sc.activation(small[b][:, 1:2], small[b][:, 0:1], ACT.Exp).then_inc(S("gap_exp"), 1)

            def wxaT(b):
                sc.wait_ge(S("wxaT_ps"), b + 1)
                sc.copy(tmp2[b][:, :], bank(b, 0, D)).then_inc(S("wxaT_sb"), 1)

            def exp3(b):
                sc.wait_ge(S("m3_done"), b + 1)
                sc.activation(p3[b].rearrange("p (i k) -> p i k", i=4), ps[:, 4 * b:4 * b + 4, :], ACT.Exp,
                              bias=m3[b][:, 1:2], scale=1.0 / 16.0, accum_out=m3[b][:, 2:3])\
                    .then_inc(S("p3_done"), 1)

            def p3_columns(b, i):
                sc.wait_ge(S("p3T_ps"), 4 * b + i + 1)
                sc.copy(p3T[b][:, 4 * i:4 * i + 4, :],
                        bank(b, i).rearrange("p (c q) -> p c q", c=4)).then_inc(S("p3T_sb"), 1)

            def state_rates():
                sc.wait_ge(S("ssm_in"), 32)
                sc.activation(ea[:, :, :], a_log[:, :, :], ACT.Exp).then_inc(S("ea_done"), 1)

            beside = {(3, 9): [(state_rates,)], (4, 1): [(weigh_masked, 0)], (4, 10): [(transposed_x, 1, 0)],
                      (4, 12): [(copy_z, 0)], (5, 0): [(softplus_exp, 0)], (5, 1): [(softplus_log, 0)], (6, 2): [(decay_exp, 0, 0)],
                      (6, 6): [(decay_exp, 0, 1)],
                      (7, 11): [(transposed_x, 2, 0)], (7, 13): [(hidden_exp, 0)]}
            for i, (g, c) in enumerate(SPREAD_AT):
                beside.setdefault((g, c + 1), []).append((bc_copy, 0, i))
            max_rows(0)
            for g in range(NG):
                for c in range(NCH):
                    n = NCH * g + c
                    if (g, c) in beside:
                        for step in beside[g, c]:
                            step[0](*step[1:])
                    if g >= 1 and c == 3:
                        sc.wait_ge(S("oT_ready"), g)
                        pb, pg = divmod(g - 1, NHG)
                        sc.copy(o_all[pb][:, pg], ps[:, 6, 0:2 * P].rearrange("p (u j w) -> p u j w", u=2, j=HPG))\
                            .then_inc(S("o_all"), 1)
                    sc.wait_ge(S("score_b"), n + 1)
                    if n >= 3:
                        sc.wait_ge(S("pv_done"), n - 2)
                    sc.activation(pT[n % 3], score_b[n % 2], ACT.Exp).then_inc(S("exp_done"), 1)
                if g + 1 < NG:
                    max_rows(g + 1)
                sc.wait_ge(S("pv_done"), NCH * (g + 1))
                sc.copy(o_sb[:, :], ps[:, 7, 0:P]).then_inc(S("o_sb"), 1)
            sc.wait_ge(S("oT_ready"), NG)
            sc.copy(o_all[1][:, NHG - 1], ps[:, 6, 0:2 * P].rearrange("p (u j w) -> p u j w", u=2, j=HPG))\
                .then_inc(S("o_all"), 1)
            def projected(k, n):
                b, j = BLOCKS[k]
                sc.wait_ge(S("proj_ps"), 4 * k + n + 1)
                sc.copy((qf, kf, lv)[j][b][:, 4 * n:4 * n + 4, 0:HD],
                        bank(b, n % 2).rearrange("p (h d) -> p h d", h=4)).then_inc(S("proj_sb"), 1)

            def square(k):
                b, j = BLOCKS[k]
                sc.wait_ge(S("proj_sb"), 4 * k + 4)
                if j == 1:
                    sc.wait_ge(S("q_roped"), b + 1)
                elif b > 0:
                    sc.wait_ge(S("k_roped"), b)
                sc.activation(squares, (qf, kf)[j][b][:, :, 0:HD], ACT.Square).then_inc(S("sq_done"), 1)

            def rotated_columns(b, j):
                for i in range(4):
                    sc.wait_ge(S("qkT_ps"), 8 * b + 4 * j + i + 1)
                    sc.copy((qf, kf)[j][b][:, 4 * i:4 * i + 4, 0:HD],
                            bank(b, 2 + i % 2).rearrange("p (h d) -> p h d", h=4)).then_inc(S("qkT_sb"), 1)

            def key_tail(b):
                sc.wait_ge(S("ckT_ps"), b + 1)
                sc.copy(comp[b][:, 16:16 + NC], bank(b, 3, NC)).then_inc(S("ckT_sb"), 1)
                sc.wait_ge(S("ckT_sb"), b + 1)
                sc.copy(kf[b][:, :, HD:HD + NC], comp[b][:, 16:16 + NC].unsqueeze(1).to_broadcast([P, NH, NC]))\
                    .then_inc(S("kT_tail"), 1)
                sc.copy(kf[b][:, :, HD + NC:SW], sinkT.unsqueeze(2)).then_inc(S("kT_tail"), 1)

            weigh_masked(1)
            transposed_x(1, 1)
            copy_z(1)
            gap_exp(0)
            softplus_exp(1)
            softplus_log(1)
            wxaT(0)
            for i in range(8):
                bc_copy(1, i)
            transposed_x(3, 0)
            decay_exp(1, 0)
            decay_exp(1, 1)
            exp3(0)
            for i in range(4):
                p3_columns(0, i)
            transposed_x(2, 1)
            hidden_exp(1)
            transposed_x(4, 0)
            projected(0, 0)
            gap_exp(1)
            projected(0, 1)
            wxaT(1)
            projected(0, 2)
            projected(0, 3)
            square(0)
            transposed_x(3, 1)
            projected(1, 0)
            projected(1, 1)
            exp3(1)
            projected(1, 2)
            projected(1, 3)
            square(1)
            rotated_columns(0, 0)
            for i in range(4):
                p3_columns(1, i)
            for n in range(4):
                projected(2, n)
            transposed_x(4, 1)
            for b in range(NB):
                sc.wait_ge(S("c_shift"), b + 1)
                sc.activation(ckr[b][0:1, :], ckr[b][0:1, :], ACT.Exp).then_inc(S("c_exp"), 1)
            for n in range(4):
                projected(3, n)
            for b in range(NB):
                sc.wait_ge(S("entT_ps"), b + 1)
                sc.copy(comp[b][:, 0:2 * NC], bank(b, 2, 2 * NC)).then_inc(S("entT_sb"), 1)
            square(3)
            rotated_columns(0, 1)
            for n in range(4):
                projected(4, n)
            square(4)
            key_tail(0)
            key_tail(1)
            rotated_columns(1, 0)
            for n in range(4):
                projected(5, n)
            rotated_columns(1, 1)

            def weights(n):
                g, b = divmod(n, NB)
                sc.wait_ge(S("nb_done"), n + 1)
                for j in range(HPG):
                    s = ps[:, 4 * b + j // 2, 256 * (j % 2):256 * (j % 2) + SW]
                    scale = rms[b][:, 16 + HPG * g + j:17 + HPG * g + j]
                    sc.activation(pr[b][:, j, 0:P], s[:, 0:P], ACT.Exp, bias=att[b][:, 8 + j:9 + j],
                                  scale=scale, accum_out=att[b][:, 16 + j:17 + j]).then_inc(S("pr_exp"), 1)
                    sc.activation(pr[b][:, j, P:SW], s[:, P:SW], ACT.Exp, bias=att[b][:, 12 + j:13 + j],
                                  scale=scale, accum_out=att[b][:, 20 + j:21 + j]).then_inc(S("pr_exp"), 1)

            def weight_columns(n):
                b = n % NB
                sc.wait_ge(S("prT_ps"), n + 1)
                sc.copy(prT[b], bank(b, 2).rearrange("p (j q) -> p j q", j=HPG)).then_inc(S("prT_sb"), 1)
                sc.copy(pcT[b][32 * b:32 * b + NC + 1, :, :],
                        bank(b, 3)[0:NC + 1, :].rearrange("p (j q) -> p j q", j=HPG)).then_inc(S("prT_sb"), 1)

            weights(0)
            for n in range(NB * NHG):
                if n + 1 < NB * NHG:
                    weights(n + 1)
                weight_columns(n)

            transposed_x(5, 0)
            transposed_x(5, 1)
            for b in range(NB):
                sc.wait_ge(S("g_shift"), b + 1)
                sc.activation(comb[b][:, :], logit[b][:, 0:NE], ACT.Exp, accum_out=small[b][:, 2:3])\
                    .then_inc(S("g_exp"), 1)
            for e in range(NE):
                for m in range(MF):
                    sc.wait_ge(S("h1_ps"), MF * e + m + 1)
                    sc.activation((h1, h1b)[e % 2][:, m, :], ps[:, 2 + m % 2, 0:NB * P], ACT.Gelu,
                                  bias=b1[:, e, m:m + 1]).then_inc(S("h1_sb"), 1)
                if e == 0:
                    sc.wait_ge(S("combT_ps"), 1)
                    sc.copy(combT, ps[0:NE, 0, 0:NB * P]).then_inc(S("combT_sb"), 1)
                for m in range(MF):
                    sc.wait_ge(S("h2_ps"), MF * e + m + 1)
                    sc.activation((h2, h2b)[e % 2][:, m, :], ps[:, 4 + m % 2, 0:NB * P], ACT.Gelu,
                                  bias=b2[:, e, m:m + 1]).then_inc(S("h2_sb"), 1)

        @block.tensor
        def _(pe):
            def x_to_columns(t, b):
                pe.wait_ge(S(f"xn_done{b}"), t + 1)
                dst = side if (t, b) == (1, 0) else bank(b, 0, D)
                for k in range(KD):
                    mm = pe.transpose(dst[:, k * P:(k + 1) * P], xn[b][:, k * P:(k + 1) * P], ident)
                mm.then_inc(S(f"xT_ps{b}"), 1)

            pe.wait_ge(S("const_in"), 32)
            for b in range(NB):
                pe.wait_ge(S("q_split"), b + 1)
                for h in range(H0):
                    mm = pe.transpose(bankb(2 * b + h // 8)[0:QROWS, P * (h % 8):P * (h % 8 + 1)],
                                      q_split[b][:, h].rearrange("p t d -> p (t d)"), identb)
                mm.then_inc(S("qT_ps"), 1)

            def scores_for_max(g, part):
                b, hg = divmod(g, NHG)
                j, quarter = divmod(part, 4)
                m = 8 * g + part // 2
                i = part % 2
                if part == 0:
                    pe.wait_ge(S(f"kS_in{g % 3}"), 16 * REP * (g // 3 + 1))
                    pe.wait_ge(S("qT_sb"), 4)
                if m >= 2 and i == 0:
                    pe.wait_ge(S("max_done"), m - 1)
                q = qT[b][0:QROWS, HPG * hg + j, :]
                k = kS[g % 3][0:QROWS, j, 512 * quarter:512 * (quarter + 1)]
                if quarter < 3:
                    mm = pe.matmul(score_a[m % 2][:, i, :], q, k, start=True, stop=True)
                else:
                    pe.matmul(score_a[m % 2][:, i, 0:384], q, k[:, 0:384], start=True, stop=True)
                    pe.matmul(score_a[m % 2][:, i, 384:512], q, k[:, 384:512], start=True, stop=False)
                    mm = pe.matmul(score_a[m % 2][:, i, 384:512], identb, hide_q, start=False, stop=True)
                if i == 1:
                    mm.then_inc(S("score_a"), 1)

            def max_to_rows(g):
                b, hg = divmod(g, NHG)
                pe.wait_ge(S("nm_done"), g + 1)
                if g >= 2:
                    pe.wait_ge(S("o_all"), g - 1)
                for j in range(HPG):
                    mm = pe.transpose(bankb(6)[0:2, P * j:P * (j + 1)], nm[b][:, HPG * hg + j, :], identb)
                mm.then_inc(S("nmT_ready"), 1)

            def scores_shifted(g, c):
                b, hg = divmod(g, NHG)
                n = NCH * g + c
                if c == 0:
                    pe.wait_ge(S("nm_rows"), g + 1)
                    pe.wait_ge(S("ones_in"), 48)
                if n >= 2:
                    pe.wait_ge(S("exp_done"), n - 1)
                last = c == NCH - 1
                for j in range(HPG):
                    cols = score_b[n % 2][:, P * j:P * (j + 1)]
                    if last:
                        pe.matmul(cols, identb, hide_k, start=True, stop=False)
                    mm = pe.matmul(cols, kS[g % 3][0:SROWS, j, P * c:P * (c + 1)], qT[b][0:SROWS, HPG * hg + j, :],
                                   start=not last, stop=True)
                mm.then_inc(S("score_b"), 1)

            def values(g, c):
                n = NCH * g + c
                if c == 0:
                    pe.wait_ge(S("va_ready"), g + 1)
                    pe.wait_ge(S("va_one"), 2)
                    if g >= 1:
                        pe.wait_ge(S("o_sb"), g)
                pe.wait_ge(S("exp_done"), n + 1)
                for j in range(HPG):
                    mm = pe.matmul(ps[VW * j:VW * (j + 1), 7, 0:P], va[g % 2][:, c, j, :], pT[n % 3][:, P * j:P * (j + 1)],
                                   start=c == 0, stop=c == NCH - 1)
                mm.then_inc(S("pv_done"), 1)

            def outputs_to_rows(g):
                pe.wait_ge(S("o_sb"), g + 1)
                if g + 1 < NG:
                    pe.wait_ge(S("nm_rows"), g + 2)
                pe.transpose(ps[:, 6, 0:P], o_sb[:, :], ident)
                pe.matmul(ps[:, 6, P:2 * P], later, va[g % 2][:, NCH - 1].rearrange("p j w -> p (j w)"),
                          start=True, stop=True).then_inc(S("oT_ready"), 1)

            def step_sizes(b):
                pe.wait_ge(S("ssm_in"), 32)
                pe.wait_ge(S(f"xT_sb{b}"), 1)
                z = (side, bank(1, 1, D))[b]
                for h in range(KD):
                    for k in range(KD):
                        mm = pe.matmul(z[:, P * h:P * (h + 1)], wx[:, k, P * h:P * (h + 1)], xT[b][:, k, :],
                                       start=k == 0, stop=k == KD - 1)
                mm.then_inc(S("z_ready"), 1)

            def state_maps(b):
                pe.wait_ge(S("z_sb"), b + 1)
                bc = (side[0:96, 0:P], ps[0:96, 5, 256:256 + P])[b]
                for k in range(KD):
                    mm = pe.matmul(bc, wx[:, k, D:D + 3 * 2 * NS], xT[b][:, k, :],
                                   start=k == 0, stop=k == KD - 1)
                mm.then_inc(S("bc_rows"), 1)

            def spread(b, i):
                pe.wait_ge(S("bc_split"), b + 1)
                if b == 0 and i >= 1:
                    pe.wait_ge(S("bc_sb"), i)
                if b == 1 and i >= 2:
                    pe.wait_ge(S("bc_sb"), 16 + i - 1)
                rows = (2, 4)[b]
                dst = side if b == 0 else bank(1, 2 + i % 2)
                for r in range(rows):
                    n = rows * i + r
                    mm = pe.matmul(dst[:, P * r:P * (r + 1)], pick[:, n:n + 1].to_broadcast([96, P]), bc_split[:, :],
                                   start=True, stop=True)
                mm.then_inc(S("bc_ps"), 1)

            def sum_states(b, h):
                pe.wait_ge(S("hc_done"), KD * b + h + 1)
                for n in range(NS):
                    mm = pe.matmul(bank(b, 0)[:, P * h:P * (h + 1)], state[b][:, h, n, :], ident, start=n == 0, stop=n == NS - 1)
                if h == KD - 1:
                    mm.then_inc(S("y_ps"), 1)

            def lora_products(b):
                pe.wait_ge(S("lora_in"), 128)
                pe.wait_ge(S(f"xT_sb{b}"), 2)
                for k in range(KD):
                    mm = pe.matmul(bank(b, 1)[0:HID0, 0:P], rw1[:, k, :], xT[b][:, k, :], start=k == 0, stop=k == KD - 1)
                mm.then_inc(S("hid_ps"), 1)
                for k in range(KD):
                    mm = pe.matmul(bank(b, 2, D), xT[b][:, k, :], w_lora[:, k, D:2 * D], start=k == 0, stop=k == KD - 1)
                mm.then_inc(S("xa_ps"), 1)

            def lora_logits(b):
                pe.wait_ge(S("hid_sb"), b + 1)
                pe.matmul(bank(b, 3)[:, 0:NE0], tmp[b][0:HID0, P:2 * P], rw2[:, :], start=True, stop=True)\
                    .then_inc(S("logit_ps"), 1)
                for k in range(KD):
                    pe.matmul(bank(b, 1, D), xT[b][:, k, :], w_lora[:, k, 0:D], start=k == 0, stop=False)

            def lora_columns(b):
                pe.wait_ge(S("wxa_done"), b + 1)
                for k in range(KD):
                    mm = pe.transpose(bank(b, 0)[:, k * P:(k + 1) * P], tmp[b][:, k * P:(k + 1) * P], ident)
                mm.then_inc(S("wxaT_ps"), 1)

            def lora_up(b):
                pe.wait_ge(S("wxaT_sb"), b + 1)
                for k in range(KD):
                    mm = pe.matmul(bank(b, 1, D), tmp2[b][:, k * P:(k + 1) * P], w_up[:, k, :], start=False,
                                   stop=k == KD - 1)
                mm.then_inc(S("lora_ps"), 1)

            def scores3(b, part):
                if part == 0:
                    pe.wait_ge(S("ones_set"), 1)
                    pe.wait_ge(S("mask_row"), 2)
                    pe.wait_ge(S(f"xT_sb{b}"), 3)
                    pe.wait_ge(S(f"x_done{b}"), 3)
                    pe.wait_ge(S(f"ctxT_in{b}"), 16)
                for i in range(2 * part, 2 * part + 2):
                    for k in range(KD):
                        pe.matmul(bank(b, i), xT[b][:, k, :], ctxT[:, b, k, 512 * i:512 * (i + 1)],
                                  start=k == 0, stop=False)
                    mm = pe.matmul(bank(b, i), onesb[0:1, :], mask_row[0:1, KEYS * b + 512 * i:KEYS * b + 512 * (i + 1)],
                                   start=False, stop=True)
                if part == 1:
                    mm.then_inc(S("s3_ps"), 1)

            def p3_to_columns(b):
                pe.wait_ge(S("p3_done"), b + 1)
                for i in range(4):
                    for c in range(4):
                        mm = pe.transpose(bank(b, i)[:, P * c:P * (c + 1)],
                                          p3[b][:, P * (4 * i + c):P * (4 * i + c + 1)], ident)
                    mm.then_inc(S("p3T_ps"), 1)

            def outputs3(b):
                for c in range(NCH):
                    if c % 4 == 0:
                        pe.wait_ge(S("p3T_sb"), 4 * b + c // 4 + 1)
                    mm = pe.matmul(bank(b, 0, D), p3T[b][:, c, :], ctxN[:, b, c, :], start=c == 0, stop=c == NCH - 1)
                mm.then_inc(S("o3_ps"), 1)

            def misc_read(name, count):
                pe.wait_ge(S(name), count)

            beside = {(4, 9): [(misc_read, "o_all", 4), (x_to_columns, 1, 0)], (4, 11): [(step_sizes, 0)],
                      (5, 4): [(misc_read, "o_all", 5), (state_maps, 0)], (6, 4): [(misc_read, "o_all", 6)],
                      (7, 0): [(sum_states, 0, 0)], (7, 4): [(sum_states, 0, 1)], (7, 9): [(x_to_columns, 2, 0)],
                      (7, 11): [(lora_products, 0)], (7, 15): [(lora_logits, 0)]}
            for i, at in enumerate(SPREAD_AT):
                beside.setdefault(at, []).append((spread, 0, i))
            read_before_rows = {5: ("z_sb", 1), 6: ("bc_sb", 7), 7: ("bc_sb", 16)}
            read_before_outputs = {5: ("bc_sb", 9)}
            for part in range(16):
                scores_for_max(0, part)
            max_to_rows(0)
            for g in range(NG):
                for c in range(NCH):
                    scores_shifted(g, c)
                    if c == NCH - 1 and g + 1 < NG:
                        if g + 1 in read_before_rows:
                            misc_read(*read_before_rows[g + 1])
                        max_to_rows(g + 1)
                    if c > 0:
                        values(g, c - 1)
                    if c == 2 and g >= 1:
                        if g - 1 in read_before_outputs:
                            misc_read(*read_before_outputs[g - 1])
                        outputs_to_rows(g - 1)
                    if g + 1 < NG:
                        for part in range(16):
                            if MAX_AT[part] == c:
                                scores_for_max(g + 1, part)
                    if (g, c) in beside:
                        for step in beside[g, c]:
                            step[0](*step[1:])
                values(g, NCH - 1)
            outputs_to_rows(NG - 1)

            def projection(k, quarters=range(4)):
                b, j = BLOCKS[k]
                pe.wait_ge(S(f"xT_sb{b}"), 4)
                pe.wait_ge(S(f"wqkv_in{j}"), 16)
                pe.wait_ge(S("bias3_in"), 144)
                for n in quarters:
                    if n >= 2 or k % 3 > 0:
                        pe.wait_ge(S("proj_sb"), 4 * k + n - 1)
                    pe.matmul(bank(b, n % 2), onesb[32 * j:32 * j + 3, :], bias3[32 * j:32 * j + 3, 512 * n:512 * (n + 1)],
                              start=True, stop=False)
                    for i in range(KD):
                        mm = pe.matmul(bank(b, n % 2), xT[b][:, i, :], w_qkv[:, j, i, 512 * n:512 * (n + 1)],
                                       start=False, stop=i == KD - 1)
                    mm.then_inc(S("proj_ps"), 1)

            def rotated_to_columns(b, j):
                pe.wait_ge(S(("q_roped", "k_roped")[j]), b + 1)
                for i in range(4):
                    if i >= 2 or j == 1:
                        pe.wait_ge(S("qkT_sb"), 8 * b + 4 * j + i - 1)
                    for c in range(4):
                        mm = pe.transpose(bank(b, 2 + i % 2)[:, P * c:P * (c + 1)], roped[:, 4 * i + c, :], ident)
                    mm.then_inc(S("qkT_ps"), 1)

            x_to_columns(1, 1)
            step_sizes(1)
            state_maps(1)
            lora_columns(0)
            lora_up(0)
            for i in range(8):
                spread(1, i)
            x_to_columns(3, 0)
            scores3(0, 0)
            scores3(0, 1)
            sum_states(1, 0)
            p3_to_columns(0)
            sum_states(1, 1)
            outputs3(0)
            x_to_columns(2, 1)
            lora_products(1)
            x_to_columns(4, 0)
            lora_logits(1)
            projection(0, range(0, 2))
            lora_columns(1)
            lora_up(1)
            projection(0, range(2, 4))
            x_to_columns(3, 1)
            scores3(1, 0)
            scores3(1, 1)
            projection(1)
            rotated_to_columns(0, 0)
            p3_to_columns(1)
            outputs3(1)
            projection(2)
            x_to_columns(4, 1)
            pe.wait_ge(S("tab_in"), 224)
            for b in range(NB):
                if b == 0:
                    pe.wait_ge(S("qkT_sb"), 4)
                pe.wait_ge(S(f"xT_sb{b}"), 4)
                for k in range(KD):
                    mm = pe.matmul(bank(b, 2)[0:1, 0:P], w_c[:, k:k + 1], xT[b][:, k, :], start=k == 0, stop=k == KD - 1)
                mm.then_inc(S("c_ps"), 1)
            projection(3)
            for b in range(NB):
                pe.wait_ge(S("c_soft"), b + 1)
                pe.matmul(bank(b, 3)[:, 0:1], ckr[b][0:1, :], ident[0:1, 0:1], start=True, stop=True)\
                    .then_inc(S("ccol_ps"), 1)
            for b in range(NB):
                pe.wait_ge(S("in_blk"), b + 1)
                for k in range(KD):
                    mm = pe.matmul(bank(b, 2)[:, NC * k:NC * (k + 1)], xn[b][:, P * k:P * (k + 1)],
                                   comp[b][:, 24:24 + NC], start=True, stop=True)
                mm.then_inc(S("entT_ps"), 1)
            for b in range(NB):
                pe.wait_ge(S("entT_sb"), b + 1)
                for k in range(KD):
                    mm = pe.matmul(bank(b, 3)[0:NC, 0:2 * HD], comp[b][:, NC * k:NC * (k + 1)], wkv[:, k, :],
                                   start=k == 0, stop=k == KD - 1)
                mm.then_inc(S("ckv_ps"), 1)
            pe.wait_ge(S("cms_done"), 1)
            rotated_to_columns(0, 1)
            projection(4)
            for b in range(NB):
                pe.wait_ge(S("ck_roped"), b + 1)
                if b == 0:
                    pe.wait_ge(S("qkT_sb"), 8)
                pe.transpose(bank(b, 3)[:, 0:NC], ckr[b][:, :], ident[0:NC, 0:NC]).then_inc(S("ckT_ps"), 1)
            pe.wait_ge(S("ckT_sb"), 2)
            rotated_to_columns(1, 0)
            projection(5)
            rotated_to_columns(1, 1)
            for b in range(NB):
                pe.wait_ge(S("kT_tail"), 2 * (b + 1))
                pe.wait_ge(S("qkT_sb"), 8 * (b + 1))
            pe.wait_ge(S("proj_sb"), 24)
            pe.wait_ge(S("cvs_done"), 2)
            pe.wait_ge(S("sinkv_in"), 32)
            def scores4(n):
                g, b = divmod(n, NB)
                if g >= 1:
                    pe.wait_ge(S("pr_exp"), 8 * (n - NB + 1))
                for j in range(HPG):
                    h = HPG * g + j
                    s = ps[:, 4 * b + j // 2, 256 * (j % 2):256 * (j % 2) + SW]
                    pe.matmul(s, qf[b][:, h, :], kf[b][:, h, :], start=True, stop=False)
                    mm = pe.matmul(s, identb, hide_s, start=False, stop=True)
                mm.then_inc(S("s4_ps"), 1)

            def weights_to_columns(n):
                g, b = divmod(n, NB)
                pe.wait_ge(S("pr_norm"), 2 * (n + 1))
                if g >= 1:
                    pe.wait_ge(S("mT_sb"), n - NB + 1)
                for j in range(HPG):
                    pe.transpose(bank(b, 2)[:, P * j:P * (j + 1)], pr[b][:, j, 0:P], ident)
                for j in range(HPG):
                    mm = pe.transpose(bank(b, 3)[0:NC + 1, P * j:P * (j + 1)], pr[b][:, j, P:SW], ident)
                mm.then_inc(S("prT_ps"), 1)

            def mix_values(n):
                g, b = divmod(n, NB)
                pe.wait_ge(S("prT_sb"), 2 * (n + 1))
                for j in range(HPG):
                    h = HPG * g + j
                    pe.matmul(bank(b, 3)[:, P * j:P * (j + 1)], lv[b][:, h, :], prT[b][:, j, :], start=True, stop=False)
                    mm = pe.matmul(bank(b, 3)[:, P * j:P * (j + 1)], cvs[32 * b:32 * b + NC + 1, h, :],
                                   pcT[b][32 * b:32 * b + NC + 1, j, :], start=False, stop=True)
                mm.then_inc(S("mT_ps"), 1)

            scores4(0)
            scores4(1)
            for n in range(NB * NHG):
                if n + 2 < NB * NHG:
                    scores4(n + 2)
                weights_to_columns(n)
                if n >= 1:
                    mix_values(n - 1)
            mix_values(NB * NHG - 1)
            pe.wait_ge(S("wo_in"), 16)
            for b in range(NB):
                pe.wait_ge(S("mT_sb"), NB * NHG)
                pe.wait_ge(S("pr_exp"), 8 * NB * NHG)
                for h in range(NH):
                    mm = pe.matmul(bank(b, 0, D), qf[b][:, h, :], w_o[:, h, :], start=h == 0, stop=h == NH - 1)
                mm.then_inc(S("o4_ps"), 1)

            for b in range(NB):
                pe.wait_ge(S(f"x_done{b}"), 5)
                x_to_columns(5, b)
            pe.wait_ge(S("ffn_in"), 64)
            for b in range(NB):
                pe.wait_ge(S(f"xT_sb{b}"), 5)
                for k in range(KD):
                    mm = pe.matmul(bank(b, 1)[:, 0:NE], xT[b][:, k, :], wg[:, k, :], start=k == 0, stop=k == KD - 1)
                mm.then_inc(S("g_ps"), 1)

            def hidden1(e):
                pe.wait_ge(S(f"expert_in{e}"), 48)
                for m in range(MF):
                    n = MF * e + m
                    if n >= 2:
                        pe.wait_ge(S("h1_sb"), n - 1)
                    for k in range(KD):
                        mm = pe.matmul(ps[:, 2 + m % 2, 0:NB * P], w1[e][:, k, P * m:P * (m + 1)], xT2[:, k, :],
                                       start=k == 0, stop=k == KD - 1)
                    mm.then_inc(S("h1_ps"), 1)

            def hidden2(e):
                pe.wait_ge(S("h1_sb"), MF * (e + 1))
                for m in range(MF):
                    n = MF * e + m
                    if n >= 2:
                        pe.wait_ge(S("h2_sb"), n - 1)
                    for k in range(MF):
                        mm = pe.matmul(ps[:, 4 + m % 2, 0:NB * P], w2[e][:, k, P * m:P * (m + 1)],
                                       (h1, h1b)[e % 2][:, k, :], start=k == 0, stop=k == MF - 1)
                    mm.then_inc(S("h2_ps"), 1)

            def expert_out(e):
                pe.wait_ge(S("h2_sb"), MF * (e + 1))
                for b in range(NB):
                    if e >= 1:
                        pe.wait_ge(S("eo_added"), NB * (e - 1) + b + 1)
                    for k in range(MF):
                        mm = pe.matmul(ps[:, 6 + b, 0:D], (h2, h2b)[e % 2][:, k, P * b:P * (b + 1)], w3[e][:, k, :],
                                       start=k == 0, stop=k == MF - 1)
                    mm.then_inc(S("eo_ps"), 1)

            pe.wait_ge(S("g_read"), NB)
            for e in range(NE):
                hidden1(e)
                if e == 0:
                    for b in range(NB):
                        pe.wait_ge(S("comb_done"), b + 1)
                        mm = pe.transpose(ps[0:NE, 0, P * b:P * (b + 1)], comb[b][:, :], ident)
                    mm.then_inc(S("combT_ps"), 1)
                    pe.wait_ge(S("combT_sb"), 1)
                    pe.wait_ge(S("tab_in"), 224)
                    for b in range(NB):
                        mm = pe.matmul(ps[:, b, 0:D], combT[:, P * b:P * (b + 1)], b3, start=True, stop=True)
                        mm.then_inc(S("b3_ps"), 1)
                else:
                    expert_out(e - 1)
                hidden2(e)
            expert_out(NE - 1)

        @block.vector
        def _(ve):
            steps = [0]

            def link(ins):
                steps[0] += 1
                ins.then_inc(S("dve_step"), 1)
                ve.wait_ge(S("dve_step"), steps[0])

            def ln_stats(t, b):
                if t > 0:
                    ve.wait_ge(S(f"x_done{b}"), t)
                link(ve.bn_stats(stats[b][:, :], x[b][:, :]))
                link(ve.bn_aggr(mean_var[b][:, :], stats[b][:, :]))
                ve.tensor_scalar(var_eps[b][:, :], mean_var[b][:, 1:2], 1e-5, None, ALU.add)\
                    .then_inc(S(f"ln_var{b}"), 1)

            def ln_apply(t, b):
                ve.wait_ge(S(f"ln_rstd{b}"), t + 1)
                ve.tensor_scalar(xn[b][:, :], x[b][:, :], mean_var[b][:, 0:1], rstd[b][:, :],
                                 ALU.subtract, ALU.mult).then_inc(S(f"xn_done{b}"), 1)

            def layer_norm(t):
                for b in range(NB):
                    ln_stats(t, b)
                for b in range(NB):
                    ln_apply(t, b)

            ve.wait_ge(S("x_in"), 32)
            layer_norm(0)

            def key_residue(n):
                b, pair = divmod(n, 2)
                ve.wait_ge(S("k1_done"), n + 1)
                keys = ctxK[:, b, 2 * pair:2 * pair + 2, :]
                ve.tensor_tensor(keys, keys, ks3[b][0][:, 2 * pair:2 * pair + 2, :], ALU.subtract)\
                    .then_inc(S("kres_done"), 1)

            def key_part3(n):
                b, pair = divmod(n, 2)
                ve.wait_ge(S("k2_done"), n + 1)
                ve.wait_ge(S("kres_done"), n + 1)
                ve.tensor_tensor(ks3[b][2][:, 2 * pair:2 * pair + 2, :], ctxK[:, b, 2 * pair:2 * pair + 2, :],
                                 ks3[b][1][:, 2 * pair:2 * pair + 2, :], ALU.subtract).then_inc(S("k3_done"), 1)

            def key_part2(n):
                b, pair = divmod(n, 2)
                ve.wait_ge(S("kres_done"), n + 1)
                ve.tensor_copy(ks3[b][1][:, 2 * pair:2 * pair + 2, :], ctxK[:, b, 2 * pair:2 * pair + 2, :])\
                    .then_inc(S("k2_done"), 1)

            def split_queries(b):
                ve.wait_ge(S(f"xn_done{b}"), 1)
                q = tmp[b][:, :].rearrange("p (h d) -> p h d", h=H0)
                r = tmp2[b][:, :].rearrange("p (h d) -> p h d", h=H0)
                link(ve.tensor_scalar(tmp[b][:, :], xn[b][:, :], 1.0 / math.sqrt(HD0), None, ALU.mult))
                link(ve.tensor_copy(q_split[b][:, :, 0:3, :], q.unsqueeze(2).to_broadcast([P, H0, 3, HD0])))
                link(ve.tensor_tensor(r, q, q_split[b][:, :, 0, :], ALU.subtract))
                link(ve.tensor_copy(q_split[b][:, :, 3:5, :], r.unsqueeze(2).to_broadcast([P, H0, 2, HD0])))
                ve.tensor_tensor(q_split[b][:, :, 5, :], r, q_split[b][:, :, 3, :], ALU.subtract)\
                    .then_inc(S("q_split"), 1)

            def masked_weight(b):
                link(ve.tensor_tensor(e_arg[b][:, :], nm[b][:, :, 0], nm[b][:, :, 1], ALU.add))
                ve.tensor_scalar(e_arg[b][:, :], e_arg[b][:, :], MASKED0, 80.0, ALU.add, ALU.min)\
                    .then_inc(S("e_arg"), 1)

            def normalise(b):
                ve.wait_ge(S("o_all"), NHG * (b + 1))
                ve.wait_ge(S("e_val"), b + 1)
                o, u = o_all[b][:, :, 0], o_all[b][:, :, 1]
                weight = e_val[b][:, :].rearrange("p (g j) -> p g j", g=NHG).unsqueeze(3).to_broadcast([P, NHG, HPG, VW])
                link(ve.tensor_tensor(u, u, weight, ALU.mult))
                link(ve.tensor_tensor(o, o, u, ALU.add))
                r3 = rec[b][:, :].rearrange("p (g j) -> p g j", g=NHG)
                link(ve.reciprocal(r3, o[:, :, :, HD0]))
                link(ve.tensor_tensor(tmp[b][:, :].rearrange("p (g j d) -> p g j d", g=NHG, j=HPG), o[:, :, :, 0:HD0],
                                      r3.unsqueeze(3).to_broadcast([P, NHG, HPG, HD0]), ALU.mult))
                ve.tensor_tensor(x[b][:, :], x[b][:, :], tmp[b][:, :], ALU.add).then_inc(S(f"x_done{b}"), 1)

            def step_magnitude(b):
                ve.wait_ge(S("z_sb"), b + 1)
                ve.scalar_tensor_tensor(tmp[b][:, :], dt[b][:, :], -1.0, dt[b][:, :], ALU.mult, ALU.max)\
                    .then_inc(S("z_abs"), 1)

            def step_and_input(b):
                ve.wait_ge(S("log_done"), b + 1)
                link(ve.scalar_tensor_tensor(dt[b][:, :], dt[b][:, :], 0.0, tmp[b][:, :], ALU.max, ALU.add))
                ve.wait_ge(S(f"xT_sb{b}"), 1)
                ve.tensor_tensor(tmp[b][:, :].rearrange("p (k l) -> p k l", k=KD),
                                 dt[b][:, :].rearrange("p (k l) -> p k l", k=KD), xT[b], ALU.mult)\
                    .then_inc(S("dtx_done"), 1)

            def split_maps(b):
                ve.wait_ge(S("bc_rows"), b + 1)
                if b == 1:
                    ve.wait_ge(S("bc_ps"), 16)
                bc = (side[0:96, 0:P], ps[0:96, 5, 256:256 + P])[b]
                link(ve.tensor_copy(bc_split[:, :], bc))
                for row, src in ((32, bc), (64, bc), (64, bc_res)):
                    rows = slice(row, row + 32)
                    link(ve.tensor_tensor(bc_res[rows, :], src[rows, :], bc_split[rows, :], ALU.subtract))
                    last = ve.tensor_copy(bc_split[rows, :], bc_res[rows, :])
                    if src is not bc_res:
                        link(last)
                last.then_inc(S("bc_split"), 1)

            def decay_exponent(b, h):
                ve.wait_ge(S("ea_done"), 1)
                ve.wait_ge(S("dtx_done"), b + 1)
                ve.tensor_tensor(decay[b][:, h], dt[b][:, P * h:P * (h + 1)].unsqueeze(1).to_broadcast([P, NS, P]),
                                 ea[:, h, :].unsqueeze(2).to_broadcast([P, NS, P]), ALU.mult)\
                    .then_inc(S("dta_done"), 1)

            def scan(b, h):
                ve.wait_ge(S("decay_done"), KD * b + h + 1)
                link(ve.memset(decay[b][:, h, :, 0:1], 0.0))
                ve.wait_ge(S("dbx_done"), KD * b + h + 1)
                ve.tensor_tensor_scan(state[b][:, h].rearrange("p n l -> p (n l)"),
                                      decay[b][:, h].rearrange("p n l -> p (n l)"),
                                      state[b][:, h].rearrange("p n l -> p (n l)"), 0.0, ALU.mult, ALU.add)\
                    .then_inc(S("scan_done"), 1)

            def read_states(b, h):
                ve.wait_ge(S("scan_done"), KD * b + h + 1)
                ve.wait_ge(S("bc_sb"), (16, 24)[b])
                ve.tensor_tensor(state[b][:, h], state[b][:, h], bc_row[b][:, NS:2 * NS, :], ALU.mult)\
                    .then_inc(S("hc_done"), 1)

            def add_states(b):
                ve.wait_ge(S("lora_in"), 128)
                ve.wait_ge(S("dta_done"), KD * (b + 1))
                link(ve.tensor_tensor(tmp2[b][:, :], xn[b][:, :], d_row, ALU.mult))
                link(ve.tensor_tensor(x[b][:, :], x[b][:, :], tmp2[b][:, :], ALU.add))
                ve.wait_ge(S("y_ps"), b + 1)
                ve.tensor_tensor(x[b][:, :], bank(b, 0, D), x[b][:, :], ALU.add)\
                    .then_inc(S(f"x_done{b}"), 1)

            def lora_hidden(b):
                ve.wait_ge(S("lora_in"), 128)
                ve.wait_ge(S("hid_ps"), b + 1)
                ve.tensor_scalar(tmp[b][0:HID0, 0:P], bank(b, 1)[0:HID0, 0:P], rb1[:, :], None, ALU.add)\
                    .then_inc(S("hid_lin"), 1)
                ve.wait_ge(S("hid_exp"), b + 1)
                link(ve.tensor_scalar(tmp2[b][0:HID0, 0:P], tmp2[b][0:HID0, 0:P], 1.0, None, ALU.add))
                link(ve.reciprocal(tmp2[b][0:HID0, 0:P], tmp2[b][0:HID0, 0:P]))
                ve.wait_ge(S("hid_lin"), b + 1)
                ve.tensor_tensor(tmp[b][0:HID0, P:2 * P], tmp[b][0:HID0, 0:P], tmp2[b][0:HID0, 0:P], ALU.mult)\
                    .then_inc(S("hid_sb"), 1)

            def lora_top(b):
                ve.wait_ge(S("logit_ps"), b + 1)
                link(ve.tensor_tensor(logit[b][:, :], bank(b, 3, NE0), rb2[:, :], ALU.add))
                link(ve.tensor_tensor(logit[b][:, :], logit[b][:, :], gates[:, :], ALU.add))
                link(ve.max(top8[b][:, :], logit[b][:, :]))
                ve.tensor_tensor(small[b][:, 0:1], top8[b][:, 1:2], top8[b][:, 0:1], ALU.subtract)\
                    .then_inc(S("gap_done"), 1)
                link(ve.max_index(idx8[b][:, :], top8[b][:, :], logit[b][:, :]))
                link(ve.tensor_copy(idxf[b][:, :], idx8[b][:, :]))
                ve.wait_ge(S("gap_exp"), b + 1)
                link(ve.tensor_scalar(small[b][:, 2:3], small[b][:, 1:2], 1.0, None, ALU.add))
                link(ve.reciprocal(small[b][:, 3:4], small[b][:, 2:3]))
                link(ve.tensor_tensor(small[b][:, 4:5], small[b][:, 1:2], small[b][:, 3:4], ALU.mult))
                link(ve.tensor_scalar(coef[b][:, :], iota, idxf[b][:, 0:1], small[b][:, 3:4], ALU.is_equal, ALU.mult))
                link(ve.tensor_scalar(coef2[b][:, :], iota, idxf[b][:, 1:2], small[b][:, 4:5], ALU.is_equal, ALU.mult))
                link(ve.tensor_tensor(coef[b][:, :], coef[b][:, :], coef2[b][:, :], ALU.add))
                ve.wait_ge(S("xa_ps"), b + 1)
                ve.tensor_tensor(tmp[b][:, :].rearrange("p (e r) -> p e r", e=NE0),
                                 bank(b, 2, D).rearrange("p (e r) -> p e r", e=NE0),
                                 coef[b][:, :].unsqueeze(2).to_broadcast([P, NE0, RANK]), ALU.mult)\
                    .then_inc(S("wxa_done"), 1)

            def lora_add(b):
                ve.wait_ge(S("mask_in"), 32)
                link(ve.tensor_tensor(x[b][:, :], x[b][:, :], bias0, ALU.add))
                ve.wait_ge(S("lora_ps"), b + 1)
                ve.tensor_tensor(x[b][:, :], bank(b, 1, D), x[b][:, :], ALU.add).then_inc(S(f"x_done{b}"), 1)

            def key_mask():
                ve.wait_ge(S("mask_in"), 32)
                ve.tensor_scalar(mask_row[0:1, :], mask8.bitcast(U8), 16.0e30, -16.0e30, ALU.mult, ALU.add)\
                    .then_inc(S("mask_row"), 2)

            def max3(b):
                ve.wait_ge(S("s3_ps"), b + 1)
                link(ve.reduce_max(m3[b][:, 0:1], ps[:, 4 * b:4 * b + 4, :].rearrange("p i k -> p (i k)"), X_AXIS))
                ve.tensor_scalar(m3[b][:, 1:2], m3[b][:, 0:1], -1.0 / 16.0, None, ALU.mult).then_inc(S("m3_done"), 1)

            def add3(b):
                ve.wait_ge(S("p3_done"), b + 1)
                link(ve.reciprocal(m3[b][:, 3:4], m3[b][:, 2:3]))
                link(ve.tensor_scalar(m3[b][:, 3:4], m3[b][:, 0:1], -8.0e30, m3[b][:, 3:4], ALU.is_gt, ALU.mult))
                ve.wait_ge(S("o3_ps"), b + 1)
                ve.scalar_tensor_tensor(x[b][:, :], bank(b, 0, D), m3[b][:, 3:4], x[b][:, :], ALU.mult, ALU.add)\
                    .then_inc(S(f"x_done{b}"), 1)

            def tables():
                ve.wait_ge(S("tab_in"), 224)
                link(ve.tensor_copy(split48[0:48, 0, :], bias48[0:48, :]))
                link(ve.tensor_tensor(res48[0:48, :], bias48[0:48, :], split48[0:48, 0, :], ALU.subtract))
                link(ve.tensor_copy(split48[0:48, 1, :], res48[0:48, :]))
                ve.tensor_tensor(split48[0:48, 2, :], res48[0:48, :], split48[0:48, 1, :], ALU.subtract)\
                    .then_inc(S("b48_split"), 1)
                for name, c, s, rows in (("q", cos2, sin2, P), ("k", cos2, sin2, P), ("e", cose, sine, NC)):
                    w = w_n[name]
                    link(ve.tensor_tensor(ct[name][0:rows, :], c[0:rows, :], w[0:rows, 0:ROPE], ALU.mult))
                    link(ve.tensor_tensor(st[name][0:rows, 0:HALF], s[0:rows, 0:HALF], w[0:rows, HALF:ROPE], ALU.mult))
                    link(ve.tensor_tensor(st[name][0:rows, HALF:ROPE], s[0:rows, HALF:ROPE], w[0:rows, 0:HALF], ALU.mult))

            def block_scores(b):
                ve.wait_ge(S("c_ps"), b + 1)
                row = ckr[b][0:1, :]
                row3 = row.rearrange("p (c r) -> p c r", c=NC)
                mxb = comp[b][0:1, 120:128]
                link(ve.tensor_scalar(row, bank(b, 2)[0:1, 0:P], b_c, None, ALU.add))
                link(ve.reduce_max(mxb, row3, X_AXIS))
                ve.tensor_tensor(row3, row3, mxb.unsqueeze(2).to_broadcast([1, NC, BLK]), ALU.subtract)\
                    .then_inc(S("c_shift"), 1)

            def block_softmax(b):
                row3 = ckr[b][0:1, :].rearrange("p (c r) -> p c r", c=NC)
                mxb = comp[b][0:1, 120:128]
                ve.wait_ge(S("c_exp"), b + 1)
                link(ve.reduce_sum(mxb, row3, X_AXIS))
                link(ve.reciprocal(mxb, mxb))
                ve.tensor_tensor(row3, row3, mxb.unsqueeze(2).to_broadcast([1, NC, BLK]), ALU.mult)\
                    .then_inc(S("c_soft"), 1)

            def block_map(b):
                ve.wait_ge(S("ccol_ps"), b + 1)
                ve.tensor_scalar(comp[b][:, 24:24 + NC], in_block, bank(b, 3)[:, 0:1], None, ALU.mult)\
                    .then_inc(S("in_blk"), 1)

            def compressed(b):
                ve.wait_ge(S("ckv_ps"), b + 1)
                ck = ckv[b][:, 0:HD]
                link(ve.tensor_tensor(ckv[b][:, :], bank(b, 3)[0:NC, 0:2 * HD], b_kv, ALU.add))
                link(ve.tensor_tensor(cks[b][:, :], ck, ck, ALU.mult))
                link(ve.reduce_sum(comp[b][0:NC, 38:39], cks[b][:, :], X_AXIS))
                ve.tensor_scalar(comp[b][0:NC, 39:40], comp[b][0:NC, 38:39], 1.0 / HD, 1e-6, ALU.mult, ALU.add)\
                    .then_inc(S("cms_done"), 1)
                ve.wait_ge(S("crstd_done"), b + 1)
                link(ve.tensor_scalar(ck, ck, comp[b][0:NC, 40:41], None, ALU.mult))
                link(ve.tensor_tensor(ckr[b][:, 0:ROPE], ck[:, 0:ROPE], ct["e"][0:NC, :], ALU.mult))
                link(ve.tensor_tensor(cks[b][:, 0:HALF], ck[:, HALF:ROPE], st["e"][0:NC, 0:HALF], ALU.mult))
                link(ve.tensor_tensor(cks[b][:, HALF:ROPE], ck[:, 0:HALF], st["e"][0:NC, HALF:ROPE], ALU.mult))
                link(ve.tensor_tensor(ckr[b][:, ROPE:HD], ck[:, ROPE:HD], wk_n[0:NC, ROPE:HD], ALU.mult))
                ve.tensor_tensor(ckr[b][:, 0:ROPE], ckr[b][:, 0:ROPE], cks[b][:, 0:ROPE], ALU.add)\
                    .then_inc(S("ck_roped"), 1)
                ve.tensor_copy(cvs[32 * b:32 * b + NC, :, :],
                               ckv[b][:, HD:2 * HD].unsqueeze(1).to_broadcast([NC, NH, HD])).then_inc(S("cvs_done"), 1)

            def rope(b, j, src, name, done):
                rows = rms[b][:, 32 * j:32 * j + 16]
                ve.wait_ge(S("sq_done"), 2 * b + j + 1)
                link(ve.reduce_sum(rows, squares, X_AXIS))
                ve.tensor_scalar(rows, rows, 1.0 / HD, 1e-6, ALU.mult, ALU.add).then_inc(S("ms_done"), 1)
                if j == 0:
                    if b > 0:
                        ve.wait_ge(S("qkT_ps"), 8 * b)
                else:
                    ve.wait_ge(S("qkT_ps"), 8 * b + 4)
                rot = squares
                both = [P, NH, ROPE]
                half = [P, NH, HALF]
                link(ve.tensor_tensor(roped[:, :, 0:ROPE], src[:, :, 0:ROPE], ct[name].unsqueeze(1).to_broadcast(both),
                                      ALU.mult))
                link(ve.tensor_tensor(rot[:, :, 0:HALF], src[:, :, HALF:ROPE],
                                      st[name][:, 0:HALF].unsqueeze(1).to_broadcast(half), ALU.mult))
                link(ve.tensor_tensor(rot[:, :, HALF:ROPE], src[:, :, 0:HALF],
                                      st[name][:, HALF:ROPE].unsqueeze(1).to_broadcast(half), ALU.mult))
                link(ve.tensor_tensor(roped[:, :, ROPE:HD], src[:, :, ROPE:HD],
                                      w_n[name][:, ROPE:HD].unsqueeze(1).to_broadcast(both), ALU.mult))
                ve.wait_ge(S("qkrstd_done"), 2 * b + j + 1)
                last = ve.tensor_tensor(roped[:, :, 0:ROPE], roped[:, :, 0:ROPE], rot[:, :, 0:ROPE], ALU.add)
                if j == 1:
                    link(last)
                    last = ve.tensor_tensor(roped, roped, rms[b][:, 48:64].unsqueeze(2).to_broadcast([P, NH, HD]),
                                            ALU.mult)
                last.then_inc(S(done), 1)

            def rope_q(b):
                rope(b, 0, qf[b], "q", "q_roped")
                link(ve.tensor_scalar(rms[b][:, 16:32], rms[b][:, 16:32], 1.0 / math.sqrt(HD), None, ALU.mult))

            def rope_k(b):
                rope(b, 1, kf[b][:, :, 0:HD], "k", "k_roped")

            beside = {(0, 8): [(key_residue, 2)], (1, 3): [(key_part2, 2)], (1, 5): [(key_part3, 2)],
                      (2, 1): [(key_residue, 3)], (2, 3): [(key_part2, 3)], (2, 5): [(key_part3, 3)],
                      (3, 8): [(masked_weight, 0)], (5, 2): [(normalise, 0)], (5, 3): [(ln_stats, 1, 0)],
                      (5, 4): [(ln_apply, 1, 0)], (5, 8): [(step_magnitude, 0)], (6, 2): [(step_and_input, 0)],
                      (6, 4): [(split_maps, 0)], (7, 3): [(scan, 0, 0)], (7, 6): [(read_states, 0, 0)]}
            split_queries(0)
            key_residue(0)
            key_residue(1)
            key_part3(0)
            key_part3(1)
            split_queries(1)
            for g in range(NG):
                b, hg = divmod(g, NHG)
                for piece in range(8):
                    m = 8 * g + piece
                    ve.wait_ge(S("score_a"), m + 1)
                    ve.reduce_max(mx[:, piece // 2, piece % 2:piece % 2 + 1],
                                  score_a[m % 2].rearrange("p i k -> p (i k)"), X_AXIS).then_inc(S("max_done"), 1)
                    if (g, piece) in beside:
                        for step in beside[g, piece]:
                            step[0](*step[1:])
                ve.wait_ge(S("max_done"), 8 * g + 8)
                link(ve.tensor_tensor(m4[:, :], mx[:, :, 0], mx[:, :, 1], ALU.max))
                link(ve.tensor_scalar(negm[:, :], m4[:, :], floor0, -1.0, ALU.max, ALU.mult))
                heads = slice(HPG * hg, HPG * (hg + 1))
                link(ve.tensor_copy(nm[b][:, heads, 0], negm[:, :]))
                ve.tensor_tensor(nm[b][:, heads, 1], negm[:, :], nm[b][:, heads, 0], ALU.subtract)\
                    .then_inc(S("nm_done"), 1)
                if g in (3, 7):
                    ve.wait_ge(S("nm_done"), g + 1)
                if (g, 8) in beside:
                    for step in beside[g, 8]:
                        step[0](*step[1:])
            masked_weight(1)
            scan(0, 1)
            read_states(0, 1)
            add_states(0)
            ln_stats(2, 0)
            ln_apply(2, 0)
            lora_hidden(0)
            normalise(1)
            ln_stats(1, 1)
            ln_apply(1, 1)
            lora_top(0)
            step_magnitude(1)
            step_and_input(1)
            split_maps(1)
            decay_exponent(1, 0)
            decay_exponent(1, 1)
            key_mask()
            lora_add(0)
            ln_stats(3, 0)
            ln_apply(3, 0)
            tables()
            scan(1, 0)
            read_states(1, 0)
            max3(0)
            scan(1, 1)
            read_states(1, 1)
            add_states(1)
            ln_stats(2, 1)
            ln_apply(2, 1)
            add3(0)
            ln_stats(4, 0)
            ln_apply(4, 0)
            lora_hidden(1)
            lora_top(1)
            lora_add(1)
            ln_stats(3, 1)
            ln_apply(3, 1)
            rope_q(0)
            max3(1)
            rope_k(0)
            add3(1)
            ln_stats(4, 1)
            ln_apply(4, 1)
            block_scores(0)
            block_scores(1)
            block_softmax(0)
            block_softmax(1)
            block_map(0)
            block_map(1)
            compressed(0)
            compressed(1)
            rope_q(1)
            rope_k(1)

            def score_max(n):
                g, b = divmod(n, NB)
                scores = ps[:, 4 * b:4 * b + 2, :].rearrange("p i (j s) -> p (i j) s", j=2)
                ve.wait_ge(S("s4_ps"), n + 1)
                link(ve.reduce_max(att[b][:, 0:4], scores[:, :, 0:P], X_AXIS))
                link(ve.reduce_max(att[b][:, 4:8], scores[:, :, P:SW], X_AXIS))
                factor = rms[b][:, 16 + HPG * g:20 + HPG * g].unsqueeze(1).to_broadcast([P, 2, HPG])
                ve.scalar_tensor_tensor(att[b][:, 8:16].rearrange("p (u j) -> p u j", u=2),
                                        att[b][:, 0:8].rearrange("p (u j) -> p u j", u=2), -1.0, factor,
                                        ALU.mult, ALU.mult).then_inc(S("nb_done"), 1)

            def normalise_weights(n):
                b = n % NB
                ve.wait_ge(S("pr_exp"), 8 * (n + 1))
                link(ve.reciprocal(att[b][:, 24:32], att[b][:, 16:24]))
                link(ve.tensor_scalar(att[b][:, 24:32], att[b][:, 24:32], 0.5, None, ALU.mult))
                ve.tensor_tensor(pr[b][:, :, 0:P], pr[b][:, :, 0:P],
                                 att[b][:, 24:28].unsqueeze(2).to_broadcast([P, HPG, P]), ALU.mult)\
                    .then_inc(S("pr_norm"), 1)
                ve.tensor_tensor(pr[b][:, :, P:SW], pr[b][:, :, P:SW],
                                 att[b][:, 28:32].unsqueeze(2).to_broadcast([P, HPG, NC + 1]), ALU.mult)\
                    .then_inc(S("pr_norm"), 1)

            def mixed(n):
                g, b = divmod(n, NB)
                ve.wait_ge(S("mT_ps"), n + 1)
                ve.tensor_copy(qf[b][:, HPG * g:HPG * (g + 1), :],
                               bank(b, 3).rearrange("p (j q) -> p j q", j=HPG)).then_inc(S("mT_sb"), 1)

            score_max(0)
            score_max(1)
            for n in range(NB * NHG):
                normalise_weights(n)
                if n + 2 < NB * NHG:
                    score_max(n + 2)
                if n >= 1:
                    mixed(n - 1)
            mixed(NB * NHG - 1)
            for b in range(NB):
                link(ve.tensor_tensor(x[b][:, :], x[b][:, :], b_out, ALU.add))
                ve.wait_ge(S("o4_ps"), b + 1)
                ve.tensor_tensor(x[b][:, :], bank(b, 0, D), x[b][:, :], ALU.add).then_inc(S(f"x_done{b}"), 1)

            layer_norm(5)
            for b in range(NB):
                ve.wait_ge(S("g_ps"), b + 1)
                link(ve.tensor_tensor(logit[b][:, 0:NE], bank(b, 1, NE), bg[:, :], ALU.add))
                link(ve.reduce_max(small[b][:, 0:1], logit[b][:, 0:NE], X_AXIS))
                ve.tensor_scalar(logit[b][:, 0:NE], logit[b][:, 0:NE], small[b][:, 0:1], None, ALU.subtract)\
                    .then_inc(S("g_shift"), 1)
            ve.wait_ge(S("g_shift"), NB)
            ve.engine_nop().then_inc(S("g_read"), NB)
            for b in range(NB):
                ve.wait_ge(S("g_exp"), b + 1)
                link(ve.reciprocal(small[b][:, 3:4], small[b][:, 2:3]))
                link(ve.tensor_scalar(coef[b][:, 0:NE], comb[b][:, :], small[b][:, 3:4], None, ALU.mult))
                link(ve.max(top8[b][:, :], coef[b][:, 0:NE]))
                link(ve.max_index(idx8[b][:, :], top8[b][:, :], coef[b][:, 0:NE]))
                link(ve.tensor_copy(idxf[b][:, :], idx8[b][:, :]))
                link(ve.tensor_scalar(coef[b][:, 8:16], iota[:, 0:NE], idxf[b][:, 0:1], top8[b][:, 0:1],
                                      ALU.is_equal, ALU.mult))
                link(ve.tensor_scalar(coef2[b][:, 0:NE], iota[:, 0:NE], idxf[b][:, 1:2], top8[b][:, 1:2],
                                      ALU.is_equal, ALU.mult))
                ve.tensor_tensor(comb[b][:, :], coef[b][:, 8:16], coef2[b][:, 0:NE], ALU.add)\
                    .then_inc(S("comb_done"), 1)
            for b in range(NB):
                ve.wait_ge(S("b3_ps"), b + 1)
                link(ve.tensor_tensor(x[b][:, :], ps[:, b, 0:D], x[b][:, :], ALU.add))
            for e in range(NE):
                for b in range(NB):
                    ve.wait_ge(S("eo_ps"), NB * e + b + 1)
                    if e >= 1:
                        ve.wait_ge(S("eo_added"), NB * (e - 1) + b + 1)
                    ve.scalar_tensor_tensor(x[b][:, :], ps[:, 6 + b, 0:D], comb[b][:, e:e + 1], x[b][:, :],
                                            ALU.mult, ALU.add).then_inc(S("eo_added"), 1)
            ve.wait_ge(S("eo_added"), NB * NE)
            for b in range(NB):
                ve.engine_nop().then_inc(S(f"x_done{b}"), 1)


def constants():
    bf16 = mybir.dt.np(BF16)
    q, k = np.arange(P)[:, None], np.arange(P)[None, :]
    cf = np.zeros((P, 2 * P + 26), np.float32)
    cf[:, 0:P] = np.eye(P)
    cf[:, P:2 * P] = q > k
    cf[:, 2 * P] = MASKED0
    cf[P - 1, 2 * P] = -3.0e38
    cf[:, 2 * P + 1:2 * P + 9] = np.arange(P)[:, None] // BLK == np.arange(NC)[None, :]
    cf[:, 2 * P + 9:2 * P + 25] = np.arange(16)
    cf[:, 2 * P + 25] = -0.5
    cb = np.zeros((P, 5 * P + 2 * NS), np.float32)
    cb[0:3 * 2 * NS, 5 * P:] = np.arange(3 * 2 * NS)[:, None] % (2 * NS) == np.arange(2 * NS)[None, :]
    cb[:, 0:P] = np.eye(P)
    cb[:, P:2 * P] = np.where(k > q, HIDE, 0)
    cb[:, 2 * P:3 * P] = np.where(q > k, HIDE, 0)
    cb[:, 3 * P:4 * P] = np.where(k > q, HIDE, 0)
    ends = np.arange(NC) * BLK + BLK - 1
    cb[:, 4 * P:4 * P + NC] = np.where(ends[None, :] > q, HIDE, 0)
    inv = (1.0 / 10000.0 ** (np.arange(HALF, dtype=np.float32) * 2.0 / ROPE)).astype(np.float32)
    ang = np.arange(P, dtype=np.float32)[:, None] * inv[None, :]
    cos, sin = np.cos(ang), np.sin(ang)
    cos2 = np.concatenate([cos, cos], 1).astype(np.float32)
    sin2 = np.concatenate([-sin, sin], 1).astype(np.float32)
    return {"cf": cf, "cb": cb.astype(bf16), "ones": np.ones((2, HPG * KEYS), bf16), "cos2": cos2, "sin2": sin2,
            "cose": cos2[ends], "sine": sin2[ends]}


def kernel(**inputs):
    import concourse.bacc as bacc
    from concourse.bass_utils import run_bass_kernel_spmd as run

    a = {n: np.asarray(v) for n, v in inputs.items()}
    T = np.transpose
    arrays = {
        "x": a["x"], "ctx": a["ctx_2048"], "ctxT": T(a["ctx_2048"], (0, 2, 1)),
        "ctxK": T(a["ctx_2048"].reshape(NB, 2, HALF_K, NHG, HPG, HD0), (0, 3, 1, 5, 4, 2)).reshape(NB, P, HPG, HALF_K),
        "mask": a["mask_BxS2_bk0"].reshape(1, -1).view(np.float32),
        "a_log": a["L0_attn_A_log"], "d": a["L0_attn_D"], "wx": T(np.concatenate([a["L0_attn_W_xproj"]] + [a["L0_attn_W_xproj"][D:]] * 2)),
        "w_lora": np.concatenate([T(a["L0_ffn_W"]), T(a["L0_ffn_A"].reshape(NE0 * RANK, D))], 1),
        "w_up": T(a["L0_ffn_B"], (0, 2, 1)).reshape(NE0 * RANK, D),
        "rw1": T(a["L0_ffn_rw1"]), "rb1": a["L0_ffn_rb1"], "rw2": T(a["L0_ffn_rw2"])[:, 0:NE0],
        "rb2": a["L0_ffn_rb2"][0:NE0], "gates": a["L0_ffn_gates"], "bias0": a["L0_ffn_bias"],
        "w_qkv": np.stack([a["L1_attn_Wq"], a["L1_attn_Wlk"], a["L1_attn_Wlv"]]),
        "b48": np.concatenate([a["L1_attn_bq"], a["L1_attn_blk"], a["L1_attn_blv"]]).reshape(48, HD),
        "wc": T(a["L1_attn_Wc"].reshape(KD, P)), "bc": a["L1_attn_bc"],
        "wkv": np.concatenate([a["L1_attn_Wk"], a["L1_attn_Wv"]], 1),
        "b_kv": np.concatenate([a["L1_attn_bk"], a["L1_attn_bv"]]),
        "qn_w": a["L1_attn_qn_w"], "kn_w": a["L1_attn_kn_w"], "sink_kT": T(a["L1_attn_sink_k"]),
        "sink_v": a["L1_attn_sink_v"], "wo": a["L1_attn_Wo"], "bo": a["L1_attn_bo"],
        "w1": a["L1_ffn_W1"], "w2": a["L1_ffn_W2"], "w3": a["L1_ffn_W3"], "wg": a["L1_ffn_Wg"], "bg": a["L1_ffn_bg"],
        "b1": T(a["L1_ffn_b1"].reshape(NE, MF, P), (2, 0, 1)), "b2": T(a["L1_ffn_b2"].reshape(NE, MF, P), (2, 0, 1)),
        "b3": a["L1_ffn_b3"],
    }
    arrays.update(constants())
    arrays = {f"in_{n}": np.ascontiguousarray(v) for n, v in arrays.items()}
    nc = bacc.Bacc("TRN2", target_bir_lowering=False, num_devices=1)
    io = {n[3:]: nc.dram_tensor(n, v.shape, mybir.dt.from_np(v.dtype), kind="ExternalInput").ap()
          for n, v in arrays.items()}
    out = nc.dram_tensor("out", (NB, P, D), F32, kind="ExternalOutput").ap()
    perceiver_program(nc, io, out)
    return run(nc, [arrays], core_ids=[0]).results[0]["out"]
```

```python
import math
from contextlib import ExitStack

import numpy as np

import concourse.bass as bass
from concourse import mybir

F32 = mybir.dt.float32
F32R = mybir.dt.float32r
BF16 = mybir.dt.bfloat16
U32 = mybir.dt.uint32
U8 = mybir.dt.uint8
ALU = mybir.AluOpType
ACT = mybir.ActivationFunctionType
X_AXIS = mybir.AxisListType.X

P = 128
NB = 2
D = 256
KD = D // P
KEYS = 2048
NCH = KEYS // P

H0, HD0 = 16, 16
HPG = 4
NHG = H0 // HPG
NG = NB * NHG
HALF_K = KEYS // 2
REP = 12
PARTS = 6
QROWS = PARTS * HD0
SROWS = QROWS + 2
VW = 32
MASKED0 = -10000.0
HIDE = -1.0e30

NS = 16
MAX_AT = [0, 0, 1, 2, 3, 4, 4, 5, 6, 7, 8, 8, 9, 10, 11, 12]
SPREAD_AT = [(5, c) for c in range(8, 15)] + [(6, c) for c in (0, 1, *range(4, 11))]
NE0, RANK, HID0 = 16, 16, 64
NH, HD, BLK, NC = 16, 128, 16, 8
SW = P + NC + 1
ROPE = 64
HALF = ROPE // 2
PROJECTIONS = ([(0, j, n) for j in range(2) for n in range(4)] + [(0, 2, 0), (0, 2, 1)]
               + [(1, j, n) for j in range(2) for n in range(4)] + [(0, 2, 2), (0, 2, 3)] + [(1, 2, n) for n in range(4)])
NE, FF = 8, 512
MF = FF // P

W1, W2, W3 = KD * FF, MF * FF, MF * D
RAW = 4


def view(region, start, words, dtype=F32):
    part = region[:, start:start + words]
    return part if dtype == F32 else part.bitcast(dtype)


def perceiver_program(nc, io, out):
    ctx = ExitStack()
    sems = {}
    with ctx:
        def sb(name, shape, dt=F32):
            return ctx.enter_context(nc.sbuf_tensor(name, shape, dt))

        def S(name):
            if name not in sems:
                sems[name] = ctx.enter_context(nc.semaphore(name))
            return sems[name]

        with nc.sbuf_tensor("reg_a", [P, 16384], F32) as reg_a, nc.sbuf_tensor("reg_b", [P, 26112], F32) as reg_b:
            pass
        part_a = sb("part_a", [P, 16384], F32R)
        part_b = sb("part_b", [P, 26112], F32R)
        ctxT = reg_a[:, 0:8192].rearrange("p (b h k) -> p b h k", b=NB, h=KD)
        ctxN = reg_a[:, 8192:16384].rearrange("p (b c d) -> p b c d", b=NB, c=NCH)
        kS = [view(reg_b, 4096 * i, 4096, BF16).rearrange("p (j k) -> p j k", j=HPG) for i in range(3)]
        ctxK = reg_a[:, 0:8192].rearrange("p (b j k) -> p b j k", b=NB, j=HPG)
        part_at = [((reg_b, 12288), (reg_b, 14336), (reg_b, 16384)), ((reg_a, 0), (reg_a, 2048), (reg_b, 18432))]
        ks3 = [[view(r, a, 2048, BF16).rearrange("p (j k) -> p j k", j=HPG) for r, a in ats] for ats in part_at]
        va = [reg_b[:, 20480 + 2048 * i:20480 + 2048 * (i + 1)].rearrange("p (c j w) -> p c j w", c=NCH, j=HPG)
              for i in range(2)]
        pT = [reg_b[:, 24576 + 512 * i:24576 + 512 * (i + 1)] for i in range(3)]
        bc_row = [reg_b[:, a:a + 4096].rearrange("p (n l) -> p n l", n=2 * NS) for a in (12288, 0)]
        decay = [r[:, a:a + 4096].rearrange("p (h n l) -> p h n l", h=KD, n=NS) for r, a in ((reg_a, 0), (reg_b, 4096))]
        state = [reg_a[:, 4096:8192].rearrange("p (h n l) -> p h n l", h=KD, n=NS),
                 reg_b[:, 8192:12288].rearrange("p (h n l) -> p h n l", h=KD, n=NS)]
        w_qkv = reg_b[:, 0:12288].rearrange("p (j k n) -> p j k n", j=3, k=KD)
        w_o = reg_b[:, 12288:16384].rearrange("p (h n) -> p h n", h=NH)
        p3 = [reg_b[:, 16384 + 2048 * b:16384 + 2048 * (b + 1)] for b in range(NB)]
        p3T = [reg_b[:, 20480 + 2048 * b:20480 + 2048 * (b + 1)].rearrange("p (c q) -> p c q", c=NCH)
               for b in range(NB)]
        roped = reg_b[:, 16384:18432].rearrange("p (h d) -> p h d", h=NH)
        cvs = reg_b[:, 18432:20480].rearrange("p (h d) -> p h d", h=NH)
        bias3 = view(reg_b, 20480, 1024, BF16)
        squares = reg_b[:, 14336:16384].rearrange("p (h d) -> p h d", h=NH)
        act = [reg_a[:, 8192 * b:8192 * (b + 1)] for b in range(NB)]
        qf = [a[:, 0:2048].rearrange("p (h d) -> p h d", h=NH) for a in act]
        kf = [a[:, 2048:2048 + NH * SW].rearrange("p (h d) -> p h d", h=NH) for a in act]
        lv = [a[:, 4240:6288].rearrange("p (h d) -> p h d", h=NH) for a in act]
        pr = [a[:, 6288:6288 + HPG * SW].rearrange("p (j d) -> p j d", j=HPG) for a in act]
        prT = [a[:, 6836:7348].rearrange("p (j d) -> p j d", j=HPG) for a in act]
        pcT = [a[:, 7348:7860].rearrange("p (j d) -> p j d", j=HPG) for a in act]
        def weights_of(region, at, gap):
            one = region[:, at:at + W1].rearrange("p (k n) -> p k n", k=KD)
            two = region[:, at + gap * W1:at + gap * W1 + W2].rearrange("p (k n) -> p k n", k=MF)
            three = region[:, at + gap * (W1 + W2):at + gap * (W1 + W2) + W3].rearrange("p (k n) -> p k n", k=MF)
            return one, two, three

        raw = [weights_of(reg_b, at, 1) for at in (0, 20480, 12288, 16384)]
        high = [list(weights_of(part_b, 4096, 2)), list(weights_of(part_a, 0, 2))]
        low = [[weights_of(r, at + off, 2)[i] for i, off in enumerate((W1, W2, W3))]
               for r, at in ((part_b, 4096), (part_a, 0))]
        hid = [reg_a[:, 8192 + 1024 * i:9216 + 1024 * i].rearrange("p (m t) -> p m t", m=MF) for i in range(2)]
        hid_high = [part_a[:, 10240 + 2048 * i:11264 + 2048 * i].rearrange("p (m t) -> p m t", m=MF) for i in range(2)]
        hid_low = [part_a[:, 11264 + 2048 * i:12288 + 2048 * i].rearrange("p (m t) -> p m t", m=MF) for i in range(2)]
        x_high = part_a[:, 14336:14848].rearrange("p (k t) -> p k t", k=KD)
        x_low = part_a[:, 14848:15360].rearrange("p (k t) -> p k t", k=KD)

        cf = sb("cf", [P, 2 * P + 1 + NC + NC * 0 + 16 + 1])
        ident = cf[:, 0:P]
        later = cf[:, P:2 * P]
        floor0 = cf[:, 2 * P:2 * P + 1]
        in_block = cf[:, 2 * P + 1:2 * P + 9]
        iota = cf[:, 2 * P + 9:2 * P + 25]
        neg_half = cf[:, 2 * P + 25:2 * P + 26]
        cb = sb("cb", [P, 5 * P + 2 * NS], BF16)
        identb = cb[:, 0:P]
        hide_q = cb[:, P:2 * P]
        hide_k = cb[:, 2 * P:3 * P]
        hide_s = cb[:, 3 * P:3 * P + SW]
        pick = cb[0:3 * 2 * NS, 5 * P:5 * P + 2 * NS]
        onesb = sb("onesb", [P, P], BF16)
        bc_res = sb("bc_res", [3 * 2 * NS, P])
        bc_split = sb("bc_split", [3 * 2 * NS, P], BF16)

        x = [sb(f"x{b}", [P, D]) for b in range(NB)]
        xn = [sb(f"xn{b}", [P, D]) for b in range(NB)]
        xT2 = sb("xT", [P, KD, NB * P])
        xT = [xT2[:, :, b * P:(b + 1) * P] for b in range(NB)]
        stats = [sb(f"stats{b}", [P, 6]) for b in range(NB)]
        mean_var = [sb(f"mv{b}", [P, 2]) for b in range(NB)]
        var_eps = [sb(f"ve{b}", [P, 1]) for b in range(NB)]
        rstd = [sb(f"rstd{b}", [P, 1]) for b in range(NB)]
        tmp = [sb(f"tmp{b}", [P, D]) for b in range(NB)]
        tmp2 = [sb(f"tmpb{b}", [P, D]) for b in range(NB)]
        oreg = sb("oreg", [P, 2048])
        q_split = [view(oreg, 1024 * b, 768, BF16).rearrange("p (h t d) -> p h t d", h=H0, t=PARTS)
                   for b in range(NB)]
        o_all = [oreg[:, 1024 * b:1024 * (b + 1)].rearrange("p (g u j w) -> p g u j w", g=NHG, u=2, j=HPG)
                 for b in range(NB)]
        qreg = sb("qreg", [P, 2048])
        qT = [view(qreg, 1024 * b, 1024, BF16).rearrange("p (h q) -> p h q", h=H0) for b in range(NB)]
        mx = sb("mx", [P, HPG, 2])
        m4 = sb("m4", [P, HPG])
        negm = sb("negm", [P, HPG])
        nm = [sb(f"nm{b}", [P, H0, 2], BF16) for b in range(NB)]
        e_arg = [sb(f"e_arg{b}", [P, H0]) for b in range(NB)]
        e_val = [sb(f"e_val{b}", [P, H0]) for b in range(NB)]
        rec = [sb(f"rec{b}", [P, H0]) for b in range(NB)]
        o_sb = sb("o_sb", [P, P])
        wx = sb("wx", [P, KD, D + 3 * 2 * NS])
        a_log = sb("a_log", [P, KD, NS])
        ea = sb("ea", [P, KD, NS])
        d_row = oreg[:, 0:256]
        dt = [tmp2[b] for b in range(NB)]
        w_lora = sb("w_lora", [P, KD, 2 * D])
        w_up = oreg[:, 256:768].rearrange("p (k n) -> p k n", k=KD)
        rw1 = oreg[:, 768:896].rearrange("p (k n) -> p k n", k=KD)
        rb1 = sb("rb1", [HID0, 1])
        rw2 = sb("rw2", [HID0, NE0])
        rb2 = sb("rb2", [P, NE0])
        gates = sb("gates", [P, NE0])
        bias0 = reg_b[:, 12288:12544]
        top8 = [sb(f"top8_{b}", [P, 8]) for b in range(NB)]
        idx8 = [sb(f"idx8_{b}", [P, 8], U32) for b in range(NB)]
        idxf = [sb(f"idxf_{b}", [P, 8]) for b in range(NB)]
        logit = [sb(f"logit{b}", [P, NE0]) for b in range(NB)]
        coef = [sb(f"coef{b}", [P, NE0]) for b in range(NB)]
        coef2 = [sb(f"coefb{b}", [P, NE0]) for b in range(NB)]
        small = [sb(f"small{b}", [P, 8]) for b in range(NB)]
        xmask = view(reg_b, 18432, 2048, BF16)
        mask8 = reg_b[0:1, 12544:12544 + NB * KEYS // 4]
        mask_row = xmask[0:1, :]
        m3 = [sb(f"m3_{b}", [P, 4]) for b in range(NB)]
        tab = qreg
        cos2 = tab[:, 0:64]
        sin2 = tab[:, 64:128]
        wq_n = tab[:, 128:256]
        wk_n = tab[:, 256:384]
        ct = {"q": tab[:, 384:448], "k": tab[:, 448:512], "e": tab[:, 512:576]}
        st = {"q": tab[:, 576:640], "k": tab[:, 640:704], "e": tab[:, 704:768]}
        cose = tab[:, 768:832]
        sine = tab[:, 832:896]
        w_n = {"q": wq_n, "k": wk_n, "e": wk_n}
        bias48 = tab[:, 896:1024]
        split48 = view(tab, 1024, 192, BF16).rearrange("p (t d) -> p t d", t=3)
        res48 = tab[:, 1216:1344]
        b_out = tab[:, 1344:1600]
        sinkT = tab[:, 1600:1616]
        w_c = tab[:, 1616:1618]
        b_c = tab[0:1, 1618:1619]
        rms = [tab[:, 1620 + 64 * b:1684 + 64 * b] for b in range(NB)]
        wkv = reg_b[:, 24576:25088].rearrange("p (k n) -> p k n", k=KD)
        b_kv = reg_b[0:NC, 25088:25344]
        comp = [sb(f"comp{b}", [P, 160]) for b in range(NB)]
        ckv = [reg_b[0:NC, 12544 + 512 * b:12800 + 512 * b] for b in range(NB)]
        ckr = [reg_b[0:NC, 12800 + 512 * b:12928 + 512 * b] for b in range(NB)]
        cks = [reg_b[0:NC, 12928 + 512 * b:13056 + 512 * b] for b in range(NB)]
        att = [sb(f"att{b}", [P, 32]) for b in range(NB)]
        wg = sb("wg", [P, KD, NE])
        bg = sb("bg", [P, NE])
        b1 = sb("b1", [P, NE, MF])
        b2 = sb("b2", [P, NE, MF])
        b3 = reg_b[0:NE, 25344:25600]
        comb = [sb(f"comb{b}", [P, NE]) for b in range(NB)]
        combT = reg_b[0:NE, 25600:25856]

        ps = ctx.enter_context(nc.psum_tensor("ps", [P, 8, 512], F32))
        score_a = [ps[:, 0:2, :], ps[:, 2:4, :]]
        score_b = [ps[:, 4, :], ps[:, 5, :]]

        def bank(b, i, cols=512):
            return ps[:, 4 * b + i, 0:cols]

        side = ps[:, 6, 256:512]

        def bankb(i):
            return ps[:, i, :].bitcast(BF16)

        block = ctx.enter_context(nc.Block())

        @block.sync
        def _(sp):
            def load(dst, src, name):
                sp.dma_start(dst, src).then_inc(S(name), 16)

            load(x[0][:, :], io["x"][0], "x_in")
            load(ctxK[:, 0, 0:2, :], io["ctxK"][0][:, 0:2, :], "ctxK_in0")
            load(x[1][:, :], io["x"][1], "x_in")
            load(cf[:, :], io["cf"], "const_in")
            load(cb[:, :], io["cb"], "const_in")
            load(ctxK[:, 0, 2:4, :], io["ctxK"][0][:, 2:4, :], "ctxK_in1")
            for i in range(3):
                load(kS[i][QROWS:SROWS, :, :], io["ones"].rearrange("r (j k) -> r j k", j=HPG), "ones_in")
            for g in range(NG):
                b, hg = divmod(g, NHG)
                if g >= 3:
                    sp.wait_ge(S("pv_done"), NCH * (g - 2))
                for part, at in enumerate(((0, 3, 5), (1, 4), (2,))):
                    sp.wait_ge(S(f"k{part + 1}_done"), 2 * (b + 1))
                    for t in at:
                        for half in range(2):
                            row = 32 * hg + HD0 * half
                            sp.dma_start(kS[g % 3][HD0 * t:HD0 * (t + 1), :, HALF_K * half:HALF_K * (half + 1)],
                                         ks3[b][part][row:row + HD0, :, :]).then_inc(S(f"kS_in{g % 3}"), 16)
                if g == 0:
                    load(ctxN[:, 0, :, :], io["ctx"][0].rearrange("(c p) d -> p c d", p=P), "ctxN_in0")
                    for n in range(2):
                        load(ctxK[:, 1, 2 * n:2 * n + 2, :], io["ctxK"][1][:, 2 * n:2 * n + 2, :], f"ctxK_in{n + 2}")
                if g == 2:
                    load(ctxN[:, 1, :, :], io["ctx"][1].rearrange("(c p) d -> p c d", p=P), "ctxN_in1")
                    load(wx[:, :, :], io["wx"].rearrange("(k p) n -> p k n", p=P), "ssm_in")
                    load(a_log[:, :, :], io["a_log"].rearrange("(k p) n -> p k n", p=P), "ssm_in")
                if g == 3:
                    load(w_lora[:, :, :], io["w_lora"].rearrange("(k p) n -> p k n", p=P), "lora_in")
                    load(rb1[:, :], io["rb1"].unsqueeze(1), "lora_in")
                    load(rw2[:, :], io["rw2"], "lora_in")
                    load(rb2[:, :], io["rb2"].partition_broadcast(P), "lora_in")
                    load(gates[:, :], io["gates"].partition_broadcast(P), "lora_in")
                    load(wg[:, :, :], io["wg"].rearrange("(k p) n -> p k n", p=P), "ffn_in")
                    load(bg[:, :], io["bg"].partition_broadcast(P), "ffn_in")
                    load(b1[:, :, :], io["b1"], "ffn_in")
                    load(b2[:, :, :], io["b2"], "ffn_in")

            sp.wait_ge(S("x_done0"), 1)
            load(d_row, io["d"].partition_broadcast(P), "lora_in")
            load(w_up, io["w_up"].rearrange("(k p) n -> p k n", p=P), "lora_in")
            load(rw1, io["rw1"].rearrange("(k p) n -> p k n", p=P), "lora_in")
            sp.wait_ge(S("hc_done"), KD)
            load(mask8, io["mask"], "mask_in")
            load(bias0, io["bias0"].partition_broadcast(P), "mask_in")
            load(ctxT[:, 0, :, :], io["ctxT"][0].rearrange("(h p) k -> p h k", p=P), "ctxT_in0")
            sp.wait_ge(S("y_ps"), 1)
            load(ctxT[:, 1, :, :], io["ctxT"][1].rearrange("(h p) k -> p h k", p=P), "ctxT_in1")
            sp.wait_ge(S("x_done1"), 1)
            load(wkv, io["wkv"].rearrange("(k p) n -> p k n", p=P), "tab_in")
            load(b_kv, io["b_kv"].partition_broadcast(NC), "tab_in")
            load(b3, io["b3"], "tab_in")
            load(cos2, io["cos2"], "tab_in")
            load(sin2, io["sin2"], "tab_in")
            load(cose[0:NC, :], io["cose"], "tab_in")
            load(sine[0:NC, :], io["sine"], "tab_in")
            load(wq_n, io["qn_w"].partition_broadcast(P), "tab_in")
            load(wk_n, io["kn_w"].partition_broadcast(P), "tab_in")
            load(bias48[0:48, :], io["b48"], "tab_in")
            load(b_out, io["bo"].partition_broadcast(P), "tab_in")
            load(sinkT, io["sink_kT"], "tab_in")
            load(w_c, io["wc"], "tab_in")
            load(b_c, io["bc"].unsqueeze(0), "tab_in")
            sp.wait_ge(S("hc_done"), KD * NB)
            for j in range(3):
                if j == 2:
                    sp.wait_ge(S("y_ps"), 2)
                load(w_qkv[:, j, :, :], io["w_qkv"][j].rearrange("(k p) n -> p k n", p=P), f"wqkv_in{j}")
            sp.wait_ge(S("x_done0"), 4)
            sp.wait_ge(S("b48_split"), 1)
            for j in range(3):
                for t in range(3):
                    sp.dma_start(bias3[32 * j + t:32 * j + t + 1, :].rearrange("o (a d) -> o a d", d=HD),
                                 split48[16 * j:16 * j + 16, t, :]).then_inc(S(f"wqkv_in{j}"), 16)
            sp.wait_ge(S("x_done1"), 4)
            for b in range(NB):
                load(cvs[32 * b + NC:32 * b + NC + 1, :, :], io["sink_v"].unsqueeze(0), "sinkv_in")
            for e in range(NE):
                if e == 0:
                    sp.wait_ge(S("proj_ps"), len(PROJECTIONS))
                if e == 1:
                    sp.wait_ge(S("k_roped"), NB)
                    sp.wait_ge(S("kT_tail"), 2 * NB)
                    sp.wait_ge(S("cvs_done"), NB)
                    load(w_o[:, :, :], io["wo"].rearrange("(h p) n -> p h n", p=P), "wo_in")
                if e == 2:
                    for b in range(NB):
                        sp.wait_ge(S(f"x_done{b}"), 5)
                if e >= RAW:
                    sp.wait_ge(S("w_low"), 3 * (e - RAW + 1))
                for dst, name in zip(raw[e % RAW], ("w1", "w2", "w3")):
                    load(dst, io[name][e].rearrange("(k p) n -> p k n", p=P), f"expert_in{e % RAW}")
            for b in range(NB):
                sp.wait_ge(S(f"x_done{b}"), 6)
                sp.dma_start(out[b], x[b][:, :]).then_inc(S("out_sent"), 16)
            sp.wait_ge(S("out_sent"), 16 * NB)

        @block.gpsimd
        def _(pool):
            def inv_sqrt(t, b):
                pool.wait_ge(S(f"ln_var{b}"), t + 1)
                pool.tensor_tensor(rstd[b][:, :], var_eps[b][:, :], neg_half, ALU.pow).then_inc(S(f"ln_rstd{b}"), 1)

            pool.memset(onesb[:, :], 1.0).then_inc(S("ones_set"), 1)
            pool.wait_ge(S("const_in"), 32)
            inv_sqrt(0, 0)
            inv_sqrt(0, 1)
            for i in range(2):
                pool.memset(va[i][:, :, :, :], 0.0).then_inc(S("va_zero"), 1)
            for i in range(2):
                pool.wait_ge(S("va_zero"), 2)
                pool.memset(va[i][:, :, :, HD0:HD0 + 1], 1.0).then_inc(S("ones_set"), 1)
            def state_input(b, h):
                pool.wait_ge(S("dtx_done"), b + 1)
                pool.wait_ge(S("bc_sb"), (8, 20)[b])
                pool.tensor_tensor(state[b][:, h], tmp[b][:, h * P:(h + 1) * P].unsqueeze(1).to_broadcast([P, NS, P]),
                                   bc_row[b][:, 0:NS, :], ALU.mult).then_inc(S("dbx_done"), 1)

            def decay_exponent(h):
                pool.wait_ge(S("ea_done"), 1)
                pool.wait_ge(S("kS_in1"), 16 * REP * 3)
                pool.wait_ge(S("dtx_done"), 1)
                pool.tensor_tensor(decay[0][:, h], dt[0][:, P * h:P * (h + 1)].unsqueeze(1).to_broadcast([P, NS, P]),
                                   ea[:, h, :].unsqueeze(2).to_broadcast([P, NS, P]), ALU.mult)\
                    .then_inc(S("dta_done"), 1)

            for g in range(NG):
                b, hg = divmod(g, NHG)
                if hg == 0:
                    pool.wait_ge(S(f"ctxN_in{b}"), 16)
                if g >= 2:
                    pool.wait_ge(S("oT_ready"), g - 1)
                src = ctxN[:, b, :, hg * HPG * HD0:(hg + 1) * HPG * HD0].rearrange("p c (j d) -> p c j d", j=HPG)
                pool.tensor_copy(va[g % 2][:, :, :, 0:HD0], src).then_inc(S("va_ready"), 1)
                if g == 5:
                    inv_sqrt(1, 0)
                if g == 6:
                    decay_exponent(0)
                    decay_exponent(1)
                    state_input(0, 0)
            state_input(0, 1)
            inv_sqrt(2, 0)
            inv_sqrt(1, 1)
            inv_sqrt(3, 0)
            state_input(1, 0)
            state_input(1, 1)
            inv_sqrt(2, 1)
            inv_sqrt(4, 0)
            inv_sqrt(3, 1)

            def rotated_inv_rms(b, j):
                pool.wait_ge(S("ms_done"), 2 * b + j + 1)
                pool.tensor_tensor(rms[b][:, 16 + 32 * j:32 + 32 * j], rms[b][:, 32 * j:16 + 32 * j],
                                   neg_half.to_broadcast([P, NH]), ALU.pow).then_inc(S("qkrstd_done"), 1)

            def compressed_inv_rms(b):
                pool.wait_ge(S("cms_done"), b + 1)
                pool.tensor_tensor(comp[b][0:NC, 40:41], comp[b][0:NC, 39:40], neg_half[0:NC, :], ALU.pow)\
                    .then_inc(S("crstd_done"), 1)

            def compressed_values(b):
                pool.wait_ge(S("x_done1"), 4)
                pool.wait_ge(S("qkrstd_done"), (2, 4)[b])
                pool.tensor_copy(cvs[32 * b:32 * b + NC, :, :],
                                 ckv[b][:, HD:2 * HD].unsqueeze(1).to_broadcast([NC, NH, HD])).then_inc(S("cvs_done"), 1)

            rotated_inv_rms(0, 0)
            compressed_inv_rms(0)
            rotated_inv_rms(0, 1)
            inv_sqrt(4, 1)
            compressed_values(0)
            pool.wait_ge(S("cvs_done"), 1)
            rotated_inv_rms(1, 0)
            compressed_inv_rms(1)
            rotated_inv_rms(1, 1)
            compressed_values(1)
            pool.wait_ge(S("cvs_done"), 2)

            def round_weights(e, i, name):
                pool.tensor_copy(high[e % 2][i], raw[e % RAW][i]).then_inc(S(name), 1)

            pool.wait_ge(S("expert_in0"), 48)
            round_weights(0, 0, "w13_high")
            round_weights(0, 1, "w2_high")
            round_weights(0, 2, "w13_high")
            inv_sqrt(5, 0)
            inv_sqrt(5, 1)
            for b in range(NB):
                pool.wait_ge(S(f"x_done{b}"), 5)
            for e in range(1, NE):
                pool.wait_ge(S(f"expert_in{e % RAW}"), 48 * (e // RAW + 1))
                if e >= 2:
                    pool.wait_ge(S("h1_ps"), MF * (e - 1))
                round_weights(e, 0, "w13_high")
                if e >= 2:
                    pool.wait_ge(S("eo_ps"), NB * (e - 1))
                round_weights(e, 2, "w13_high")

        @block.scalar
        def _(sc):
            steps = [0]

            def link(ins):
                steps[0] += 1
                ins.then_inc(S("act_step"), 1)
                sc.wait_ge(S("act_step"), steps[0])

            def transposed_x(t, b):
                sc.wait_ge(S(f"xT_ps{b}"), t)
                src = side if (t, b) == (1, 0) else bank(b, 0, D)
                sc.copy(xT[b], src.rearrange("p (k q) -> p k q", k=KD)).then_inc(S(f"xT_sb{b}"), 1)

            def key_part1(n):
                b, pair = divmod(n, 2)
                if b == 1:
                    sc.wait_ge(S("k3_done"), 2)
                sc.wait_ge(S(f"ctxK_in{n}"), 16)
                sc.copy(ks3[b][0][:, 2 * pair:2 * pair + 2, :], ctxK[:, b, 2 * pair:2 * pair + 2, :])\
                    .then_inc(S("k1_done"), 1)

            def key_part2(n):
                b, pair = divmod(n, 2)
                sc.wait_ge(S("kres_done"), n + 1)
                sc.copy(ks3[b][1][:, 2 * pair:2 * pair + 2, :], ctxK[:, b, 2 * pair:2 * pair + 2, :])\
                    .then_inc(S("k2_done"), 1)

            key_part1(0)
            key_part1(1)
            key_part2(0)
            key_part2(1)
            for b in range(NB):
                sc.wait_ge(S("qT_ps"), b + 1)
                for i in range(2):
                    sc.copy(qT[b][0:QROWS, 8 * i:8 * i + 8, :],
                            bankb(2 * b + i)[0:QROWS, :].rearrange("p (h q) -> p h q", h=8))\
                        .then_inc(S("qT_sb"), 1)

            def max_rows(g):
                b, hg = divmod(g, NHG)
                sc.wait_ge(S("nmT_ready"), g + 1)
                sc.copy(qT[b][QROWS:SROWS, HPG * hg:HPG * (hg + 1), :],
                        bankb(6)[0:2, 0:HPG * P].rearrange("p (j q) -> p j q", j=HPG)).then_inc(S("nm_rows"), 1)

            key_part1(2)
            key_part1(3)
            def weigh_masked(b):
                sc.wait_ge(S("e_arg"), b + 1)
                sc.activation(e_val[b][:, :], e_arg[b][:, :], ACT.Exp).then_inc(S("e_val"), 1)

            def copy_z(b):
                sc.wait_ge(S("z_ready"), b + 1)
                sc.copy(dt[b][:, :], (side, bank(1, 1, D))[b]).then_inc(S("z_sb"), 1)

            def softplus_exp(b):
                sc.wait_ge(S("z_abs"), b + 1)
                link(sc.activation(tmp[b][:, :], tmp[b][:, :], ACT.Exp, scale=-1.0))

            def softplus_log(b):
                sc.activation(tmp[b][:, :], tmp[b][:, :], ACT.Ln, bias=1.0).then_inc(S("log_done"), 1)

            def bc_copy(b, i):
                sc.wait_ge(S("bc_ps"), 16 * b + i + 1)
                rows = (2, 4)[b]
                src = side if b == 0 else bank(1, 2 + i % 2)
                sc.copy(bc_row[b][:, rows * i:rows * (i + 1), :], src.rearrange("p (n l) -> p n l", n=rows))\
                    .then_inc(S("bc_sb"), 1)

            def decay_exp(b, h):
                sc.wait_ge(S("dta_done"), KD * b + h + 1)
                sc.activation(decay[b][:, h], decay[b][:, h], ACT.Exp, scale=-1.0).then_inc(S("decay_done"), 1)

            def hidden_exp(b):
                sc.wait_ge(S("hid_lin"), b + 1)
                sc.activation(tmp2[b][0:HID0, 0:P], tmp[b][0:HID0, 0:P], ACT.Exp, scale=-1.0)\
                    .then_inc(S("hid_exp"), 1)

            def gap_exp(b):
                sc.wait_ge(S("gap_done"), b + 1)
                sc.activation(small[b][:, 1:2], small[b][:, 0:1], ACT.Exp).then_inc(S("gap_exp"), 1)

            def wxaT(b):
                sc.wait_ge(S("wxaT_ps"), b + 1)
                sc.copy(tmp2[b][:, :], bank(b, 0, D)).then_inc(S("wxaT_sb"), 1)

            def exp3(b):
                sc.wait_ge(S("m3_done"), b + 1)
                sc.activation(p3[b].rearrange("p (i k) -> p i k", i=4), ps[:, 4 * b:4 * b + 4, :], ACT.Exp,
                              bias=m3[b][:, 1:2], scale=1.0 / 16.0, accum_out=m3[b][:, 2:3])\
                    .then_inc(S("p3_done"), 1)

            def p3_columns(b, i):
                sc.wait_ge(S("p3T_ps"), 4 * b + i + 1)
                sc.copy(p3T[b][:, 4 * i:4 * i + 4, :],
                        bank(b, i).rearrange("p (c q) -> p c q", c=4)).then_inc(S("p3T_sb"), 1)

            def state_rates():
                sc.wait_ge(S("ssm_in"), 32)
                sc.activation(ea[:, :, :], a_log[:, :, :], ACT.Exp).then_inc(S("ea_done"), 1)

            beside = {(3, 9): [(state_rates,)], (4, 1): [(weigh_masked, 0)], (4, 10): [(transposed_x, 1, 0)],
                      (4, 12): [(copy_z, 0)], (5, 0): [(softplus_exp, 0)], (5, 1): [(softplus_log, 0)], (6, 2): [(decay_exp, 0, 0)],
                      (6, 6): [(decay_exp, 0, 1)],
                      (7, 11): [(transposed_x, 2, 0)], (7, 13): [(hidden_exp, 0)]}
            for i, (g, c) in enumerate(SPREAD_AT):
                beside.setdefault((g, c + 1), []).append((bc_copy, 0, i))
            max_rows(0)
            for g in range(NG):
                for c in range(NCH):
                    n = NCH * g + c
                    if (g, c) in beside:
                        for step in beside[g, c]:
                            step[0](*step[1:])
                    if g >= 1 and c == 3:
                        sc.wait_ge(S("oT_ready"), g)
                        pb, pg = divmod(g - 1, NHG)
                        sc.copy(o_all[pb][:, pg], ps[:, 6, 0:2 * P].rearrange("p (u j w) -> p u j w", u=2, j=HPG))\
                            .then_inc(S("o_all"), 1)
                    sc.wait_ge(S("score_b"), n + 1)
                    if n >= 3:
                        sc.wait_ge(S("pv_done"), n - 2)
                    sc.activation(pT[n % 3], score_b[n % 2], ACT.Exp).then_inc(S("exp_done"), 1)
                if g + 1 < NG:
                    max_rows(g + 1)
                sc.wait_ge(S("pv_done"), NCH * (g + 1))
                sc.copy(o_sb[:, :], ps[:, 7, 0:P]).then_inc(S("o_sb"), 1)
            sc.wait_ge(S("oT_ready"), NG)
            sc.copy(o_all[1][:, NHG - 1], ps[:, 6, 0:2 * P].rearrange("p (u j w) -> p u j w", u=2, j=HPG))\
                .then_inc(S("o_all"), 1)
            def projected(b, j, quarters=range(4)):
                for n in quarters:
                    sc.wait_ge(S("proj_ps"), PROJECTIONS.index((b, j, n)) + 1)
                    sc.copy((qf, kf, lv)[j][b][:, 4 * n:4 * n + 4, 0:HD],
                            bank(b, n % 2).rearrange("p (h d) -> p h d", h=4)).then_inc(S("proj_sb"), 1)

            def square(b, j):
                sc.wait_ge(S("proj_sb"), PROJECTIONS.index((b, j, 3)) + 1)
                if j == 1:
                    sc.wait_ge(S("q_roped"), b + 1)
                elif b > 0:
                    sc.wait_ge(S("k_roped"), b)
                sc.activation(squares, (qf, kf)[j][b][:, :, 0:HD], ACT.Square).then_inc(S("sq_done"), 1)

            def rotated_columns(b, j):
                for i in range(4):
                    sc.wait_ge(S("qkT_ps"), 8 * b + 4 * j + i + 1)
                    sc.copy((qf, kf)[j][b][:, 4 * i:4 * i + 4, 0:HD],
                            bank(b, 2 + i % 2).rearrange("p (h d) -> p h d", h=4)).then_inc(S("qkT_sb"), 1)

            def block_exp(b):
                sc.wait_ge(S("c_shift"), b + 1)
                sc.activation(ckr[b][0:1, :], ckr[b][0:1, :], ACT.Exp).then_inc(S("c_exp"), 1)

            def block_columns(b):
                sc.wait_ge(S("entT_ps"), b + 1)
                sc.copy(comp[b][:, 0:2 * NC], bank(b, 2, 2 * NC)).then_inc(S("entT_sb"), 1)

            def key_tail(b):
                sc.wait_ge(S("ckT_ps"), b + 1)
                sc.copy(comp[b][:, 16:16 + NC], bank(b, 3, NC)).then_inc(S("ckT_sb"), 1)
                sc.wait_ge(S("ckT_sb"), b + 1)
                sc.copy(kf[b][:, :, HD:HD + NC], comp[b][:, 16:16 + NC].unsqueeze(1).to_broadcast([P, NH, NC]))\
                    .then_inc(S("kT_tail"), 1)
                sc.copy(kf[b][:, :, HD + NC:SW], sinkT.unsqueeze(2)).then_inc(S("kT_tail"), 1)

            def weights(n):
                g, b = divmod(n, NB)
                sc.wait_ge(S("nb_done"), n + 1)
                for j in range(HPG):
                    s = ps[:, 4 * b + j // 2, 256 * (j % 2):256 * (j % 2) + SW]
                    scale = rms[b][:, 16 + HPG * g + j:17 + HPG * g + j]
                    sc.activation(pr[b][:, j, 0:P], s[:, 0:P], ACT.Exp, bias=att[b][:, 8 + j:9 + j],
                                  scale=scale, accum_out=att[b][:, 16 + j:17 + j]).then_inc(S("pr_exp"), 1)
                    sc.activation(pr[b][:, j, P:SW], s[:, P:SW], ACT.Exp, bias=att[b][:, 12 + j:13 + j],
                                  scale=scale, accum_out=att[b][:, 20 + j:21 + j]).then_inc(S("pr_exp"), 1)

            weigh_masked(1)
            gap_exp(0)
            transposed_x(1, 1)
            wxaT(0)
            copy_z(1)
            softplus_exp(1)
            softplus_log(1)
            for i in range(8):
                bc_copy(1, i)
            transposed_x(3, 0)
            decay_exp(1, 0)
            decay_exp(1, 1)
            exp3(0)
            for i in range(4):
                p3_columns(0, i)
            transposed_x(2, 1)
            hidden_exp(1)
            transposed_x(4, 0)
            block_exp(0)
            gap_exp(1)
            projected(0, 0, range(0, 2))
            wxaT(1)
            projected(0, 0, range(2, 4))
            block_columns(0)
            transposed_x(3, 1)
            square(0, 0)
            projected(0, 1, range(0, 2))
            exp3(1)
            projected(0, 1, range(2, 4))
            rotated_columns(0, 0)
            for i in range(2):
                p3_columns(1, i)
            square(0, 1)
            for i in range(2, 4):
                p3_columns(1, i)
            projected(0, 2, range(0, 2))
            transposed_x(4, 1)
            projected(1, 0, range(0, 2))
            block_exp(1)
            projected(1, 0, range(2, 4))
            square(1, 0)
            projected(1, 1, range(0, 2))
            block_columns(1)
            rotated_columns(0, 1)
            key_tail(0)
            projected(1, 1, range(2, 4))
            square(1, 1)
            projected(0, 2, range(2, 4))
            rotated_columns(1, 0)
            key_tail(1)
            projected(1, 2, range(0, 2))
            weights(0)
            projected(1, 2, range(2, 4))
            rotated_columns(1, 1)

            def weight_columns(n):
                b = n % NB
                sc.wait_ge(S("prT_ps"), n + 1)
                sc.copy(prT[b], bank(b, 2).rearrange("p (j q) -> p j q", j=HPG)).then_inc(S("prT_sb"), 1)
                sc.copy(pcT[b][32 * b:32 * b + NC + 1, :, :],
                        bank(b, 3)[0:NC + 1, :].rearrange("p (j q) -> p j q", j=HPG)).then_inc(S("prT_sb"), 1)

            for n in range(NB * NHG):
                if n + 1 < NB * NHG:
                    weights(n + 1)
                weight_columns(n)

            transposed_x(5, 0)
            transposed_x(5, 1)
            for b in range(NB):
                sc.wait_ge(S("g_shift"), b + 1)
                sc.activation(comb[b][:, :], logit[b][:, 0:NE], ACT.Exp, accum_out=small[b][:, 2:3])\
                    .then_inc(S("g_exp"), 1)
            def hidden(e, layer):
                for m in range(MF):
                    n = MF * e + m + 1
                    sc.wait_ge(S(f"h{layer + 1}_ps"), n)
                    sc.activation(hid[layer][:, m, :], ps[:, 2 + m, 0:NB * P], ACT.Gelu,
                                  bias=(b1, b2)[layer][:, e, m:m + 1]).then_inc(S(f"h{layer + 1}_sb"), 1)
                    sc.wait_ge(S(f"h{layer + 1}_sb"), n)
                    sc.copy(hid_high[layer][:, m, :], hid[layer][:, m, :]).then_inc(S(f"h{layer + 1}_high"), 1)

            for e in range(NE):
                hidden(e, 0)
                if e + 1 < NE:
                    if e >= 1:
                        sc.wait_ge(S("h2_ps"), MF * e)
                    sc.wait_ge(S(f"expert_in{(e + 1) % RAW}"), 48 * ((e + 1) // RAW + 1))
                    sc.copy(high[(e + 1) % 2][1], raw[(e + 1) % RAW][1]).then_inc(S("w2_high"), 1)
                hidden(e, 1)
                if e == 0:
                    sc.wait_ge(S("combT_ps"), 1)
                    sc.copy(combT, ps[0:NE, 0, 0:NB * P]).then_inc(S("combT_sb"), 1)

        @block.tensor
        def _(pe):
            def x_to_columns(t, b):
                pe.wait_ge(S(f"xn_done{b}"), t + 1)
                dst = side if (t, b) == (1, 0) else bank(b, 0, D)
                for k in range(KD):
                    mm = pe.transpose(dst[:, k * P:(k + 1) * P], xn[b][:, k * P:(k + 1) * P], ident)
                mm.then_inc(S(f"xT_ps{b}"), 1)

            pe.wait_ge(S("const_in"), 32)
            for b in range(NB):
                pe.wait_ge(S("q_split"), b + 1)
                for h in range(H0):
                    mm = pe.transpose(bankb(2 * b + h // 8)[0:QROWS, P * (h % 8):P * (h % 8 + 1)],
                                      q_split[b][:, h].rearrange("p t d -> p (t d)"), identb)
                mm.then_inc(S("qT_ps"), 1)

            def scores_for_max(g, part):
                b, hg = divmod(g, NHG)
                j, quarter = divmod(part, 4)
                m = 8 * g + part // 2
                i = part % 2
                if part == 0:
                    pe.wait_ge(S(f"kS_in{g % 3}"), 16 * REP * (g // 3 + 1))
                    pe.wait_ge(S("qT_sb"), 4)
                if m >= 2 and i == 0:
                    pe.wait_ge(S("max_done"), m - 1)
                q = qT[b][0:QROWS, HPG * hg + j, :]
                k = kS[g % 3][0:QROWS, j, 512 * quarter:512 * (quarter + 1)]
                if quarter < 3:
                    mm = pe.matmul(score_a[m % 2][:, i, :], q, k, start=True, stop=True)
                else:
                    pe.matmul(score_a[m % 2][:, i, 0:384], q, k[:, 0:384], start=True, stop=True)
                    pe.matmul(score_a[m % 2][:, i, 384:512], q, k[:, 384:512], start=True, stop=False)
                    mm = pe.matmul(score_a[m % 2][:, i, 384:512], identb, hide_q, start=False, stop=True)
                if i == 1:
                    mm.then_inc(S("score_a"), 1)

            def max_to_rows(g):
                b, hg = divmod(g, NHG)
                pe.wait_ge(S("nm_done"), g + 1)
                if g >= 2:
                    pe.wait_ge(S("o_all"), g - 1)
                for j in range(HPG):
                    mm = pe.transpose(bankb(6)[0:2, P * j:P * (j + 1)], nm[b][:, HPG * hg + j, :], identb)
                mm.then_inc(S("nmT_ready"), 1)

            def scores_shifted(g, c):
                b, hg = divmod(g, NHG)
                n = NCH * g + c
                if c == 0:
                    pe.wait_ge(S("nm_rows"), g + 1)
                    pe.wait_ge(S("ones_in"), 48)
                if n >= 2:
                    pe.wait_ge(S("exp_done"), n - 1)
                last = c == NCH - 1
                for j in range(HPG):
                    cols = score_b[n % 2][:, P * j:P * (j + 1)]
                    if last:
                        pe.matmul(cols, identb, hide_k, start=True, stop=False)
                    mm = pe.matmul(cols, kS[g % 3][0:SROWS, j, P * c:P * (c + 1)], qT[b][0:SROWS, HPG * hg + j, :],
                                   start=not last, stop=True)
                mm.then_inc(S("score_b"), 1)

            def values(g, c):
                n = NCH * g + c
                if c == 0:
                    pe.wait_ge(S("va_ready"), g + 1)
                    pe.wait_ge(S("ones_set"), 3)
                    if g >= 1:
                        pe.wait_ge(S("o_sb"), g)
                pe.wait_ge(S("exp_done"), n + 1)
                for j in range(HPG):
                    mm = pe.matmul(ps[VW * j:VW * (j + 1), 7, 0:P], va[g % 2][:, c, j, :], pT[n % 3][:, P * j:P * (j + 1)],
                                   start=c == 0, stop=c == NCH - 1)
                mm.then_inc(S("pv_done"), 1)

            def outputs_to_rows(g):
                pe.wait_ge(S("o_sb"), g + 1)
                if g + 1 < NG:
                    pe.wait_ge(S("nm_rows"), g + 2)
                pe.transpose(ps[:, 6, 0:P], o_sb[:, :], ident)
                pe.matmul(ps[:, 6, P:2 * P], later, va[g % 2][:, NCH - 1].rearrange("p j w -> p (j w)"),
                          start=True, stop=True).then_inc(S("oT_ready"), 1)

            def step_sizes(b):
                pe.wait_ge(S("ssm_in"), 32)
                pe.wait_ge(S(f"xT_sb{b}"), 1)
                z = (side, bank(1, 1, D))[b]
                for h in range(KD):
                    for k in range(KD):
                        mm = pe.matmul(z[:, P * h:P * (h + 1)], wx[:, k, P * h:P * (h + 1)], xT[b][:, k, :],
                                       start=k == 0, stop=k == KD - 1)
                mm.then_inc(S("z_ready"), 1)

            def state_maps(b):
                pe.wait_ge(S("z_sb"), b + 1)
                bc = (side[0:96, 0:P], ps[0:96, 5, 256:256 + P])[b]
                for k in range(KD):
                    mm = pe.matmul(bc, wx[:, k, D:D + 3 * 2 * NS], xT[b][:, k, :],
                                   start=k == 0, stop=k == KD - 1)
                mm.then_inc(S("bc_rows"), 1)

            def spread(b, i):
                pe.wait_ge(S("bc_split"), b + 1)
                if b == 0 and i >= 1:
                    pe.wait_ge(S("bc_sb"), i)
                if b == 1 and i >= 2:
                    pe.wait_ge(S("bc_sb"), 16 + i - 1)
                rows = (2, 4)[b]
                dst = side if b == 0 else bank(1, 2 + i % 2)
                for r in range(rows):
                    n = rows * i + r
                    mm = pe.matmul(dst[:, P * r:P * (r + 1)], pick[:, n:n + 1].to_broadcast([96, P]), bc_split[:, :],
                                   start=True, stop=True)
                mm.then_inc(S("bc_ps"), 1)

            def sum_states(b, h):
                pe.wait_ge(S("hc_done"), KD * b + h + 1)
                for n in range(NS):
                    mm = pe.matmul(bank(b, 0)[:, P * h:P * (h + 1)], state[b][:, h, n, :], ident, start=n == 0, stop=n == NS - 1)
                if h == KD - 1:
                    mm.then_inc(S("y_ps"), 1)

            def lora_products(b):
                pe.wait_ge(S("lora_in"), 128)
                pe.wait_ge(S(f"xT_sb{b}"), 2)
                for k in range(KD):
                    mm = pe.matmul(bank(b, 1)[0:HID0, 0:P], rw1[:, k, :], xT[b][:, k, :], start=k == 0, stop=k == KD - 1)
                mm.then_inc(S("hid_ps"), 1)
                for k in range(KD):
                    mm = pe.matmul(bank(b, 2, D), xT[b][:, k, :], w_lora[:, k, D:2 * D], start=k == 0, stop=k == KD - 1)
                mm.then_inc(S("xa_ps"), 1)

            def lora_logits(b):
                pe.wait_ge(S("hid_sb"), b + 1)
                pe.matmul(bank(b, 3)[:, 0:NE0], tmp[b][0:HID0, P:2 * P], rw2[:, :], start=True, stop=True)\
                    .then_inc(S("logit_ps"), 1)
                for k in range(KD):
                    pe.matmul(bank(b, 1, D), xT[b][:, k, :], w_lora[:, k, 0:D], start=k == 0, stop=False)

            def lora_columns(b):
                pe.wait_ge(S("wxa_done"), b + 1)
                for k in range(KD):
                    mm = pe.transpose(bank(b, 0)[:, k * P:(k + 1) * P], tmp[b][:, k * P:(k + 1) * P], ident)
                mm.then_inc(S("wxaT_ps"), 1)

            def lora_up(b):
                pe.wait_ge(S("wxaT_sb"), b + 1)
                for k in range(KD):
                    mm = pe.matmul(bank(b, 1, D), tmp2[b][:, k * P:(k + 1) * P], w_up[:, k, :], start=False,
                                   stop=k == KD - 1)
                mm.then_inc(S("lora_ps"), 1)

            def scores3(b, part):
                if part == 0:
                    pe.wait_ge(S("mask_row"), 2)
                    pe.wait_ge(S(f"xT_sb{b}"), 3)
                    pe.wait_ge(S(f"x_done{b}"), 3)
                    pe.wait_ge(S(f"ctxT_in{b}"), 16)
                for i in range(2 * part, 2 * part + 2):
                    for k in range(KD):
                        pe.matmul(bank(b, i), xT[b][:, k, :], ctxT[:, b, k, 512 * i:512 * (i + 1)],
                                  start=k == 0, stop=False)
                    mm = pe.matmul(bank(b, i), onesb[0:1, :], mask_row[0:1, KEYS * b + 512 * i:KEYS * b + 512 * (i + 1)],
                                   start=False, stop=True)
                if part == 1:
                    mm.then_inc(S("s3_ps"), 1)

            def p3_to_columns(b):
                pe.wait_ge(S("p3_done"), b + 1)
                for i in range(4):
                    for c in range(4):
                        mm = pe.transpose(bank(b, i)[:, P * c:P * (c + 1)],
                                          p3[b][:, P * (4 * i + c):P * (4 * i + c + 1)], ident)
                    mm.then_inc(S("p3T_ps"), 1)

            def outputs3(b):
                for c in range(NCH):
                    if c % 4 == 0:
                        pe.wait_ge(S("p3T_sb"), 4 * b + c // 4 + 1)
                    mm = pe.matmul(bank(b, 0, D), p3T[b][:, c, :], ctxN[:, b, c, :], start=c == 0, stop=c == NCH - 1)
                mm.then_inc(S("o3_ps"), 1)

            def misc_read(name, count):
                pe.wait_ge(S(name), count)

            beside = {(4, 9): [(misc_read, "o_all", 4), (x_to_columns, 1, 0)], (4, 11): [(step_sizes, 0)],
                      (5, 4): [(misc_read, "o_all", 5), (state_maps, 0)], (6, 4): [(misc_read, "o_all", 6)],
                      (7, 0): [(sum_states, 0, 0)], (7, 4): [(sum_states, 0, 1)], (7, 9): [(x_to_columns, 2, 0)],
                      (7, 11): [(lora_products, 0)], (7, 15): [(lora_logits, 0)]}
            for i, at in enumerate(SPREAD_AT):
                beside.setdefault(at, []).append((spread, 0, i))
            read_before_rows = {5: ("z_sb", 1), 6: ("bc_sb", 7), 7: ("bc_sb", 16)}
            read_before_outputs = {5: ("bc_sb", 9)}
            for part in range(16):
                scores_for_max(0, part)
            max_to_rows(0)
            for g in range(NG):
                for c in range(NCH):
                    scores_shifted(g, c)
                    if c == NCH - 1 and g + 1 < NG:
                        if g + 1 in read_before_rows:
                            misc_read(*read_before_rows[g + 1])
                        max_to_rows(g + 1)
                    if c > 0:
                        values(g, c - 1)
                    if c == 2 and g >= 1:
                        if g - 1 in read_before_outputs:
                            misc_read(*read_before_outputs[g - 1])
                        outputs_to_rows(g - 1)
                    if g + 1 < NG:
                        for part in range(16):
                            if MAX_AT[part] == c:
                                scores_for_max(g + 1, part)
                    if (g, c) in beside:
                        for step in beside[g, c]:
                            step[0](*step[1:])
                values(g, NCH - 1)
            outputs_to_rows(NG - 1)

            def projection(b, j, quarters=range(4)):
                pe.wait_ge(S(f"xT_sb{b}"), 4)
                pe.wait_ge(S(f"wqkv_in{j}"), 64)
                for n in quarters:
                    at = PROJECTIONS.index((b, j, n))
                    before = [i for i in range(at) if PROJECTIONS[i][0] == b and PROJECTIONS[i][2] % 2 == n % 2]
                    if before:
                        pe.wait_ge(S("proj_sb"), before[-1] + 1)
                    pe.matmul(bank(b, n % 2), onesb[32 * j:32 * j + 3, :], bias3[32 * j:32 * j + 3, 512 * n:512 * (n + 1)],
                              start=True, stop=False)
                    for i in range(KD):
                        mm = pe.matmul(bank(b, n % 2), xT[b][:, i, :], w_qkv[:, j, i, 512 * n:512 * (n + 1)],
                                       start=False, stop=i == KD - 1)
                    mm.then_inc(S("proj_ps"), 1)

            def rotated_to_columns(b, j):
                pe.wait_ge(S(("q_roped", "k_roped")[j]), b + 1)
                for i in range(4):
                    if i >= 2 or j == 1:
                        pe.wait_ge(S("qkT_sb"), 8 * b + 4 * j + i - 1)
                    for c in range(4):
                        mm = pe.transpose(bank(b, 2 + i % 2)[:, P * c:P * (c + 1)], roped[:, 4 * i + c, :], ident)
                    mm.then_inc(S("qkT_ps"), 1)

            def block_scores(b):
                pe.wait_ge(S("tab_in"), 224)
                pe.wait_ge(S(f"xT_sb{b}"), 4)
                for k in range(KD):
                    mm = pe.matmul(bank(b, 2)[0:1, 0:P], w_c[:, k:k + 1], xT[b][:, k, :], start=k == 0, stop=k == KD - 1)
                mm.then_inc(S("c_ps"), 1)

            def block_column(b):
                pe.wait_ge(S("c_soft"), b + 1)
                pe.matmul(bank(b, 3)[:, 0:1], ckr[b][0:1, :], ident[0:1, 0:1], start=True, stop=True)\
                    .then_inc(S("ccol_ps"), 1)

            def block_entries(b):
                pe.wait_ge(S("in_blk"), b + 1)
                for k in range(KD):
                    mm = pe.matmul(bank(b, 2)[:, NC * k:NC * (k + 1)], xn[b][:, P * k:P * (k + 1)],
                                   comp[b][:, 24:24 + NC], start=True, stop=True)
                mm.then_inc(S("entT_ps"), 1)

            def compressed(b):
                pe.wait_ge(S("entT_sb"), b + 1)
                for k in range(KD):
                    mm = pe.matmul(bank(b, 3)[0:NC, 0:2 * HD], comp[b][:, NC * k:NC * (k + 1)], wkv[:, k, :],
                                   start=k == 0, stop=k == KD - 1)
                mm.then_inc(S("ckv_ps"), 1)

            def compressed_key_columns(b):
                pe.wait_ge(S("ck_roped"), b + 1)
                pe.wait_ge(S("qkT_sb"), (8, 12)[b])
                pe.transpose(bank(b, 3)[:, 0:NC], ckr[b][:, :], ident[0:NC, 0:NC]).then_inc(S("ckT_ps"), 1)

            def scores4(n):
                g, b = divmod(n, NB)
                if g >= 1:
                    pe.wait_ge(S("pr_exp"), 8 * (n - NB + 1))
                for j in range(HPG):
                    h = HPG * g + j
                    s = ps[:, 4 * b + j // 2, 256 * (j % 2):256 * (j % 2) + SW]
                    pe.matmul(s, qf[b][:, h, :], kf[b][:, h, :], start=True, stop=False)
                    mm = pe.matmul(s, identb, hide_s, start=False, stop=True)
                mm.then_inc(S("s4_ps"), 1)

            x_to_columns(1, 1)
            lora_columns(0)
            step_sizes(1)
            lora_up(0)
            state_maps(1)
            for i in range(8):
                spread(1, i)
            x_to_columns(3, 0)
            scores3(0, 0)
            scores3(0, 1)
            sum_states(1, 0)
            sum_states(1, 1)
            p3_to_columns(0)
            outputs3(0)
            x_to_columns(2, 1)
            lora_products(1)
            x_to_columns(4, 0)
            block_scores(0)
            lora_logits(1)
            projection(0, 0, range(0, 2))
            lora_columns(1)
            block_column(0)
            lora_up(1)
            projection(0, 0, range(2, 4))
            block_entries(0)
            x_to_columns(3, 1)
            scores3(1, 0)
            compressed(0)
            scores3(1, 1)
            projection(0, 1)
            pe.wait_ge(S("cms_done"), 1)
            rotated_to_columns(0, 0)
            p3_to_columns(1)
            outputs3(1)
            projection(0, 2, range(0, 2))
            x_to_columns(4, 1)
            block_scores(1)
            projection(1, 0)
            block_column(1)
            projection(1, 1, range(0, 2))
            block_entries(1)
            rotated_to_columns(0, 1)
            projection(1, 1, range(2, 4))
            compressed(1)
            compressed_key_columns(0)
            projection(0, 2, range(2, 4))
            pe.wait_ge(S("cms_done"), 2)
            rotated_to_columns(1, 0)
            compressed_key_columns(1)
            pe.wait_ge(S("kT_tail"), 2)
            pe.wait_ge(S("qkT_sb"), 8)
            pe.wait_ge(S("proj_sb"), PROJECTIONS.index((0, 2, 3)) + 1)
            scores4(0)
            projection(1, 2)
            rotated_to_columns(1, 1)
            pe.wait_ge(S("kT_tail"), 4)
            pe.wait_ge(S("qkT_sb"), 16)
            pe.wait_ge(S("proj_sb"), len(PROJECTIONS))
            scores4(1)
            pe.wait_ge(S("cvs_done"), 2)
            pe.wait_ge(S("sinkv_in"), 32)

            def weights_to_columns(n):
                g, b = divmod(n, NB)
                pe.wait_ge(S("pr_norm"), 2 * (n + 1))
                if g >= 1:
                    pe.wait_ge(S("mT_sb"), n - NB + 1)
                for j in range(HPG):
                    pe.transpose(bank(b, 2)[:, P * j:P * (j + 1)], pr[b][:, j, 0:P], ident)
                for j in range(HPG):
                    mm = pe.transpose(bank(b, 3)[0:NC + 1, P * j:P * (j + 1)], pr[b][:, j, P:SW], ident)
                mm.then_inc(S("prT_ps"), 1)

            def mix_values(n):
                g, b = divmod(n, NB)
                pe.wait_ge(S("prT_sb"), 2 * (n + 1))
                for j in range(HPG):
                    h = HPG * g + j
                    pe.matmul(bank(b, 3)[:, P * j:P * (j + 1)], lv[b][:, h, :], prT[b][:, j, :], start=True, stop=False)
                    mm = pe.matmul(bank(b, 3)[:, P * j:P * (j + 1)], cvs[32 * b:32 * b + NC + 1, h, :],
                                   pcT[b][32 * b:32 * b + NC + 1, j, :], start=False, stop=True)
                mm.then_inc(S("mT_ps"), 1)

            def attention_out(b, heads):
                for h in heads:
                    if h == 0:
                        pe.wait_ge(S("wo_in"), 16)
                        pe.wait_ge(S("pr_exp"), 8 * (NB * (NHG - 1) + b + 1))
                    if h % HPG == 0:
                        pe.wait_ge(S("mT_sb"), NB * (h // HPG) + b + 1)
                    mm = pe.matmul(bank(b, 0, D), qf[b][:, h, :], w_o[:, h, :], start=h == 0, stop=h == NH - 1)
                if h == NH - 1:
                    mm.then_inc(S("o4_ps"), 1)

            for n in range(NB * NHG):
                if n + 2 < NB * NHG:
                    scores4(n + 2)
                else:
                    attention_out(n % NB, range(0, NH - 2 * HPG))
                weights_to_columns(n)
                if n >= 1:
                    mix_values(n - 1)
            attention_out(0, range(NH - 2 * HPG, NH - HPG))
            mix_values(NB * NHG - 1)
            attention_out(0, range(NH - HPG, NH))
            attention_out(1, range(NH - 2 * HPG, NH))

            for b in range(NB):
                pe.wait_ge(S(f"x_done{b}"), 5)
                x_to_columns(5, b)
            pe.wait_ge(S("ffn_in"), 64)
            for b in range(NB):
                pe.wait_ge(S(f"xT_sb{b}"), 5)
                for k in range(KD):
                    mm = pe.matmul(bank(b, 1)[:, 0:NE], xT[b][:, k, :], wg[:, k, :], start=k == 0, stop=k == KD - 1)
                mm.then_inc(S("g_ps"), 1)

            def products(out, terms, lower_done=None, done=0):
                terms = list(terms)
                for i, (left, right) in enumerate(terms):
                    if lower_done:
                        pe.wait_ge(S(lower_done), done + i + 1)
                    for u, v in ((0, 0), (1, 0), (0, 1)):
                        mm = pe.matmul(out, left[u], right[v], start=(i, u, v) == (0, 0, 0),
                                       stop=(i, u, v) == (len(terms) - 1, 0, 1))
                return mm

            def hidden1(e):
                w = high[e % 2][0], low[e % 2][0]
                pe.wait_ge(S("w_low"), 3 * e + 1)
                for m in range(MF):
                    if e >= 1:
                        pe.wait_ge(S("h2_sb"), MF * (e - 1) + m + 1)
                    elif m == MF - 1:
                        pe.wait_ge(S("g_shift"), NB)
                    products(ps[:, 2 + m, 0:NB * P],
                             (([part[:, k, P * m:P * (m + 1)] for part in w], (x_high[:, k, :], x_low[:, k, :]))
                              for k in range(KD))).then_inc(S("h1_ps"), 1)

            def hidden2(e):
                w = high[e % 2][1], low[e % 2][1]
                h = hid_high[0], hid_low[0]
                pe.wait_ge(S("w_low"), 3 * e + 2)
                for m in range(MF):
                    pe.wait_ge(S("h1_sb"), MF * e + m + 1)
                    products(ps[:, 2 + m, 0:NB * P],
                             (([part[:, k, P * m:P * (m + 1)] for part in w], [part[:, k, :] for part in h])
                              for k in range(MF)), "h1_low", MF * e).then_inc(S("h2_ps"), 1)

            def expert_out(e):
                w = high[e % 2][2], low[e % 2][2]
                h = hid_high[1], hid_low[1]
                pe.wait_ge(S("w_low"), 3 * e + 3)
                for b in range(NB):
                    if e >= 1:
                        pe.wait_ge(S("eo_added"), NB * (e - 1) + b + 1)
                    products(ps[:, 6 + b, 0:D],
                             (([part[:, k, P * b:P * (b + 1)] for part in h], [part[:, k, :] for part in w])
                              for k in range(MF)), "h2_low", MF * e).then_inc(S("eo_ps"), 1)

            pe.wait_ge(S("x_split"), NB)
            for e in range(NE):
                hidden1(e)
                if e == 1:
                    pe.wait_ge(S("combT_sb"), 1)
                    pe.wait_ge(S("tab_in"), 224)
                    for b in range(NB):
                        mm = pe.matmul(ps[:, b, 0:D], combT[:, P * b:P * (b + 1)], b3, start=True, stop=True)
                        mm.then_inc(S("b3_ps"), 1)
                if e >= 1:
                    expert_out(e - 1)
                hidden2(e)
                if e == 0:
                    for b in range(NB):
                        pe.wait_ge(S("comb_done"), b + 1)
                        mm = pe.transpose(ps[0:NE, 0, P * b:P * (b + 1)], comb[b][:, :], ident)
                    mm.then_inc(S("combT_ps"), 1)
            expert_out(NE - 1)

        @block.vector
        def _(ve):
            steps = [0]

            def link(ins):
                steps[0] += 1
                ins.then_inc(S("dve_step"), 1)
                ve.wait_ge(S("dve_step"), steps[0])

            def ln_stats(t, b):
                if t > 0:
                    ve.wait_ge(S(f"x_done{b}"), t)
                link(ve.bn_stats(stats[b][:, :], x[b][:, :]))
                link(ve.bn_aggr(mean_var[b][:, :], stats[b][:, :]))
                ve.tensor_scalar(var_eps[b][:, :], mean_var[b][:, 1:2], 1e-5, None, ALU.add)\
                    .then_inc(S(f"ln_var{b}"), 1)

            def ln_apply(t, b):
                ve.wait_ge(S(f"ln_rstd{b}"), t + 1)
                ve.tensor_scalar(xn[b][:, :], x[b][:, :], mean_var[b][:, 0:1], rstd[b][:, :],
                                 ALU.subtract, ALU.mult).then_inc(S(f"xn_done{b}"), 1)

            def layer_norm(t):
                for b in range(NB):
                    ln_stats(t, b)
                for b in range(NB):
                    ln_apply(t, b)

            ve.wait_ge(S("x_in"), 32)
            layer_norm(0)

            def key_residue(n):
                b, pair = divmod(n, 2)
                ve.wait_ge(S("k1_done"), n + 1)
                keys = ctxK[:, b, 2 * pair:2 * pair + 2, :]
                ve.tensor_tensor(keys, keys, ks3[b][0][:, 2 * pair:2 * pair + 2, :], ALU.subtract)\
                    .then_inc(S("kres_done"), 1)

            def key_part3(n):
                b, pair = divmod(n, 2)
                ve.wait_ge(S("k2_done"), n + 1)
                ve.wait_ge(S("kres_done"), n + 1)
                ve.tensor_tensor(ks3[b][2][:, 2 * pair:2 * pair + 2, :], ctxK[:, b, 2 * pair:2 * pair + 2, :],
                                 ks3[b][1][:, 2 * pair:2 * pair + 2, :], ALU.subtract).then_inc(S("k3_done"), 1)

            def key_part2(n):
                b, pair = divmod(n, 2)
                ve.wait_ge(S("kres_done"), n + 1)
                ve.tensor_copy(ks3[b][1][:, 2 * pair:2 * pair + 2, :], ctxK[:, b, 2 * pair:2 * pair + 2, :])\
                    .then_inc(S("k2_done"), 1)

            def split_queries(b):
                ve.wait_ge(S(f"xn_done{b}"), 1)
                q = tmp[b][:, :].rearrange("p (h d) -> p h d", h=H0)
                r = tmp2[b][:, :].rearrange("p (h d) -> p h d", h=H0)
                link(ve.tensor_scalar(tmp[b][:, :], xn[b][:, :], 1.0 / math.sqrt(HD0), None, ALU.mult))
                link(ve.tensor_copy(q_split[b][:, :, 0:3, :], q.unsqueeze(2).to_broadcast([P, H0, 3, HD0])))
                link(ve.tensor_tensor(r, q, q_split[b][:, :, 0, :], ALU.subtract))
                link(ve.tensor_copy(q_split[b][:, :, 3:5, :], r.unsqueeze(2).to_broadcast([P, H0, 2, HD0])))
                ve.tensor_tensor(q_split[b][:, :, 5, :], r, q_split[b][:, :, 3, :], ALU.subtract)\
                    .then_inc(S("q_split"), 1)

            def masked_weight(b):
                link(ve.tensor_tensor(e_arg[b][:, :], nm[b][:, :, 0], nm[b][:, :, 1], ALU.add))
                ve.tensor_scalar(e_arg[b][:, :], e_arg[b][:, :], MASKED0, 80.0, ALU.add, ALU.min)\
                    .then_inc(S("e_arg"), 1)

            def normalise(b):
                ve.wait_ge(S("o_all"), NHG * (b + 1))
                ve.wait_ge(S("e_val"), b + 1)
                o, u = o_all[b][:, :, 0], o_all[b][:, :, 1]
                weight = e_val[b][:, :].rearrange("p (g j) -> p g j", g=NHG).unsqueeze(3).to_broadcast([P, NHG, HPG, VW])
                link(ve.tensor_tensor(u, u, weight, ALU.mult))
                link(ve.tensor_tensor(o, o, u, ALU.add))
                r3 = rec[b][:, :].rearrange("p (g j) -> p g j", g=NHG)
                link(ve.reciprocal(r3, o[:, :, :, HD0]))
                link(ve.tensor_tensor(tmp[b][:, :].rearrange("p (g j d) -> p g j d", g=NHG, j=HPG), o[:, :, :, 0:HD0],
                                      r3.unsqueeze(3).to_broadcast([P, NHG, HPG, HD0]), ALU.mult))
                ve.tensor_tensor(x[b][:, :], x[b][:, :], tmp[b][:, :], ALU.add).then_inc(S(f"x_done{b}"), 1)

            def step_magnitude(b):
                ve.wait_ge(S("z_sb"), b + 1)
                ve.scalar_tensor_tensor(tmp[b][:, :], dt[b][:, :], -1.0, dt[b][:, :], ALU.mult, ALU.max)\
                    .then_inc(S("z_abs"), 1)

            def step_and_input(b):
                ve.wait_ge(S("log_done"), b + 1)
                link(ve.scalar_tensor_tensor(dt[b][:, :], dt[b][:, :], 0.0, tmp[b][:, :], ALU.max, ALU.add))
                ve.wait_ge(S(f"xT_sb{b}"), 1)
                ve.tensor_tensor(tmp[b][:, :].rearrange("p (k l) -> p k l", k=KD),
                                 dt[b][:, :].rearrange("p (k l) -> p k l", k=KD), xT[b], ALU.mult)\
                    .then_inc(S("dtx_done"), 1)

            def split_maps(b):
                ve.wait_ge(S("bc_rows"), b + 1)
                if b == 1:
                    ve.wait_ge(S("bc_ps"), 16)
                bc = (side[0:96, 0:P], ps[0:96, 5, 256:256 + P])[b]
                link(ve.tensor_copy(bc_split[:, :], bc))
                for row, src in ((32, bc), (64, bc), (64, bc_res)):
                    rows = slice(row, row + 32)
                    link(ve.tensor_tensor(bc_res[rows, :], src[rows, :], bc_split[rows, :], ALU.subtract))
                    last = ve.tensor_copy(bc_split[rows, :], bc_res[rows, :])
                    if src is not bc_res:
                        link(last)
                last.then_inc(S("bc_split"), 1)

            def decay_exponent(b, h):
                ve.wait_ge(S("ea_done"), 1)
                ve.wait_ge(S("dtx_done"), b + 1)
                ve.tensor_tensor(decay[b][:, h], dt[b][:, P * h:P * (h + 1)].unsqueeze(1).to_broadcast([P, NS, P]),
                                 ea[:, h, :].unsqueeze(2).to_broadcast([P, NS, P]), ALU.mult)\
                    .then_inc(S("dta_done"), 1)

            def scan(b, h):
                ve.wait_ge(S("decay_done"), KD * b + h + 1)
                link(ve.memset(decay[b][:, h, :, 0:1], 0.0))
                ve.wait_ge(S("dbx_done"), KD * b + h + 1)
                link(ve.tensor_tensor_scan(state[b][:, h].rearrange("p n l -> p (n l)"),
                                           decay[b][:, h].rearrange("p n l -> p (n l)"),
                                           state[b][:, h].rearrange("p n l -> p (n l)"), 0.0, ALU.mult, ALU.add))

            def read_states(b, h):
                ve.wait_ge(S("bc_sb"), (16, 24)[b])
                ve.tensor_tensor(state[b][:, h], state[b][:, h], bc_row[b][:, NS:2 * NS, :], ALU.mult)\
                    .then_inc(S("hc_done"), 1)

            def add_states(b):
                ve.wait_ge(S("lora_in"), 128)
                ve.wait_ge(S("dta_done"), KD * (b + 1))
                link(ve.tensor_tensor(tmp2[b][:, :], xn[b][:, :], d_row, ALU.mult))
                link(ve.tensor_tensor(x[b][:, :], x[b][:, :], tmp2[b][:, :], ALU.add))
                ve.wait_ge(S("y_ps"), b + 1)
                ve.tensor_tensor(x[b][:, :], bank(b, 0, D), x[b][:, :], ALU.add)\
                    .then_inc(S(f"x_done{b}"), 1)

            def lora_hidden(b):
                ve.wait_ge(S("lora_in"), 128)
                ve.wait_ge(S("hid_ps"), b + 1)
                ve.tensor_scalar(tmp[b][0:HID0, 0:P], bank(b, 1)[0:HID0, 0:P], rb1[:, :], None, ALU.add)\
                    .then_inc(S("hid_lin"), 1)
                ve.wait_ge(S("hid_exp"), b + 1)
                link(ve.tensor_scalar(tmp2[b][0:HID0, 0:P], tmp2[b][0:HID0, 0:P], 1.0, None, ALU.add))
                link(ve.reciprocal(tmp2[b][0:HID0, 0:P], tmp2[b][0:HID0, 0:P]))
                ve.wait_ge(S("hid_lin"), b + 1)
                ve.tensor_tensor(tmp[b][0:HID0, P:2 * P], tmp[b][0:HID0, 0:P], tmp2[b][0:HID0, 0:P], ALU.mult)\
                    .then_inc(S("hid_sb"), 1)

            def lora_top(b):
                ve.wait_ge(S("logit_ps"), b + 1)
                link(ve.tensor_tensor(logit[b][:, :], bank(b, 3, NE0), rb2[:, :], ALU.add))
                link(ve.tensor_tensor(logit[b][:, :], logit[b][:, :], gates[:, :], ALU.add))
                link(ve.max(top8[b][:, :], logit[b][:, :]))
                ve.tensor_tensor(small[b][:, 0:1], top8[b][:, 1:2], top8[b][:, 0:1], ALU.subtract)\
                    .then_inc(S("gap_done"), 1)
                link(ve.max_index(idx8[b][:, :], top8[b][:, :], logit[b][:, :]))
                link(ve.tensor_copy(idxf[b][:, :], idx8[b][:, :]))

            def lora_weighted(b):
                ve.wait_ge(S("gap_exp"), b + 1)
                link(ve.tensor_scalar(small[b][:, 2:3], small[b][:, 1:2], 1.0, None, ALU.add))
                link(ve.reciprocal(small[b][:, 3:4], small[b][:, 2:3]))
                link(ve.tensor_tensor(small[b][:, 4:5], small[b][:, 1:2], small[b][:, 3:4], ALU.mult))
                link(ve.tensor_scalar(coef[b][:, :], iota, idxf[b][:, 0:1], small[b][:, 3:4], ALU.is_equal, ALU.mult))
                link(ve.tensor_scalar(coef2[b][:, :], iota, idxf[b][:, 1:2], small[b][:, 4:5], ALU.is_equal, ALU.mult))
                link(ve.tensor_tensor(coef[b][:, :], coef[b][:, :], coef2[b][:, :], ALU.add))
                ve.wait_ge(S("xa_ps"), b + 1)
                ve.tensor_tensor(tmp[b][:, :].rearrange("p (e r) -> p e r", e=NE0),
                                 bank(b, 2, D).rearrange("p (e r) -> p e r", e=NE0),
                                 coef[b][:, :].unsqueeze(2).to_broadcast([P, NE0, RANK]), ALU.mult)\
                    .then_inc(S("wxa_done"), 1)

            def lora_add(b):
                ve.wait_ge(S("mask_in"), 32)
                link(ve.tensor_tensor(x[b][:, :], x[b][:, :], bias0, ALU.add))
                ve.wait_ge(S("lora_ps"), b + 1)
                ve.tensor_tensor(x[b][:, :], bank(b, 1, D), x[b][:, :], ALU.add).then_inc(S(f"x_done{b}"), 1)

            def key_mask():
                ve.wait_ge(S("mask_in"), 32)
                ve.tensor_scalar(mask_row[0:1, :], mask8.bitcast(U8), 16.0e30, -16.0e30, ALU.mult, ALU.add)\
                    .then_inc(S("mask_row"), 2)

            def max3(b):
                ve.wait_ge(S("s3_ps"), b + 1)
                link(ve.reduce_max(m3[b][:, 0:1], ps[:, 4 * b:4 * b + 4, :].rearrange("p i k -> p (i k)"), X_AXIS))
                ve.tensor_scalar(m3[b][:, 1:2], m3[b][:, 0:1], -1.0 / 16.0, None, ALU.mult).then_inc(S("m3_done"), 1)

            def add3(b):
                ve.wait_ge(S("p3_done"), b + 1)
                link(ve.reciprocal(m3[b][:, 3:4], m3[b][:, 2:3]))
                link(ve.tensor_scalar(m3[b][:, 3:4], m3[b][:, 0:1], -8.0e30, m3[b][:, 3:4], ALU.is_gt, ALU.mult))
                ve.wait_ge(S("o3_ps"), b + 1)
                ve.scalar_tensor_tensor(x[b][:, :], bank(b, 0, D), m3[b][:, 3:4], x[b][:, :], ALU.mult, ALU.add)\
                    .then_inc(S(f"x_done{b}"), 1)

            def tables():
                ve.wait_ge(S("tab_in"), 224)
                link(ve.tensor_copy(split48[0:48, 0, :], bias48[0:48, :]))
                link(ve.tensor_tensor(res48[0:48, :], bias48[0:48, :], split48[0:48, 0, :], ALU.subtract))
                link(ve.tensor_copy(split48[0:48, 1, :], res48[0:48, :]))
                ve.tensor_tensor(split48[0:48, 2, :], res48[0:48, :], split48[0:48, 1, :], ALU.subtract)\
                    .then_inc(S("b48_split"), 1)
                for name, c, s, rows in (("q", cos2, sin2, P), ("k", cos2, sin2, P), ("e", cose, sine, NC)):
                    w = w_n[name]
                    link(ve.tensor_tensor(ct[name][0:rows, :], c[0:rows, :], w[0:rows, 0:ROPE], ALU.mult))
                    link(ve.tensor_tensor(st[name][0:rows, 0:HALF], s[0:rows, 0:HALF], w[0:rows, HALF:ROPE], ALU.mult))
                    link(ve.tensor_tensor(st[name][0:rows, HALF:ROPE], s[0:rows, HALF:ROPE], w[0:rows, 0:HALF], ALU.mult))

            def block_scores(b):
                ve.wait_ge(S("c_ps"), b + 1)
                row = ckr[b][0:1, :]
                row3 = row.rearrange("p (c r) -> p c r", c=NC)
                mxb = comp[b][0:1, 120:128]
                link(ve.tensor_scalar(row, bank(b, 2)[0:1, 0:P], b_c, None, ALU.add))
                link(ve.reduce_max(mxb, row3, X_AXIS))
                ve.tensor_tensor(row3, row3, mxb.unsqueeze(2).to_broadcast([1, NC, BLK]), ALU.subtract)\
                    .then_inc(S("c_shift"), 1)

            def block_softmax(b):
                row3 = ckr[b][0:1, :].rearrange("p (c r) -> p c r", c=NC)
                mxb = comp[b][0:1, 120:128]
                ve.wait_ge(S("c_exp"), b + 1)
                link(ve.reduce_sum(mxb, row3, X_AXIS))
                link(ve.reciprocal(mxb, mxb))
                ve.tensor_tensor(row3, row3, mxb.unsqueeze(2).to_broadcast([1, NC, BLK]), ALU.mult)\
                    .then_inc(S("c_soft"), 1)

            def block_map(b):
                ve.wait_ge(S("ccol_ps"), b + 1)
                ve.tensor_scalar(comp[b][:, 24:24 + NC], in_block, bank(b, 3)[:, 0:1], None, ALU.mult)\
                    .then_inc(S("in_blk"), 1)

            def compressed(b):
                ve.wait_ge(S("ckv_ps"), b + 1)
                ck = ckv[b][:, 0:HD]
                link(ve.tensor_tensor(ckv[b][:, :], bank(b, 3)[0:NC, 0:2 * HD], b_kv, ALU.add))
                link(ve.tensor_tensor(cks[b][:, :], ck, ck, ALU.mult))
                link(ve.reduce_sum(comp[b][0:NC, 38:39], cks[b][:, :], X_AXIS))
                ve.tensor_scalar(comp[b][0:NC, 39:40], comp[b][0:NC, 38:39], 1.0 / HD, 1e-6, ALU.mult, ALU.add)\
                    .then_inc(S("cms_done"), 1)
                ve.wait_ge(S("crstd_done"), b + 1)
                link(ve.tensor_scalar(ck, ck, comp[b][0:NC, 40:41], None, ALU.mult))
                link(ve.tensor_tensor(ckr[b][:, 0:ROPE], ck[:, 0:ROPE], ct["e"][0:NC, :], ALU.mult))
                link(ve.tensor_tensor(cks[b][:, 0:HALF], ck[:, HALF:ROPE], st["e"][0:NC, 0:HALF], ALU.mult))
                link(ve.tensor_tensor(cks[b][:, HALF:ROPE], ck[:, 0:HALF], st["e"][0:NC, HALF:ROPE], ALU.mult))
                link(ve.tensor_tensor(ckr[b][:, ROPE:HD], ck[:, ROPE:HD], wk_n[0:NC, ROPE:HD], ALU.mult))
                ve.tensor_tensor(ckr[b][:, 0:ROPE], ckr[b][:, 0:ROPE], cks[b][:, 0:ROPE], ALU.add)\
                    .then_inc(S("ck_roped"), 1)

            def rope(b, j, src, name, done, meanwhile=()):
                rows = rms[b][:, 32 * j:32 * j + 16]
                ve.wait_ge(S("sq_done"), 2 * b + j + 1)
                link(ve.reduce_sum(rows, squares, X_AXIS))
                ve.tensor_scalar(rows, rows, 1.0 / HD, 1e-6, ALU.mult, ALU.add).then_inc(S("ms_done"), 1)
                if j == 0:
                    if b > 0:
                        ve.wait_ge(S("qkT_ps"), 8 * b)
                else:
                    ve.wait_ge(S("qkT_ps"), 8 * b + 4)
                rot = squares
                both = [P, NH, ROPE]
                half = [P, NH, HALF]
                link(ve.tensor_tensor(roped[:, :, 0:ROPE], src[:, :, 0:ROPE], ct[name].unsqueeze(1).to_broadcast(both),
                                      ALU.mult))
                link(ve.tensor_tensor(rot[:, :, 0:HALF], src[:, :, HALF:ROPE],
                                      st[name][:, 0:HALF].unsqueeze(1).to_broadcast(half), ALU.mult))
                link(ve.tensor_tensor(rot[:, :, HALF:ROPE], src[:, :, 0:HALF],
                                      st[name][:, HALF:ROPE].unsqueeze(1).to_broadcast(half), ALU.mult))
                link(ve.tensor_tensor(roped[:, :, ROPE:HD], src[:, :, ROPE:HD],
                                      w_n[name][:, ROPE:HD].unsqueeze(1).to_broadcast(both), ALU.mult))
                for step in meanwhile:
                    step[0](*step[1:])
                ve.wait_ge(S("qkrstd_done"), 2 * b + j + 1)
                last = ve.tensor_tensor(roped[:, :, 0:ROPE], roped[:, :, 0:ROPE], rot[:, :, 0:ROPE], ALU.add)
                if j == 1:
                    link(last)
                    last = ve.tensor_tensor(roped, roped, rms[b][:, 48:64].unsqueeze(2).to_broadcast([P, NH, HD]),
                                            ALU.mult)
                last.then_inc(S(done), 1)

            def rope_q(b):
                rope(b, 0, qf[b], "q", "q_roped")
                link(ve.tensor_scalar(rms[b][:, 16:32], rms[b][:, 16:32], 1.0 / math.sqrt(HD), None, ALU.mult))

            def rope_k(b, meanwhile):
                rope(b, 1, kf[b][:, :, 0:HD], "k", "k_roped", meanwhile)

            def score_max(n):
                g, b = divmod(n, NB)
                scores = ps[:, 4 * b:4 * b + 2, :].rearrange("p i (j s) -> p (i j) s", j=2)
                ve.wait_ge(S("s4_ps"), n + 1)
                link(ve.reduce_max(att[b][:, 0:4], scores[:, :, 0:P], X_AXIS))
                link(ve.reduce_max(att[b][:, 4:8], scores[:, :, P:SW], X_AXIS))
                factor = rms[b][:, 16 + HPG * g:20 + HPG * g].unsqueeze(1).to_broadcast([P, 2, HPG])
                ve.scalar_tensor_tensor(att[b][:, 8:16].rearrange("p (u j) -> p u j", u=2),
                                        att[b][:, 0:8].rearrange("p (u j) -> p u j", u=2), -1.0, factor,
                                        ALU.mult, ALU.mult).then_inc(S("nb_done"), 1)

            beside = {(0, 8): [(key_residue, 2)], (1, 3): [(key_part2, 2)], (1, 5): [(key_part3, 2)],
                      (2, 1): [(key_residue, 3)], (2, 3): [(key_part2, 3)], (2, 5): [(key_part3, 3)],
                      (3, 8): [(masked_weight, 0)], (5, 2): [(normalise, 0)], (5, 3): [(ln_stats, 1, 0)],
                      (5, 4): [(ln_apply, 1, 0)], (5, 8): [(step_magnitude, 0)], (6, 2): [(split_maps, 0)],
                      (6, 3): [(step_and_input, 0)], (7, 3): [(scan, 0, 0)], (7, 6): [(read_states, 0, 0)]}
            key_residue(0)
            split_queries(0)
            key_residue(1)
            key_part3(0)
            key_part3(1)
            split_queries(1)
            for g in range(NG):
                b, hg = divmod(g, NHG)
                for piece in range(8):
                    m = 8 * g + piece
                    ve.wait_ge(S("score_a"), m + 1)
                    ve.reduce_max(mx[:, piece // 2, piece % 2:piece % 2 + 1],
                                  score_a[m % 2].rearrange("p i k -> p (i k)"), X_AXIS).then_inc(S("max_done"), 1)
                    if (g, piece) in beside:
                        for step in beside[g, piece]:
                            step[0](*step[1:])
                ve.wait_ge(S("max_done"), 8 * g + 8)
                link(ve.tensor_tensor(m4[:, :], mx[:, :, 0], mx[:, :, 1], ALU.max))
                link(ve.tensor_scalar(negm[:, :], m4[:, :], floor0, -1.0, ALU.max, ALU.mult))
                heads = slice(HPG * hg, HPG * (hg + 1))
                link(ve.tensor_copy(nm[b][:, heads, 0], negm[:, :]))
                ve.tensor_tensor(nm[b][:, heads, 1], negm[:, :], nm[b][:, heads, 0], ALU.subtract)\
                    .then_inc(S("nm_done"), 1)
                if g in (3, 7):
                    ve.wait_ge(S("nm_done"), g + 1)
                if (g, 8) in beside:
                    for step in beside[g, 8]:
                        step[0](*step[1:])
            masked_weight(1)
            scan(0, 1)
            read_states(0, 1)
            key_mask()
            add_states(0)
            ln_stats(2, 0)
            ln_apply(2, 0)
            lora_hidden(0)
            lora_top(0)
            normalise(1)
            ln_stats(1, 1)
            ln_apply(1, 1)
            lora_weighted(0)
            step_magnitude(1)
            split_maps(1)
            lora_add(0)
            ln_stats(3, 0)
            step_and_input(1)
            ln_apply(3, 0)
            decay_exponent(1, 0)
            decay_exponent(1, 1)
            scan(1, 0)
            read_states(1, 0)
            scan(1, 1)
            read_states(1, 1)
            max3(0)
            tables()
            add_states(1)
            ln_stats(2, 1)
            ln_apply(2, 1)
            add3(0)
            ln_stats(4, 0)
            ln_apply(4, 0)
            lora_hidden(1)
            block_scores(0)
            lora_top(1)
            lora_weighted(1)
            block_softmax(0)
            lora_add(1)
            ln_stats(3, 1)
            ln_apply(3, 1)
            block_map(0)
            rope_q(0)
            max3(1)
            compressed(0)
            rope_k(0, [(add3, 1), (ln_stats, 4, 1), (ln_apply, 4, 1)])
            block_scores(1)
            block_softmax(1)
            block_map(1)
            rope_q(1)
            compressed(1)
            rope_k(1, [(score_max, 0)])

            def normalise_weights(n):
                b = n % NB
                ve.wait_ge(S("pr_exp"), 8 * (n + 1))
                link(ve.reciprocal(att[b][:, 24:32], att[b][:, 16:24]))
                link(ve.tensor_scalar(att[b][:, 24:32], att[b][:, 24:32], 0.5, None, ALU.mult))
                ve.tensor_tensor(pr[b][:, :, 0:P], pr[b][:, :, 0:P],
                                 att[b][:, 24:28].unsqueeze(2).to_broadcast([P, HPG, P]), ALU.mult)\
                    .then_inc(S("pr_norm"), 1)
                ve.tensor_tensor(pr[b][:, :, P:SW], pr[b][:, :, P:SW],
                                 att[b][:, 28:32].unsqueeze(2).to_broadcast([P, HPG, NC + 1]), ALU.mult)\
                    .then_inc(S("pr_norm"), 1)

            def mixed(n):
                g, b = divmod(n, NB)
                ve.wait_ge(S("mT_ps"), n + 1)
                ve.tensor_copy(qf[b][:, HPG * g:HPG * (g + 1), :],
                               bank(b, 3).rearrange("p (j q) -> p j q", j=HPG)).then_inc(S("mT_sb"), 1)

            def lower_weights(e, i):
                ve.wait_ge(S(("w13_high", "w2_high", "w13_high")[i]), (2 * e + 1, e + 1, 2 * e + 2)[i])
                ve.tensor_tensor(low[e % 2][i], raw[e % RAW][i], high[e % 2][i], ALU.subtract).then_inc(S("w_low"), 1)

            for n in range(NB * NHG):
                normalise_weights(n)
                if n == 0:
                    score_max(1)
                if n + 2 < NB * NHG:
                    score_max(n + 2)
                if n >= 1:
                    mixed(n - 1)
            lower_weights(0, 0)
            for b in range(NB):
                link(ve.tensor_tensor(x[b][:, :], x[b][:, :], b_out, ALU.add))
            mixed(NB * NHG - 1)
            for b in range(NB):
                ve.wait_ge(S("o4_ps"), b + 1)
                ve.tensor_tensor(x[b][:, :], bank(b, 0, D), x[b][:, :], ALU.add).then_inc(S(f"x_done{b}"), 1)
                ln_stats(5, b)
                ln_apply(5, b)

            for b in range(NB):
                half = slice(P * b, P * (b + 1))
                ve.wait_ge(S(f"xT_sb{b}"), 5)
                link(ve.tensor_copy(x_high[:, :, half], xT2[:, :, half]))
                ve.tensor_tensor(x_low[:, :, half], xT2[:, :, half], x_high[:, :, half], ALU.subtract)\
                    .then_inc(S("x_split"), 1)
            for b in range(NB):
                ve.wait_ge(S("g_ps"), b + 1)
                link(ve.tensor_tensor(logit[b][:, 0:NE], bank(b, 1, NE), bg[:, :], ALU.add))
                link(ve.reduce_max(small[b][:, 0:1], logit[b][:, 0:NE], X_AXIS))
                ve.tensor_scalar(logit[b][:, 0:NE], logit[b][:, 0:NE], small[b][:, 0:1], None, ALU.subtract)\
                    .then_inc(S("g_shift"), 1)
            lower_weights(0, 1)
            lower_weights(0, 2)
            def gate_weights(b):
                ve.wait_ge(S("g_exp"), b + 1)
                link(ve.reciprocal(small[b][:, 3:4], small[b][:, 2:3]))
                link(ve.tensor_scalar(coef[b][:, 0:NE], comb[b][:, :], small[b][:, 3:4], None, ALU.mult))
                link(ve.max(top8[b][:, :], coef[b][:, 0:NE]))
                link(ve.max_index(idx8[b][:, :], top8[b][:, :], coef[b][:, 0:NE]))
                link(ve.tensor_copy(idxf[b][:, :], idx8[b][:, :]))
                link(ve.tensor_scalar(coef[b][:, 8:16], iota[:, 0:NE], idxf[b][:, 0:1], top8[b][:, 0:1],
                                      ALU.is_equal, ALU.mult))
                link(ve.tensor_scalar(coef2[b][:, 0:NE], iota[:, 0:NE], idxf[b][:, 1:2], top8[b][:, 1:2],
                                      ALU.is_equal, ALU.mult))
                ve.tensor_tensor(comb[b][:, :], coef[b][:, 8:16], coef2[b][:, 0:NE], ALU.add)\
                    .then_inc(S("comb_done"), 1)

            def lower_hidden(e, layer):
                for m in range(MF):
                    ve.wait_ge(S(f"h{layer + 1}_high"), MF * e + m + 1)
                    ve.tensor_tensor(hid_low[layer][:, m, :], hid[layer][:, m, :], hid_high[layer][:, m, :],
                                     ALU.subtract).then_inc(S(f"h{layer + 1}_low"), 1)

            def add_expert(e):
                for b in range(NB):
                    ve.wait_ge(S("eo_ps"), NB * e + b + 1)
                    if e >= 1:
                        ve.wait_ge(S("eo_added"), NB * (e - 1) + b + 1)
                    ve.scalar_tensor_tensor(x[b][:, :], ps[:, 6 + b, 0:D], comb[b][:, e:e + 1], x[b][:, :],
                                            ALU.mult, ALU.add).then_inc(S("eo_added"), 1)

            for e in range(NE):
                lower_hidden(e, 0)
                if e == 0:
                    for b in range(NB):
                        gate_weights(b)
                if e + 1 < NE:
                    lower_weights(e + 1, 0)
                    lower_weights(e + 1, 1)
                if e == 1:
                    for b in range(NB):
                        ve.wait_ge(S("b3_ps"), b + 1)
                        link(ve.tensor_tensor(x[b][:, :], ps[:, b, 0:D], x[b][:, :], ALU.add))
                if e >= 1:
                    add_expert(e - 1)
                lower_hidden(e, 1)
                if e + 1 < NE:
                    lower_weights(e + 1, 2)
            add_expert(NE - 1)
            ve.wait_ge(S("eo_added"), NB * NE)
            for b in range(NB):
                ve.engine_nop().then_inc(S(f"x_done{b}"), 1)


def constants():
    bf16 = mybir.dt.np(BF16)
    q, k = np.arange(P)[:, None], np.arange(P)[None, :]
    cf = np.zeros((P, 2 * P + 26), np.float32)
    cf[:, 0:P] = np.eye(P)
    cf[:, P:2 * P] = q > k
    cf[:, 2 * P] = MASKED0
    cf[P - 1, 2 * P] = -3.0e38
    cf[:, 2 * P + 1:2 * P + 9] = np.arange(P)[:, None] // BLK == np.arange(NC)[None, :]
    cf[:, 2 * P + 9:2 * P + 25] = np.arange(16)
    cf[:, 2 * P + 25] = -0.5
    cb = np.zeros((P, 5 * P + 2 * NS), np.float32)
    cb[0:3 * 2 * NS, 5 * P:] = np.arange(3 * 2 * NS)[:, None] % (2 * NS) == np.arange(2 * NS)[None, :]
    cb[:, 0:P] = np.eye(P)
    cb[:, P:2 * P] = np.where(k > q, HIDE, 0)
    cb[:, 2 * P:3 * P] = np.where(q > k, HIDE, 0)
    cb[:, 3 * P:4 * P] = np.where(k > q, HIDE, 0)
    ends = np.arange(NC) * BLK + BLK - 1
    cb[:, 4 * P:4 * P + NC] = np.where(ends[None, :] > q, HIDE, 0)
    inv = (1.0 / 10000.0 ** (np.arange(HALF, dtype=np.float32) * 2.0 / ROPE)).astype(np.float32)
    ang = np.arange(P, dtype=np.float32)[:, None] * inv[None, :]
    cos, sin = np.cos(ang), np.sin(ang)
    cos2 = np.concatenate([cos, cos], 1).astype(np.float32)
    sin2 = np.concatenate([-sin, sin], 1).astype(np.float32)
    return {"cf": cf, "cb": cb.astype(bf16), "ones": np.ones((2, HPG * KEYS), bf16), "cos2": cos2, "sin2": sin2,
            "cose": cos2[ends], "sine": sin2[ends]}


def kernel(**inputs):
    import concourse.bacc as bacc
    from concourse.bass_utils import run_bass_kernel_spmd as run

    a = {n: np.asarray(v) for n, v in inputs.items()}
    T = np.transpose
    arrays = {
        "x": a["x"], "ctx": a["ctx_2048"], "ctxT": T(a["ctx_2048"], (0, 2, 1)),
        "ctxK": T(a["ctx_2048"].reshape(NB, 2, HALF_K, NHG, HPG, HD0), (0, 3, 1, 5, 4, 2)).reshape(NB, P, HPG, HALF_K),
        "mask": a["mask_BxS2_bk0"].reshape(1, -1).view(np.float32),
        "a_log": a["L0_attn_A_log"], "d": a["L0_attn_D"], "wx": T(np.concatenate([a["L0_attn_W_xproj"]] + [a["L0_attn_W_xproj"][D:]] * 2)),
        "w_lora": np.concatenate([T(a["L0_ffn_W"]), T(a["L0_ffn_A"].reshape(NE0 * RANK, D))], 1),
        "w_up": T(a["L0_ffn_B"], (0, 2, 1)).reshape(NE0 * RANK, D),
        "rw1": T(a["L0_ffn_rw1"]), "rb1": a["L0_ffn_rb1"], "rw2": T(a["L0_ffn_rw2"])[:, 0:NE0],
        "rb2": a["L0_ffn_rb2"][0:NE0], "gates": a["L0_ffn_gates"], "bias0": a["L0_ffn_bias"],
        "w_qkv": np.stack([a["L1_attn_Wq"], a["L1_attn_Wlk"], a["L1_attn_Wlv"]]),
        "b48": np.concatenate([a["L1_attn_bq"], a["L1_attn_blk"], a["L1_attn_blv"]]).reshape(48, HD),
        "wc": T(a["L1_attn_Wc"].reshape(KD, P)), "bc": a["L1_attn_bc"],
        "wkv": np.concatenate([a["L1_attn_Wk"], a["L1_attn_Wv"]], 1),
        "b_kv": np.concatenate([a["L1_attn_bk"], a["L1_attn_bv"]]),
        "qn_w": a["L1_attn_qn_w"], "kn_w": a["L1_attn_kn_w"], "sink_kT": T(a["L1_attn_sink_k"]),
        "sink_v": a["L1_attn_sink_v"], "wo": a["L1_attn_Wo"], "bo": a["L1_attn_bo"],
        "w1": a["L1_ffn_W1"], "w2": a["L1_ffn_W2"], "w3": a["L1_ffn_W3"], "wg": a["L1_ffn_Wg"], "bg": a["L1_ffn_bg"],
        "b1": T(a["L1_ffn_b1"].reshape(NE, MF, P), (2, 0, 1)), "b2": T(a["L1_ffn_b2"].reshape(NE, MF, P), (2, 0, 1)),
        "b3": a["L1_ffn_b3"],
    }
    arrays.update(constants())
    arrays = {f"in_{n}": np.ascontiguousarray(v) for n, v in arrays.items()}
    nc = bacc.Bacc("TRN2", target_bir_lowering=False, num_devices=1)
    io = {n[3:]: nc.dram_tensor(n, v.shape, mybir.dt.from_np(v.dtype), kind="ExternalInput").ap()
          for n, v in arrays.items()}
    out = nc.dram_tensor("out", (NB, P, D), F32, kind="ExternalOutput").ap()
    perceiver_program(nc, io, out)
    return run(nc, [arrays], core_ids=[0]).results[0]["out"]
```
